# Optimizing a Trainium2 kernel written in Bass

```python
import numpy as np
import jax
import jax.numpy as jnp

def _softmax(x, axis=-1):
    return jax.nn.softmax(x, axis=axis)

def _gelu(x):
    return jax.nn.gelu(x, approximate=True)

def _silu(x):
    return jax.nn.silu(x)

def _sigmoid(x):
    return jax.nn.sigmoid(x)

def _layernorm(x, axis=-1, eps=1e-05):
    m = jnp.mean(x, axis=axis, keepdims=True)
    v = jnp.var(x, axis=axis, keepdims=True)
    return (x - m) / jnp.sqrt(v + eps)

def _scatter_add(tgt, idx, src, axis=0):
    return tgt.at[idx].add(src)

def _segment_sum(src, seg, n):
    return jax.ops.segment_sum(src, seg, n)
kernel_name = 'mk_adj_ffn_d4_adj_r2_1f68c5'

def setup_inputs(seed: int=0):
    np.random.seed(seed)
    _w = jnp.asarray

    def _rec_inputs():
        import jax
        import jax.numpy as jnp
        _gk = jax.random.key(seed)
        x = -0.0002928 + 1 * jax.random.normal(jax.random.fold_in(_gk, 1), (1354, 256), jnp.float32)
        _a = jax.random.bernoulli(jax.random.fold_in(_gk, 2), 0.00590842, (1354, 1354))
        _af = _a.astype(jnp.float32)
        adj = _af
        return (x, adj)
    x, adj = _rec_inputs()

    def _L0_gnn_setup():
        import jax, jax.numpy as jnp
        import numpy as np
        N = 4096
        D = 256
        L = 2
        NEG_SLOPE = 0.01

        def _gat_layer(x, W, adj):
            proj = x @ W
            Wh, Ws = jnp.split(proj, 2, axis=-1)
            scores = Wh @ Ws.T
            a = jax.nn.softmax(scores, axis=-1) * adj
            out = a @ Wh
            out = out + x
            return jax.nn.leaky_relu(out, NEG_SLOPE)
        key = jax.random.key(seed)
        k1, k2, k3 = jax.random.split(key, 3)
        inputs = jax.random.normal(k1, (N, D), dtype=jnp.float32)
        adj = jax.random.randint(k2, (N, N), 0, 2).astype(jnp.float32)
        W_stack = jax.random.normal(k3, (L, D, 2 * D), dtype=jnp.float32) * (1.0 / np.sqrt(D))
        return {'inputs': inputs, 'adj': adj, 'W_stack': W_stack}
    _L0_gnn_all = _L0_gnn_setup()
    _L0_gnn_in = {k: v for k, v in _L0_gnn_all.items() if k in ('W_stack',)}
    del _L0_gnn_all

    def _L0_ffn_setup():
        import jax, jax.numpy as jnp
        import numpy as np
        D_MODEL = 256
        DFF = 1024
        TOP_K = 2
        EXPERTS_PER_LEVEL = (4, 8)

        def _moe_level(x, Wr, W1, b1, W2, b2, k):
            probs = jax.nn.softmax(jnp.einsum('bsd,de->bse', x, Wr), axis=-1)
            _, top_idx = jax.lax.top_k(probs, k)
            dispatch = jax.nn.one_hot(top_idx, probs.shape[-1], dtype=x.dtype).sum(axis=-2)
            xm = x[:, :, None, :] * dispatch[..., None]
            h = jax.nn.relu(jnp.einsum('bsed,edf->bsef', xm, W1) + b1)
            y = jnp.einsum('bsef,efd->bsed', h, W2) + b2
            return jnp.sum(y * probs[..., None], axis=2)
        key = jax.random.key(seed)
        ks = jax.random.split(key, 12)

        def w(k, fan_in, shape):
            return jax.random.normal(k, shape, jnp.float32) * (1.0 / np.sqrt(fan_in))

        def b(k, shape):
            return jax.random.normal(k, shape, jnp.float32) * 0.01
        E0, E1 = EXPERTS_PER_LEVEL
        return {'x': jax.random.normal(ks[0], (4, 1024, D_MODEL), jnp.float32), 'Wr0': w(ks[1], D_MODEL, (D_MODEL, E0)), 'W1_0': w(ks[2], D_MODEL, (E0, D_MODEL, DFF)), 'b1_0': b(ks[3], (E0, DFF)), 'W2_0': w(ks[4], DFF, (E0, DFF, D_MODEL)), 'b2_0': b(ks[5], (E0, D_MODEL)), 'Wr1': w(ks[6], D_MODEL, (D_MODEL, E1)), 'W1_1': w(ks[7], D_MODEL, (E1, D_MODEL, DFF)), 'b1_1': b(ks[8], (E1, DFF)), 'W2_1': w(ks[9], DFF, (E1, DFF, D_MODEL)), 'b2_1': b(ks[10], (E1, D_MODEL))}
    _L0_ffn_all = _L0_ffn_setup()
    _L0_ffn_in = {k: v for k, v in _L0_ffn_all.items() if k in ('Wr0', 'W1_0', 'b1_0', 'W2_0', 'b2_0', 'Wr1', 'W1_1', 'b1_1', 'W2_1', 'b2_1')}
    del _L0_ffn_all

    def _L1_gnn_setup():
        import jax, jax.numpy as jnp
        import numpy as np
        N = 4096
        D_IN = 256
        D_OUT = 256
        EDGE_P = 0.004

        def _xavier_uniform(key, fan_in, fan_out):
            bound = np.sqrt(6.0 / (fan_in + fan_out))
            return jax.random.uniform(key, (fan_in, fan_out), jnp.float32, -bound, bound)
        key = jax.random.key(seed)
        kx, ks, kw, ku = jax.random.split(key, 4)
        x = jax.random.normal(kx, (N, D_IN), dtype=jnp.float32)
        S = (jax.random.uniform(ks, (N, N), dtype=jnp.float32) < EDGE_P).astype(jnp.float32)
        W = _xavier_uniform(kw, D_IN, D_OUT)
        U = _xavier_uniform(ku, D_OUT, D_OUT)
        return {'x': x, 'S': S, 'W': W, 'U': U}
    _L1_gnn_all = _L1_gnn_setup()
    _L1_gnn_in = {k: v for k, v in _L1_gnn_all.items() if k in ('W', 'U')}
    del _L1_gnn_all

    def _L1_ffn_setup():
        import jax, jax.numpy as jnp
        import numpy as np
        B, T, C = (8, 512, 256)
        H = 512
        G, EG = (2, 4)
        E = G * EG
        K = 2
        LN_EPS = 1e-05

        def _swiglu(x):
            a, b = jnp.split(x, 2, axis=-1)
            return jax.nn.silu(a) * b
        key = jax.random.key(seed)
        ks = jax.random.split(key, 8)
        n = lambda k, shape, s: jax.random.normal(k, shape, dtype=jnp.float32) * s
        return {'x': n(ks[0], (B, T, C), 1.0), 'ln_scale': jnp.ones((C,), jnp.float32), 'ln_bias': jnp.zeros((C,), jnp.float32), 'shared_in_w': n(ks[1], (2 * H, C), 0.02), 'shared_out_w': n(ks[2], (C, H), 0.02), 'shared_out_b': jnp.zeros((C,), jnp.float32), 'expert_in_w': n(ks[3], (2 * H, C), 0.02), 'expert_out_weight': n(ks[4], (E, C, H), 0.02), 'expert_out_bias': jnp.zeros((E, C), jnp.float32), 'group_gate_w': n(ks[5], (G, C), 0.02), 'expert_gate_w': n(ks[6], (E, C), 0.02), 'group_bias': jnp.zeros((G,), jnp.float32), 'expert_bias': jnp.zeros((E,), jnp.float32)}
    _L1_ffn_all = _L1_ffn_setup()
    _L1_ffn_in = {k: v for k, v in _L1_ffn_all.items() if k in ('ln_scale', 'ln_bias', 'shared_in_w', 'shared_out_w', 'shared_out_b', 'expert_in_w', 'expert_out_weight', 'expert_out_bias', 'group_gate_w', 'expert_gate_w', 'group_bias', 'expert_bias')}
    del _L1_ffn_all

    def _L2_gnn_setup():
        import jax, jax.numpy as jnp
        import numpy as np
        N = 4096
        D = 256
        key = jax.random.key(seed)
        k1, k2 = jax.random.split(key)
        inp = jax.random.normal(k1, (N, D), dtype=jnp.float32)
        A = jax.random.uniform(k2, (N, N), dtype=jnp.float32)
        W = jnp.ones((D,), dtype=jnp.float32)
        return {'input': inp, 'A': A, 'W': W}
    _L2_gnn_all = _L2_gnn_setup()
    _L2_gnn_in = {k: v for k, v in _L2_gnn_all.items() if k in ('W',)}
    del _L2_gnn_all

    def _L2_ffn_setup():
        import jax, jax.numpy as jnp
        import numpy as np
        B, S, D, F, E, K, H = (4, 512, 256, 1024, 8, 2, 8)
        HEAD_DIM = D // H

        def _layernorm(x, g, b):
            m = x.mean(-1, keepdims=True)
            v = ((x - m) ** 2).mean(-1, keepdims=True)
            return (x - m) * jax.lax.rsqrt(v + 1e-05) * g + b

        def _expert(x, Wqkv, bqkv, Wo, bo, g1, be1, W1, bf1, W2, bf2, g2, be2):
            b, s, d = x.shape
            qkv = x @ Wqkv.T + bqkv
            q, k, v = jnp.split(qkv, 3, axis=-1)
            to_heads = lambda t: t.reshape(b, s, H, HEAD_DIM).transpose(0, 2, 1, 3)
            q, k, v = (to_heads(q), to_heads(k), to_heads(v))
            scale = 1.0 / np.sqrt(HEAD_DIM).astype(np.float32)
            attn = jax.nn.softmax(jnp.einsum('bhqd,bhkd->bhqk', q * scale, k), axis=-1)
            ctx = jnp.einsum('bhqk,bhkd->bhqd', attn, v).transpose(0, 2, 1, 3).reshape(b, s, d)
            ctx = ctx @ Wo.T + bo
            x = _layernorm(x + ctx, g1, be1)
            h = jax.nn.gelu(x @ W1.T + bf1, approximate=False)
            h = jax.nn.gelu(h @ W2.T + bf2, approximate=False)
            return _layernorm(x + h, g2, be2)
        key = jax.random.key(seed)
        ks = jax.random.split(key, 8)
        s = 0.02
        return {'x': jax.random.normal(ks[0], (B, S, D), jnp.float32), 'gate_Wk': jax.random.normal(ks[1], (D, D), jnp.float32) * s, 'gate_bk': jnp.zeros((D,), jnp.float32), 'expert_queries': jax.random.normal(ks[2], (E, D), jnp.float32), 'Wqkv': jax.random.normal(ks[3], (E, 3 * D, D), jnp.float32) * s, 'bqkv': jnp.zeros((E, 3 * D), jnp.float32), 'Wo': jax.random.normal(ks[4], (E, D, D), jnp.float32) * s, 'bo': jnp.zeros((E, D), jnp.float32), 'g1': jnp.ones((E, D), jnp.float32), 'be1': jnp.zeros((E, D), jnp.float32), 'W1': jax.random.normal(ks[5], (E, F, D), jnp.float32) * s, 'bf1': jnp.zeros((E, F), jnp.float32), 'W2': jax.random.normal(ks[6], (E, D, F), jnp.float32) * s, 'bf2': jnp.zeros((E, D), jnp.float32), 'g2': jnp.ones((E, D), jnp.float32), 'be2': jnp.zeros((E, D), jnp.float32)}
    _L2_ffn_all = _L2_ffn_setup()
    _L2_ffn_in = {k: v for k, v in _L2_ffn_all.items() if k in ('gate_Wk', 'gate_bk', 'expert_queries', 'Wqkv', 'bqkv', 'Wo', 'bo', 'g1', 'be1', 'W1', 'bf1', 'W2', 'bf2', 'g2', 'be2')}
    del _L2_ffn_all

    def _L3_gnn_setup():
        import jax, jax.numpy as jnp
        import numpy as np
        KAPPA = -1.0
        EPS = 1e-10
        N, D_IN, D_OUT = (4096, 256, 256)

        def _artan_k(x):
            sc = np.sqrt(-KAPPA)
            return jnp.arctanh(jnp.clip(sc * x, -1.0 + 1e-07, 1.0 - 1e-07)) / sc

        def _tan_k(x):
            sc = np.sqrt(-KAPPA)
            return jnp.tanh(sc * x) / sc

        def _clamp_abs(x, eps=EPS):
            return jnp.where(x >= 0, 1.0, -1.0) * jnp.maximum(jnp.abs(x), eps)

        def _norm(x):
            return jnp.sqrt(jnp.maximum(jnp.sum(x * x, axis=-1, keepdims=True), EPS * EPS))

        def mobius_matvec(W, x):
            x_norm = _norm(x)
            mx = x @ W
            mx_norm = _norm(mx)
            res = _tan_k(mx_norm / x_norm * _artan_k(x_norm)) * (mx / mx_norm)
            return jnp.where(mx_norm <= EPS, 0.0, res)

        def mobius_scalar_mul(r, x):
            x_norm = _norm(x)
            return _tan_k(r * _artan_k(x_norm)) * (x / x_norm)

        def weighted_midpoint_lincomb(A, X):
            gamma = jnp.maximum(2.0 / (1.0 + KAPPA * jnp.sum(X * X, axis=-1, keepdims=True)), 1e-15)
            denom = _clamp_abs(A @ (gamma - 1.0))
            nom = A @ (gamma * X)
            two_mean = nom / denom
            sq = jnp.sum(two_mean * two_mean, axis=-1, keepdims=True)
            a_mean = two_mean / (1.0 + jnp.sqrt(jnp.maximum(1.0 + KAPPA * sq, EPS)))
            alpha = jnp.sum(A, axis=-1, keepdims=True)
            return mobius_scalar_mul(alpha, a_mean)

        def logmap0(x):
            xn = _norm(x)
            return _artan_k(xn) * x / xn

        def expmap0(u):
            un = _norm(u)
            return _tan_k(un) * u / un
        key = jax.random.key(seed)
        k1, k2, k3 = jax.random.split(key, 3)
        X = jax.random.normal(k1, (N, D_IN), dtype=jnp.float32) * 0.001
        A_hat = jax.random.uniform(k2, (N, N), dtype=jnp.float32) / N
        W = jax.random.normal(k3, (D_IN, D_OUT), dtype=jnp.float32) * 0.01
        return {'X': X, 'A_hat': A_hat, 'W': W}
    _L3_gnn_all = _L3_gnn_setup()
    _L3_gnn_in = {k: v for k, v in _L3_gnn_all.items() if k in ('W',)}
    del _L3_gnn_all

    def _L3_ffn_setup():
        import jax, jax.numpy as jnp
        import numpy as np
        EPS = 1e-05
        TOP_K = 2

        def _moe_forward(x, Wg, W1, b1, W2, b2, gamma, beta):
            B, S, D = x.shape
            xf = x.reshape(-1, D)
            logits = xf @ Wg
            topv, topi = jax.lax.top_k(logits, TOP_K)
            gate_w = jax.nn.softmax(topv, axis=-1)
            h = jax.nn.relu(jnp.einsum('td,edh->teh', xf, W1) + b1[None])
            y = jnp.einsum('teh,ehd->ted', h, W2) + b2[None]
            mu = jnp.mean(y, axis=-1, keepdims=True)
            var = jnp.mean((y - mu) ** 2, axis=-1, keepdims=True)
            y = (y - mu) / jnp.sqrt(var + EPS) * gamma[None] + beta[None]
            y_sel = jnp.take_along_axis(y, topi[:, :, None], axis=1)
            out = jnp.sum(gate_w[:, :, None] * y_sel, axis=1)
            return out.reshape(B, S, D)
        key = jax.random.key(seed)
        ks = jax.random.split(key, 8)
        B, S, D, H, E = (4, 1024, 256, 256, 8)
        sd = lambda fan_in: 1.0 / np.sqrt(fan_in)
        x = jax.random.normal(ks[0], (B, S, D), dtype=jnp.float32)
        Wg = jax.random.uniform(ks[1], (D, E), jnp.float32, -sd(D), sd(D))
        W1 = jax.random.uniform(ks[2], (E, D, H), jnp.float32, -sd(D), sd(D))
        b1 = jax.random.uniform(ks[3], (E, H), jnp.float32, -sd(D), sd(D))
        W2 = jax.random.uniform(ks[4], (E, H, D), jnp.float32, -sd(H), sd(H))
        b2 = jax.random.uniform(ks[5], (E, D), jnp.float32, -sd(H), sd(H))
        gamma = jnp.ones((E, D), jnp.float32)
        beta = jnp.zeros((E, D), jnp.float32)
        return {'x': x, 'Wg': Wg, 'W1': W1, 'b1': b1, 'W2': W2, 'b2': b2, 'gamma': gamma, 'beta': beta}
    _L3_ffn_all = _L3_ffn_setup()
    _L3_ffn_in = {k: v for k, v in _L3_ffn_all.items() if k in ('Wg', 'W1', 'b1', 'W2', 'b2', 'gamma', 'beta')}
    del _L3_ffn_all
    return {'x': x, 'adj': adj, 'L0_gnn_W_stack': _L0_gnn_in['W_stack'], 'L0_ffn_Wr0': _L0_ffn_in['Wr0'], 'L0_ffn_W1_0': _L0_ffn_in['W1_0'], 'L0_ffn_b1_0': _L0_ffn_in['b1_0'], 'L0_ffn_W2_0': _L0_ffn_in['W2_0'], 'L0_ffn_b2_0': _L0_ffn_in['b2_0'], 'L0_ffn_Wr1': _L0_ffn_in['Wr1'], 'L0_ffn_W1_1': _L0_ffn_in['W1_1'], 'L0_ffn_b1_1': _L0_ffn_in['b1_1'], 'L0_ffn_W2_1': _L0_ffn_in['W2_1'], 'L0_ffn_b2_1': _L0_ffn_in['b2_1'], 'L1_gnn_W': _L1_gnn_in['W'], 'L1_gnn_U': _L1_gnn_in['U'], 'L1_ffn_ln_scale': _L1_ffn_in['ln_scale'], 'L1_ffn_ln_bias': _L1_ffn_in['ln_bias'], 'L1_ffn_shared_in_w': _L1_ffn_in['shared_in_w'], 'L1_ffn_shared_out_w': _L1_ffn_in['shared_out_w'], 'L1_ffn_shared_out_b': _L1_ffn_in['shared_out_b'], 'L1_ffn_expert_in_w': _L1_ffn_in['expert_in_w'], 'L1_ffn_expert_out_weight': _L1_ffn_in['expert_out_weight'], 'L1_ffn_expert_out_bias': _L1_ffn_in['expert_out_bias'], 'L1_ffn_group_gate_w': _L1_ffn_in['group_gate_w'], 'L1_ffn_expert_gate_w': _L1_ffn_in['expert_gate_w'], 'L1_ffn_group_bias': _L1_ffn_in['group_bias'], 'L1_ffn_expert_bias': _L1_ffn_in['expert_bias'], 'L2_gnn_W': _L2_gnn_in['W'], 'L2_ffn_gate_Wk': _L2_ffn_in['gate_Wk'], 'L2_ffn_gate_bk': _L2_ffn_in['gate_bk'], 'L2_ffn_expert_queries': _L2_ffn_in['expert_queries'], 'L2_ffn_Wqkv': _L2_ffn_in['Wqkv'], 'L2_ffn_bqkv': _L2_ffn_in['bqkv'], 'L2_ffn_Wo': _L2_ffn_in['Wo'], 'L2_ffn_bo': _L2_ffn_in['bo'], 'L2_ffn_g1': _L2_ffn_in['g1'], 'L2_ffn_be1': _L2_ffn_in['be1'], 'L2_ffn_W1': _L2_ffn_in['W1'], 'L2_ffn_bf1': _L2_ffn_in['bf1'], 'L2_ffn_W2': _L2_ffn_in['W2'], 'L2_ffn_bf2': _L2_ffn_in['bf2'], 'L2_ffn_g2': _L2_ffn_in['g2'], 'L2_ffn_be2': _L2_ffn_in['be2'], 'L3_gnn_W': _L3_gnn_in['W'], 'L3_ffn_Wg': _L3_ffn_in['Wg'], 'L3_ffn_W1': _L3_ffn_in['W1'], 'L3_ffn_b1': _L3_ffn_in['b1'], 'L3_ffn_W2': _L3_ffn_in['W2'], 'L3_ffn_b2': _L3_ffn_in['b2'], 'L3_ffn_gamma': _L3_ffn_in['gamma'], 'L3_ffn_beta': _L3_ffn_in['beta']}

def reference(x, adj, L0_gnn_W_stack, L0_ffn_Wr0, L0_ffn_W1_0, L0_ffn_b1_0, L0_ffn_W2_0, L0_ffn_b2_0, L0_ffn_Wr1, L0_ffn_W1_1, L0_ffn_b1_1, L0_ffn_W2_1, L0_ffn_b2_1, L1_gnn_W, L1_gnn_U, L1_ffn_ln_scale, L1_ffn_ln_bias, L1_ffn_shared_in_w, L1_ffn_shared_out_w, L1_ffn_shared_out_b, L1_ffn_expert_in_w, L1_ffn_expert_out_weight, L1_ffn_expert_out_bias, L1_ffn_group_gate_w, L1_ffn_expert_gate_w, L1_ffn_group_bias, L1_ffn_expert_bias, L2_gnn_W, L2_ffn_gate_Wk, L2_ffn_gate_bk, L2_ffn_expert_queries, L2_ffn_Wqkv, L2_ffn_bqkv, L2_ffn_Wo, L2_ffn_bo, L2_ffn_g1, L2_ffn_be1, L2_ffn_W1, L2_ffn_bf1, L2_ffn_W2, L2_ffn_bf2, L2_ffn_g2, L2_ffn_be2, L3_gnn_W, L3_ffn_Wg, L3_ffn_W1, L3_ffn_b1, L3_ffn_W2, L3_ffn_b2, L3_ffn_gamma, L3_ffn_beta):
    import jax
    import jax.numpy as jnp

    def _L0_gnn_ref(inputs, adj, W_stack):
        import jax, jax.numpy as jnp
        import numpy as np
        N = 4096
        D = 256
        L = 2
        NEG_SLOPE = 0.01

        def _gat_layer(x, W, adj):
            proj = x @ W
            Wh, Ws = jnp.split(proj, 2, axis=-1)
            scores = Wh @ Ws.T
            a = jax.nn.softmax(scores, axis=-1) * adj
            out = a @ Wh
            out = out + x
            return jax.nn.leaky_relu(out, NEG_SLOPE)
        x = inputs
        for l in range(W_stack.shape[0]):
            x = _gat_layer(x, W_stack[l], adj)
        return x

    def _L0_ffn_ref(x, Wr0, W1_0, b1_0, W2_0, b2_0, Wr1, W1_1, b1_1, W2_1, b2_1):
        import jax, jax.numpy as jnp
        import numpy as np
        D_MODEL = 256
        DFF = 1024
        TOP_K = 2
        EXPERTS_PER_LEVEL = (4, 8)

        def _moe_level(x, Wr, W1, b1, W2, b2, k):
            probs = jax.nn.softmax(jnp.einsum('bsd,de->bse', x, Wr), axis=-1)
            _, top_idx = jax.lax.top_k(probs, k)
            dispatch = jax.nn.one_hot(top_idx, probs.shape[-1], dtype=x.dtype).sum(axis=-2)
            xm = x[:, :, None, :] * dispatch[..., None]
            h = jax.nn.relu(jnp.einsum('bsed,edf->bsef', xm, W1) + b1)
            y = jnp.einsum('bsef,efd->bsed', h, W2) + b2
            return jnp.sum(y * probs[..., None], axis=2)
        h0 = _moe_level(x, Wr0, W1_0, b1_0, W2_0, b2_0, TOP_K)
        out = _moe_level(h0, Wr1, W1_1, b1_1, W2_1, b2_1, TOP_K)
        return out

    def _L1_gnn_ref(x, S, W, U):
        import jax, jax.numpy as jnp
        import numpy as np
        N = 4096
        D_IN = 256
        D_OUT = 256
        EDGE_P = 0.004

        def _xavier_uniform(key, fan_in, fan_out):
            bound = np.sqrt(6.0 / (fan_in + fan_out))
            return jax.random.uniform(key, (fan_in, fan_out), jnp.float32, -bound, bound)
        n = x.shape[0]
        S = S + jnp.eye(n, dtype=S.dtype)
        h = x @ W
        scores = h @ U @ h.T
        mask = S > 0
        scores = jnp.where(mask, scores, -jnp.inf)
        att = jax.nn.softmax(scores, axis=-1)
        att = att * mask.astype(att.dtype)
        S_tilde = S * att
        return S_tilde @ h

    def _L1_ffn_ref(x, ln_scale, ln_bias, shared_in_w, shared_out_w, shared_out_b, expert_in_w, expert_out_weight, expert_out_bias, group_gate_w, expert_gate_w, group_bias, expert_bias):
        import jax, jax.numpy as jnp
        import numpy as np
        B, T, C = (8, 512, 256)
        H = 512
        G, EG = (2, 4)
        E = G * EG
        K = 2
        LN_EPS = 1e-05

        def _swiglu(x):
            a, b = jnp.split(x, 2, axis=-1)
            return jax.nn.silu(a) * b
        Bx, Tx, Cx = x.shape
        S = Bx * Tx
        flat = x.reshape(S, Cx)
        mu = flat.mean(-1, keepdims=True)
        var = ((flat - mu) ** 2).mean(-1, keepdims=True)
        flat = (flat - mu) * jax.lax.rsqrt(var + LN_EPS) * ln_scale + ln_bias
        h_shared = _swiglu(flat @ shared_in_w.T)
        out_shared = h_shared @ shared_out_w.T + shared_out_b
        g_logits = flat @ group_gate_w.T + group_bias
        g_idx = jnp.argmax(g_logits, axis=-1)
        e_logits = (flat @ expert_gate_w.T).reshape(S, G, EG)
        e_sel = jnp.take_along_axis(e_logits, g_idx[:, None, None], axis=1)[:, 0, :]
        e_sel = e_sel + expert_bias.reshape(G, EG)[g_idx]
        e_probs = jax.nn.softmax(e_sel, axis=-1)
        topv, topi = jax.lax.top_k(e_probs, K)
        topv = topv / (topv.sum(-1, keepdims=True) + 1e-08)
        disp = g_idx[:, None] * EG + topi
        h_expert = _swiglu(flat @ expert_in_w.T)
        rows = jnp.arange(S)[:, None]
        comb = jnp.zeros((S, E), flat.dtype).at[rows, disp].add(topv)
        cnt = jnp.zeros((S, E), flat.dtype).at[rows, disp].add(1.0)
        routed = cnt @ expert_out_bias
        for e in range(E):
            routed = routed + comb[:, e:e + 1] * (h_expert @ expert_out_weight[e].T)
        return (out_shared + routed).reshape(Bx, Tx, Cx)

    def _L2_gnn_ref(input, A, W):
        import jax, jax.numpy as jnp
        import numpy as np
        N = 4096
        D = 256
        hidden = input * W
        return A @ hidden

    def _L2_ffn_ref(x, gate_Wk, gate_bk, expert_queries, Wqkv, bqkv, Wo, bo, g1, be1, W1, bf1, W2, bf2, g2, be2):
        import jax, jax.numpy as jnp
        import numpy as np
        B, S, D, F, E, K, H = (4, 512, 256, 1024, 8, 2, 8)
        HEAD_DIM = D // H

        def _layernorm(x, g, b):
            m = x.mean(-1, keepdims=True)
            v = ((x - m) ** 2).mean(-1, keepdims=True)
            return (x - m) * jax.lax.rsqrt(v + 1e-05) * g + b

        def _expert(x, Wqkv, bqkv, Wo, bo, g1, be1, W1, bf1, W2, bf2, g2, be2):
            b, s, d = x.shape
            qkv = x @ Wqkv.T + bqkv
            q, k, v = jnp.split(qkv, 3, axis=-1)
            to_heads = lambda t: t.reshape(b, s, H, HEAD_DIM).transpose(0, 2, 1, 3)
            q, k, v = (to_heads(q), to_heads(k), to_heads(v))
            scale = 1.0 / np.sqrt(HEAD_DIM).astype(np.float32)
            attn = jax.nn.softmax(jnp.einsum('bhqd,bhkd->bhqk', q * scale, k), axis=-1)
            ctx = jnp.einsum('bhqk,bhkd->bhqd', attn, v).transpose(0, 2, 1, 3).reshape(b, s, d)
            ctx = ctx @ Wo.T + bo
            x = _layernorm(x + ctx, g1, be1)
            h = jax.nn.gelu(x @ W1.T + bf1, approximate=False)
            h = jax.nn.gelu(h @ W2.T + bf2, approximate=False)
            return _layernorm(x + h, g2, be2)
        keys = x @ gate_Wk.T + gate_bk
        scores = jnp.einsum('bsd,ed->bse', keys, expert_queries) * D ** (-0.5)
        probs = jax.nn.softmax(scores, axis=-1)
        _, idx = jax.lax.top_k(probs, K)
        mask = jax.nn.one_hot(idx, E, dtype=probs.dtype).sum(-2)
        gated = probs * mask
        gated = gated / (gated.sum(-1, keepdims=True) + 1e-09)
        eo = jax.vmap(_expert, in_axes=(None,) + (0,) * 12)(x, Wqkv, bqkv, Wo, bo, g1, be1, W1, bf1, W2, bf2, g2, be2)
        return jnp.einsum('ebsd,bse->bsd', eo, gated)

    def _L3_gnn_ref(X, A_hat, W):
        import jax, jax.numpy as jnp
        import numpy as np
        KAPPA = -1.0
        EPS = 1e-10
        N, D_IN, D_OUT = (4096, 256, 256)

        def _artan_k(x):
            sc = np.sqrt(-KAPPA)
            return jnp.arctanh(jnp.clip(sc * x, -1.0 + 1e-07, 1.0 - 1e-07)) / sc

        def _tan_k(x):
            sc = np.sqrt(-KAPPA)
            return jnp.tanh(sc * x) / sc

        def _clamp_abs(x, eps=EPS):
            return jnp.where(x >= 0, 1.0, -1.0) * jnp.maximum(jnp.abs(x), eps)

        def _norm(x):
            return jnp.sqrt(jnp.maximum(jnp.sum(x * x, axis=-1, keepdims=True), EPS * EPS))

        def mobius_matvec(W, x):
            x_norm = _norm(x)
            mx = x @ W
            mx_norm = _norm(mx)
            res = _tan_k(mx_norm / x_norm * _artan_k(x_norm)) * (mx / mx_norm)
            return jnp.where(mx_norm <= EPS, 0.0, res)

        def mobius_scalar_mul(r, x):
            x_norm = _norm(x)
            return _tan_k(r * _artan_k(x_norm)) * (x / x_norm)

        def weighted_midpoint_lincomb(A, X):
            gamma = jnp.maximum(2.0 / (1.0 + KAPPA * jnp.sum(X * X, axis=-1, keepdims=True)), 1e-15)
            denom = _clamp_abs(A @ (gamma - 1.0))
            nom = A @ (gamma * X)
            two_mean = nom / denom
            sq = jnp.sum(two_mean * two_mean, axis=-1, keepdims=True)
            a_mean = two_mean / (1.0 + jnp.sqrt(jnp.maximum(1.0 + KAPPA * sq, EPS)))
            alpha = jnp.sum(A, axis=-1, keepdims=True)
            return mobius_scalar_mul(alpha, a_mean)

        def logmap0(x):
            xn = _norm(x)
            return _artan_k(xn) * x / xn

        def expmap0(u):
            un = _norm(u)
            return _tan_k(un) * u / un
        XW = mobius_matvec(W, X)
        AXW = weighted_midpoint_lincomb(A_hat, XW)
        return expmap0(jax.nn.relu(logmap0(AXW)))

    def _L3_ffn_ref(x, Wg, W1, b1, W2, b2, gamma, beta):
        import jax, jax.numpy as jnp
        import numpy as np
        EPS = 1e-05
        TOP_K = 2

        def _moe_forward(x, Wg, W1, b1, W2, b2, gamma, beta):
            B, S, D = x.shape
            xf = x.reshape(-1, D)
            logits = xf @ Wg
            topv, topi = jax.lax.top_k(logits, TOP_K)
            gate_w = jax.nn.softmax(topv, axis=-1)
            h = jax.nn.relu(jnp.einsum('td,edh->teh', xf, W1) + b1[None])
            y = jnp.einsum('teh,ehd->ted', h, W2) + b2[None]
            mu = jnp.mean(y, axis=-1, keepdims=True)
            var = jnp.mean((y - mu) ** 2, axis=-1, keepdims=True)
            y = (y - mu) / jnp.sqrt(var + EPS) * gamma[None] + beta[None]
            y_sel = jnp.take_along_axis(y, topi[:, :, None], axis=1)
            out = jnp.sum(gate_w[:, :, None] * y_sel, axis=1)
            return out.reshape(B, S, D)
        return _moe_forward(x, Wg, W1, b1, W2, b2, gamma, beta)
    x = x + _L0_gnn_ref(_layernorm(x, axis=-1), adj, L0_gnn_W_stack)
    x = x + _L0_ffn_ref(_layernorm(x, axis=-1)[None], L0_ffn_Wr0, L0_ffn_W1_0, L0_ffn_b1_0, L0_ffn_W2_0, L0_ffn_b2_0, L0_ffn_Wr1, L0_ffn_W1_1, L0_ffn_b1_1, L0_ffn_W2_1, L0_ffn_b2_1)[0]
    x = x + _L1_gnn_ref(_layernorm(x, axis=-1), adj, L1_gnn_W, L1_gnn_U)
    x = x + _L1_ffn_ref(_layernorm(x, axis=-1)[None], L1_ffn_ln_scale, L1_ffn_ln_bias, L1_ffn_shared_in_w, L1_ffn_shared_out_w, L1_ffn_shared_out_b, L1_ffn_expert_in_w, L1_ffn_expert_out_weight, L1_ffn_expert_out_bias, L1_ffn_group_gate_w, L1_ffn_expert_gate_w, L1_ffn_group_bias, L1_ffn_expert_bias)[0]
    x = x + _L2_gnn_ref(_layernorm(x, axis=-1), adj, L2_gnn_W)
    x = x + _L2_ffn_ref(_layernorm(x, axis=-1)[None], L2_ffn_gate_Wk, L2_ffn_gate_bk, L2_ffn_expert_queries, L2_ffn_Wqkv, L2_ffn_bqkv, L2_ffn_Wo, L2_ffn_bo, L2_ffn_g1, L2_ffn_be1, L2_ffn_W1, L2_ffn_bf1, L2_ffn_W2, L2_ffn_bf2, L2_ffn_g2, L2_ffn_be2)[0]
    x = x + _L3_gnn_ref(_layernorm(x, axis=-1), adj, L3_gnn_W)
    x = x + _L3_ffn_ref(_layernorm(x, axis=-1)[None], L3_ffn_Wg, L3_ffn_W1, L3_ffn_b1, L3_ffn_W2, L3_ffn_b2, L3_ffn_gamma, L3_ffn_beta)[0]
    return x

_drawn_inputs = setup_inputs


def setup_inputs(seed=0):
    import zlib

    import numpy as np

    out = dict(_drawn_inputs(seed))
    spreads = {'L1_ffn_ln_scale': (1.0, 0.2),
     'L1_ffn_ln_bias': (0.0, 0.1),
     'L1_ffn_shared_out_b': (0.0, 0.1),
     'L1_ffn_expert_out_bias': (0.0, 0.1),
     'L1_ffn_group_bias': (0.0, 0.1),
     'L1_ffn_expert_bias': (0.0, 0.1),
     'L2_gnn_W': (1.0, 0.2),
     'L2_ffn_gate_bk': (0.0, 0.1),
     'L2_ffn_bqkv': (0.0, 0.8),
     'L2_ffn_bo': (0.0, 0.304),
     'L2_ffn_g1': (1.0, 0.2),
     'L2_ffn_be1': (0.0, 0.331),
     'L2_ffn_bf1': (0.0, 0.8),
     'L2_ffn_bf2': (0.0, 0.613),
     'L2_ffn_g2': (1.0, 0.2),
     'L2_ffn_be2': (0.0, 0.307),
     'L3_ffn_gamma': (1.0, 0.2),
     'L3_ffn_beta': (0.0, 0.509)}
    factors = {'L0_ffn_b1_0': 6.078,
     'L0_ffn_b2_0': 3.39,
     'L0_ffn_b1_1': 5.875,
     'L0_ffn_b2_1': 3.91,
     'L1_ffn_expert_in_w': 3.262,
     'L1_ffn_expert_out_weight': 3.043,
     'L2_ffn_Wqkv': 7.824,
     'L2_ffn_Wo': 5.174,
     'L2_ffn_W1': 3.587,
     'L2_ffn_W2': 3.468,
     'L3_gnn_W': 2.995,
     'L3_ffn_b1': 5.682}
    for name, (base, spread) in spreads.items():
        noise = np.random.default_rng([zlib.crc32(name.encode()), seed]).standard_normal(out[name].shape)
        drawn = base * np.exp(spread * noise) if base else spread * noise
        out[name] = jnp.asarray(drawn.astype(out[name].dtype))
    for name, factor in factors.items():
        out[name] = (out[name] * factor).astype(out[name].dtype)
    return out
```

```python
from contextlib import ExitStack

import numpy as np

import concourse.bass as bass
from concourse import mybir

F32 = mybir.dt.float32
F32R = mybir.dt.float32r
BF16 = mybir.dt.bfloat16
ALU = mybir.AluOpType
ACT = mybir.ActivationFunctionType
AX_X = mybir.AxisListType.X

P = 128
N = 1354
D = 256
KD = D // P
NB = -(-N // P)
NP = NB * P
CH = 3
CW = -(-N // CH)
NT = CH * CW
TG = [(0, 4), (4, 4), (8, 3)]
KCH = [(0, 512), (512, 512), (1024, N - 1024)]
BANK = 512
LN_EPS = 1e-5
BIG = 1e30
FF = 1024
FT = FF // P
LOG2_HALF_ULP = 1.1920929e-07


class Pool:

    def __init__(self, nc, ctx, tag):
        self.nc, self.ctx, self.tag = nc, ctx, tag

    def sb(self, name, shape, dt=F32):
        return self.ctx.enter_context(self.nc.sbuf_tensor(f"{self.tag}_{name}", shape, dt))

    def ps(self, name, shape, dt=F32):
        return self.ctx.enter_context(self.nc.psum_tensor(f"{self.tag}_{name}", shape, dt))

    def sem(self, name):
        return self.ctx.enter_context(self.nc.semaphore(f"{self.tag}_{name}"))


def chain(eng, sem, count=0):
    n = [count]

    def link(instruction):
        n[0] += 1
        instruction.then_inc(sem, 1)
        eng.wait_ge(sem, n[0])
    return link


def over(col, width):
    return col.unsqueeze(2).to_broadcast([P, NB, width])



def stage_load(nc, g, x):
    with ExitStack() as ctx:
        s = Pool(nc, ctx, "load")
        x_loaded, zeroed, made = s.sem("x_loaded"), s.sem("zeroed"), s.sem("made")
        block = ctx.enter_context(nc.Block())

        @block.sync
        def _(sync):
            sync.dma_start(g.x[:], x.rearrange("(b p) d -> p b d", p=P)).then_inc(x_loaded, 16)
            sync.wait_ge(x_loaded, 16)

        @block.gpsimd
        def _(pool):
            nc.gpsimd.memset(g.ident[:], 0.0).then_inc(zeroed, 1)
            pool.wait_ge(zeroed, 1)
            nc.gpsimd.affine_select(out=g.ident[:], in_=g.ident[:], compare_op=ALU.not_equal, fill=1.0, base=0,
                                    pattern=[[-1, P]], channel_multiplier=1).then_inc(made, 1)
            nc.gpsimd.memset(g.eps[:], LN_EPS).then_inc(made, 1)
            nc.gpsimd.memset(g.one[:], 1.0).then_inc(made, 1)
            for e in range(8):
                nc.gpsimd.memset(g.ramp[:, :, e], float(8 - e)).then_inc(made, 1)
            pool.wait_ge(made, 11)


def stage_adjacency(nc, g, tag, adj_t):
    g.adj_loads += 1
    with ExitStack() as ctx:
        block = ctx.enter_context(nc.Block())

        @block.gpsimd
        def _(pool):
            pool.dma_start(g.adj_t[:], adj_t.rearrange("(b p) q -> p b q", p=P)).then_inc(g.adj_loaded, 16)
            pool.wait_ge(g.adj_loaded, 16 * g.adj_loads)



def stage_norm(nc, g, tag, src, dst, dst_t, gain=None, shift=None):
    with ExitStack() as ctx:
        s = Pool(nc, ctx, tag)
        stats = s.sb("stats", [P, NB, 6])
        mean_var = s.sb("mean_var", [P, NB, 2])
        std = s.sb("std", [P, NB])
        rstd = s.sb("rstd", [P, NB])
        turned = [s.ps(f"turned{i}", [P, BANK]) for i in range(4)]
        v_step, std_done, normed = s.sem("v_step"), s.sem("std_done"), s.sem("normed")
        turned_full, turned_read = s.sem("turned_full"), s.sem("turned_read")
        normalise = dst is not None
        out = dst if normalise else src
        block = ctx.enter_context(nc.Block())

        if normalise:
            @block.vector
            def _(dve):
                for b in range(NB):
                    nc.vector.bn_stats(stats[:, b, :], src[:, b, :]).then_inc(v_step, 1)
                dve.wait_ge(v_step, NB)
                for b in range(NB):
                    nc.vector.bn_aggr(mean_var[:, b, :], stats[:, b, :]).then_inc(v_step, 1)
                dve.wait_ge(std_done, 1)
                nc.vector.reciprocal(rstd[:], std[:]).then_inc(v_step, 1)
                dve.wait_ge(v_step, 2 * NB + 1)
                for b in range(NB):
                    nc.vector.tensor_scalar(dst[:, b, :], src[:, b, :], mean_var[:, b, 0:1], rstd[:, b:b + 1],
                                            ALU.subtract, ALU.mult).then_inc(normed, 1)

        @block.tensor
        def _(pe):
            t = 0
            for b0, nb in TG:
                for k in range(KD):
                    if t >= 4:
                        pe.wait_ge(turned_read, t - 3)
                    for b in range(b0, b0 + nb):
                        if normalise:
                            pe.wait_ge(normed, b + 1)
                        last = nc.tensor.transpose(turned[t % 4][:, (b - b0) * P:(b - b0 + 1) * P],
                                                   out[:, b, k * P:(k + 1) * P], g.ident[:])
                    last.then_inc(turned_full, 1)
                    t += 1

        @block.scalar
        def _(act):
            if normalise:
                act.wait_ge(v_step, 2 * NB)
                nc.scalar.activation(std[:], mean_var[:, :, 1], ACT.Sqrt, bias=g.eps[:]).then_inc(std_done, 1)
            t = 0
            for b0, nb in TG:
                for k in range(KD):
                    act.wait_ge(turned_full, t + 1)
                    into = dst_t[:, k, b0 * P:(b0 + nb) * P]
                    if gain is None:
                        nc.scalar.activation(into, turned[t % 4][:, 0:nb * P], ACT.Copy).then_inc(turned_read, 1)
                    else:
                        nc.scalar.activation(into, turned[t % 4][:, 0:nb * P], ACT.Identity, scale=gain[:, k:k + 1],
                                             bias=shift[:, k:k + 1]).then_inc(turned_read, 1)
                    t += 1



def stage_project(nc, g, tag, src_t, w_dram, feature_major, token_major):
    cols = w_dram.shape[1]
    tiles = [(c0 + j * P, target, j) for c0, target in feature_major for j in range(KD)]
    with ExitStack() as ctx:
        s = Pool(nc, ctx, tag)
        w = s.sb("w", [P, KD, cols])
        wide = [s.ps(f"wide{i}", [P, CH, BANK]) for i in range(2)]
        row = [s.ps(f"row{i}", [P, BANK]) for i in range(2)]
        w_loaded, pads_zero = s.sem("w_loaded"), s.sem("pads_zero")
        wide_full, row_full = s.sem("wide_full"), s.sem("row_full")
        wide_read_act, wide_read_dve = s.sem("wide_read_act"), s.sem("wide_read_dve")
        row_read_act, row_read_dve = s.sem("row_read_act"), s.sem("row_read_dve")
        block = ctx.enter_context(nc.Block())

        @block.sync
        def _(sync):
            sync.dma_start(w[:], w_dram.rearrange("(k p) o -> p k o", p=P)).then_inc(w_loaded, 16)

        @block.gpsimd
        def _(pool):
            for _, target in feature_major:
                nc.gpsimd.memset(target[:, :, NT:NP], 0.0).then_inc(pads_zero, 1)
            pool.wait_ge(pads_zero, len(feature_major))

        @block.tensor
        def _(pe):
            pe.wait_ge(w_loaded, 16)
            for t, (c0, _, _) in enumerate(tiles):
                if t >= 2:
                    pe.wait_ge([wide_read_act, wide_read_dve][t % 2], t // 2)
                for c in range(CH):
                    for k in range(KD):
                        last = nc.tensor.matmul(wide[t % 2][:, c, 0:CW], w[:, k, c0:c0 + P],
                                                src_t[:, k, c * CW:(c + 1) * CW], start=(k == 0), stop=(k == KD - 1))
                last.then_inc(wide_full, 1)
            if token_major:
                c0 = token_major[0]
                for b in range(NB):
                    if b >= 2:
                        pe.wait_ge([row_read_act, row_read_dve][b % 2], b // 2)
                    for k in range(KD):
                        last = nc.tensor.matmul(row[b % 2][:, 0:D], src_t[:, k, b * P:(b + 1) * P],
                                                w[:, k, c0:c0 + D], start=(k == 0), stop=(k == KD - 1))
                    last.then_inc(row_full, 1)

        def drain(eng, copy, parity, wide_read, row_read):
            for t, (_, target, j) in enumerate(tiles):
                if t % 2 == parity:
                    eng.wait_ge(wide_full, t + 1)
                    copy(target[:, j, 0:NT].rearrange("p (c n) -> p c n", c=CH), wide[t % 2][:, :, 0:CW])\
                        .then_inc(wide_read, 1)
            if token_major:
                for b in range(parity, NB, 2):
                    eng.wait_ge(row_full, b + 1)
                    copy(token_major[1][:, b, :], row[b % 2][:, 0:D]).then_inc(row_read, 1)

        @block.scalar
        def _(act):
            drain(act, lambda o, i: nc.scalar.activation(o, i, ACT.Copy), 0, wide_read_act, row_read_act)

        @block.vector
        def _(dve):
            drain(dve, nc.vector.tensor_copy, 1, wide_read_dve, row_read_dve)



def stage_graph_attention(nc, g, tag, q_t, k_t, v, finish, masked_rows=None):
    with ExitStack() as ctx:
        s = Pool(nc, ctx, tag)
        e = [s.sb(f"e{i}", [P, NP]) for i in range(2)]
        e_t = s.sb("e_t", [P, NB, P])
        neg_max = s.sb("neg_max", [P, NB])
        row_sum = s.sb("row_sum", [P, NB])
        inv = s.sb("inv", [P, NB])
        scratch = s.sb("scratch", [P, D])
        scores = [s.ps(f"scores{i}", [P, CH * BANK]) for i in range(2)]
        turned = s.ps("turned", [P, BANK])
        out = s.ps("out", [P, BANK])
        scores_full, turned_full, out_full = s.sem("scores_full"), s.sem("turned_full"), s.sem("out_full")
        max_done, exp_done, e_pad = s.sem("max_done"), s.sem("exp_done"), s.sem("e_pad")
        e_t_done, finished, v_step = s.sem("e_t_done"), s.sem("finished"), s.sem("v_step")
        if masked_rows is not None:
            rows = [s.sb(f"rows{i}", [P, N]) for i in range(2)]
            kept = [s.sb(f"kept{i}", [P, N]) for i in range(2)]
            rows_loaded, bias_done = [s.sem(f"rows_loaded{i}") for i in range(2)], s.sem("bias_done")
            pool_step, self_added = s.sem("pool_step"), s.sem("self_added")
        block = ctx.enter_context(nc.Block())

        if masked_rows is not None:
            @block.sync
            def _(sync):
                for b in range(NB):
                    if b >= 2:
                        sync.wait_ge(max_done, b - 1)
                    sync.dma_start(rows[b % 2][:], masked_rows[b * P:(b + 1) * P, 0:N]).then_inc(rows_loaded[b % 2], 16)

        @block.gpsimd
        def _(pool):
            for i in range(2):
                nc.gpsimd.memset(e[i][:, N:NP], 0.0).then_inc(e_pad, 1)
            if masked_rows is not None:
                link = chain(pool, pool_step)
                for b in range(NB):
                    own = g.adj_t[:, b, b * P:(b + 1) * P]
                    nc.gpsimd.tensor_tensor(own, own, g.ident[:], ALU.add).then_inc(self_added, 1)
                for b in range(NB):
                    pool.wait_ge(rows_loaded[b % 2], 16 * (b // 2 + 1))
                    r = rows[b % 2]
                    nc_last = nc.gpsimd.tensor_scalar(r[:], r[:], -1.0, BIG, ALU.add, ALU.mult)
                    link(nc_last)
                    w = min(P, N - b * P)
                    own = r[:, b * P:b * P + w]
                    nc.gpsimd.affine_select(out=own, in_=own, compare_op=ALU.not_equal, fill=0.0, base=0,
                                            pattern=[[-1, w]], channel_multiplier=1).then_inc(bias_done, 1)
                pool.wait_ge(e_t_done, CH * NB)
                for b in range(NB):
                    own = g.adj_t[:, b, b * P:(b + 1) * P]
                    nc.gpsimd.tensor_tensor(own, own, g.ident[:], ALU.subtract).then_inc(self_added, 1)
                pool.wait_ge(self_added, 2 * NB)
            pool.wait_ge(e_pad, 2)

        @block.tensor
        def _(pe):
            def score(b, c):
                if c == 0 and b >= 2:
                    pe.wait_ge(max_done if masked_rows is not None else exp_done, b - 1)
                k0, w = KCH[c]
                for k in range(KD):
                    last = nc.tensor.matmul(scores[b % 2][:, k0:k0 + w], q_t[:, k, b * P:(b + 1) * P],
                                            k_t[:, k, k0:k0 + w], start=(k == 0), stop=(k == KD - 1))
                if c == CH - 1:
                    last.then_inc(scores_full, 1)

            def turn(b, c):
                if c == 0:
                    pe.wait_ge(exp_done, b + 1)
                    pe.wait_ge(e_pad, 2)
                if b + c:
                    pe.wait_ge(e_t_done, CH * b + c)
                t0, n = TG[c]
                for t in range(t0, t0 + n):
                    last = nc.tensor.transpose(turned[:, (t - t0) * P:(t - t0 + 1) * P],
                                               e[b % 2][:, t * P:(t + 1) * P], g.ident[:])
                last.then_inc(turned_full, 1)

            def mix(b):
                pe.wait_ge(e_t_done, CH * (b + 1))
                if b:
                    pe.wait_ge(finished, b)
                for t in range(NB):
                    last = nc.tensor.matmul(out[:, 0:D], e_t[:, t, :], v[:, t, :], start=(t == 0), stop=(t == NB - 1))
                last.then_inc(out_full, 1)

            for c in range(CH):
                score(0, c)
            for b in range(NB):
                for c in range(CH):
                    turn(b, c)
                    if b + 1 < NB:
                        score(b + 1, c)
                mix(b)

        @block.scalar
        def _(act):
            for b in range(NB):
                act.wait_ge(max_done, b + 1)
                if b >= 2:
                    act.wait_ge(turned_full, CH * (b - 1))
                seen = scores[b % 2][:, 0:N] if masked_rows is None else kept[b % 2][:]
                nc.scalar.activation(e[b % 2][:, 0:N], seen, ACT.Exp, bias=neg_max[:, b:b + 1],
                                     accum_out=row_sum[:, b:b + 1]).then_inc(exp_done, 1)

        @block.vector
        def _(dve):
            link = chain(dve, v_step)

            def row_max(b):
                dve.wait_ge(scores_full, b + 1)
                if masked_rows is None:
                    nc.vector.tensor_reduce(neg_max[:, b:b + 1], scores[b % 2][:, 0:N], AX_X, ALU.max, negate=True)\
                        .then_inc(max_done, 1)
                    return
                dve.wait_ge(bias_done, b + 1)
                if b >= 2:
                    dve.wait_ge(exp_done, b - 1)
                link(nc.vector.tensor_tensor(kept[b % 2][:], scores[b % 2][:, 0:N], rows[b % 2][:], ALU.add))
                nc.vector.tensor_reduce(neg_max[:, b:b + 1], kept[b % 2][:], AX_X, ALU.max, negate=True)\
                    .then_inc(max_done, 1)

            row_max(0)
            if masked_rows is not None:
                dve.wait_ge(self_added, NB)
            for b in range(NB):
                for c, (t0, n) in enumerate(TG):
                    dve.wait_ge(turned_full, CH * b + c + 1)
                    if b:
                        dve.wait_ge(out_full, b)
                    nc.vector.tensor_tensor(e_t[:, t0:t0 + n, :],
                                            turned[:, 0:n * P].rearrange("p (t q) -> p t q", q=P),
                                            g.adj_t[:, t0:t0 + n, b * P:(b + 1) * P], ALU.mult).then_inc(e_t_done, 1)
                if b + 1 < NB:
                    row_max(b + 1)
                link(nc.vector.reciprocal(inv[:, b:b + 1], row_sum[:, b:b + 1]))
                dve.wait_ge(out_full, b + 1)
                finish(link, b, out[:, 0:D], inv[:, b:b + 1], scratch).then_inc(finished, 1)
            dve.wait_ge(finished, NB)


def gat_layers(nc, g, w_stack):
    layers = w_stack.shape[0]
    for layer in range(layers):
        with ExitStack() as ctx:
            s = Pool(nc, ctx, f"gat{layer}")
            wh_t, ws_t, wh = s.sb("wh_t", [P, KD, NP]), s.sb("ws_t", [P, KD, NP]), s.sb("wh", [P, NB, D])
            stage_project(nc, g, f"gat{layer}p", g.xn_t, w_stack[layer], [(0, wh_t), (D, ws_t)], (0, wh))
            last_layer = layer == layers - 1

            def finish(link, b, out, inv, scratch):
                link(nc.vector.scalar_tensor_tensor(out=scratch[:], in0=out, scalar=inv, in1=g.xn[:, b, :],
                                                    op0=ALU.mult, op1=ALU.add))
                leaky = nc.vector.scalar_tensor_tensor(out=g.xn[:, b, :], in0=scratch[:], scalar=0.01, in1=scratch[:],
                                                       op0=ALU.mult, op1=ALU.max)
                if not last_layer:
                    return leaky
                link(leaky)
                return nc.vector.tensor_tensor(g.x[:, b, :], g.x[:, b, :], g.xn[:, b, :], ALU.add)

            stage_graph_attention(nc, g, f"gat{layer}a", wh_t, ws_t, wh, finish)
        if not last_layer:
            stage_norm(nc, g, f"gat{layer}t", g.xn, None, g.xn_t)


def masked_attention(nc, g, w, u, adj):
    with ExitStack() as ctx:
        s = Pool(nc, ctx, "nbr")
        h_t, hu_t, h = s.sb("h_t", [P, KD, NP]), s.sb("hu_t", [P, KD, NP]), s.sb("h", [P, NB, D])
        stage_project(nc, g, "nbrh", g.xn_t, w, [(0, h_t)], (0, h))
        stage_project(nc, g, "nbru", h_t, u, [(0, hu_t)], None)

        def finish(link, b, out, inv, scratch):
            return nc.vector.scalar_tensor_tensor(out=g.x[:, b, :], in0=out, scalar=inv, in1=g.x[:, b, :],
                                                  op0=ALU.mult, op1=ALU.add)

        stage_graph_attention(nc, g, "nbra", hu_t, h_t, h, finish, masked_rows=adj)



def top_two(link, nc, g, values, mask, work, work2, col, width, below):
    ramp = g.ramp[:, :, 0:width]
    left = values
    for turn in range(2):
        link(nc.vector.tensor_reduce(col, left, AX_X, ALU.max))
        link(nc.vector.tensor_tensor(work, left, over(col, width), ALU.is_equal))
        link(nc.vector.tensor_tensor(work, work, ramp, ALU.mult))
        link(nc.vector.tensor_reduce(col, work, AX_X, ALU.max))
        link(nc.vector.tensor_tensor(work, work, over(col, width), ALU.is_equal))
        if turn == 0:
            link(nc.vector.tensor_copy(mask, work))
            link(nc.vector.tensor_scalar(work2, work, -below, None, ALU.mult))
            link(nc.vector.tensor_tensor(work2, work2, values, ALU.add))
            left = work2
        else:
            link(nc.vector.tensor_tensor(mask, mask, work, ALU.add))


def softmax_to(link, nc, dve, values, probs, col, width, exp_asked, exp_done, n):
    link(nc.vector.tensor_reduce(col, values, AX_X, ALU.max))
    nc.vector.tensor_tensor(probs, values, over(col, width), ALU.subtract).then_inc(exp_asked, 1)
    dve.wait_ge(exp_done, n)


def divide_by_sum(link, nc, values, col, width, eps=None):
    link(nc.vector.tensor_reduce(col, values, AX_X, ALU.add))
    if eps is not None:
        link(nc.vector.tensor_scalar(col, col, eps, None, ALU.add))
    link(nc.vector.reciprocal(col, col))
    link(nc.vector.tensor_tensor(values, values, over(col, width), ALU.mult))


def stage_route(nc, g, tag, src_t, gate, width, rule, weights, mask, bias=None, keys=None):
    with ExitStack() as ctx:
        s = Pool(nc, ctx, tag)
        w = s.sb("w", [P, KD, width])
        logits = s.sb("logits", [P, NB, width])
        work = [s.sb(f"work{i}", [P, NB, 8]) for i in range(4)]
        cols = [s.sb(f"col{i}", [P, NB]) for i in range(3)]
        ps = s.ps("ps", [P, NB, width])
        w_loaded, full, v_step = s.sem("w_loaded"), s.sem("full"), s.sem("v_step")
        exp_asked, exp_done = s.sem("exp_asked"), s.sem("exp_done")
        if bias is not None:
            bias_all = s.sb("bias_all", [P, width])
        if keys is not None:
            wk = s.sb("wk", [P, KD, D])
            bk = s.sb("bk", [P, KD])
            keys_t = s.sb("keys_t", [P, KD, NP])
            wide = [s.ps(f"wide{i}", [P, CH, BANK]) for i in range(2)]
            keys_full, keys_done, pads = s.sem("keys_full"), s.sem("keys_done"), s.sem("pads")
        weights_view = weights[:] if rule != "grouped" else work[3][:, :, 0:4]
        loads = 1 + (bias is not None) + 2 * (keys is not None)
        block = ctx.enter_context(nc.Block())

        @block.sync
        def _(sync):
            sync.dma_start(w[:], gate.rearrange("(k p) e -> p k e", p=P)).then_inc(w_loaded, 16)
            if bias is not None:
                sync.dma_start(bias_all[:], bias.partition_broadcast(P)).then_inc(w_loaded, 16)
            if keys is not None:
                sync.dma_start(wk[:], keys[0].rearrange("(k p) o -> p k o", p=P)).then_inc(w_loaded, 16)
                sync.dma_start(bk[:], keys[1]).then_inc(w_loaded, 16)

        if keys is not None:
            @block.gpsimd
            def _(pool):
                nc.gpsimd.memset(keys_t[:, :, NT:NP], 0.0).then_inc(pads, 1)

        @block.tensor
        def _(pe):
            pe.wait_ge(w_loaded, 16 * loads)
            seen = src_t
            if keys is not None:
                for j in range(KD):
                    for c in range(CH):
                        for k in range(KD):
                            last = nc.tensor.matmul(wide[j][:, c, 0:CW], wk[:, k, j * P:(j + 1) * P],
                                                    src_t[:, k, c * CW:(c + 1) * CW], start=(k == 0), stop=(k == KD - 1))
                    last.then_inc(keys_full, 1)
                pe.wait_ge(keys_done, KD)
                pe.wait_ge(pads, 1)
                seen = keys_t
            for b in range(NB):
                for k in range(KD):
                    last = nc.tensor.matmul(ps[:, b, :], seen[:, k, b * P:(b + 1) * P], w[:, k, :],
                                            start=(k == 0), stop=(k == KD - 1))
            last.then_inc(full, 1)

        @block.scalar
        def _(act):
            if keys is not None:
                act.wait_ge(w_loaded, 16 * loads)
                for j in range(KD):
                    act.wait_ge(keys_full, j + 1)
                    nc.scalar.activation(keys_t[:, j, 0:NT].rearrange("p (c n) -> p c n", c=CH), wide[j][:, :, 0:CW],
                                         ACT.Identity, bias=bk[:, j:j + 1]).then_inc(keys_done, 1)
            act.wait_ge(exp_asked, 1)
            nc.scalar.activation(weights_view, weights_view, ACT.Exp).then_inc(exp_done, 1)

        @block.vector
        def _(dve):
            link = chain(dve, v_step)
            dve.wait_ge(full, 1)
            c0, c1, c2 = (c[:] for c in cols)
            if rule == "grouped":
                dve.wait_ge(w_loaded, 16 * loads)
                link(nc.vector.tensor_tensor(logits[:], ps[:], bias_all[:].unsqueeze(1).to_broadcast([P, NB, width]),
                                             ALU.add))
                first, second = c1, c2
                link(nc.vector.tensor_tensor(first, logits[:, :, 8], logits[:, :, 9], ALU.is_ge))
                link(nc.vector.tensor_scalar(second, first, -1.0, 1.0, ALU.mult, ALU.add))
                chosen, other, exps = work[0][:, :, 0:4], work[1][:, :, 0:4], work[3][:, :, 0:4]
                link(nc.vector.tensor_tensor(chosen, logits[:, :, 0:4], over(first, 4), ALU.mult))
                link(nc.vector.tensor_tensor(other, logits[:, :, 4:8], over(second, 4), ALU.mult))
                link(nc.vector.tensor_tensor(chosen, chosen, other, ALU.add))
                softmax_to(link, nc, dve, chosen, exps, c0, 4, exp_asked, exp_done, 1)
                divide_by_sum(link, nc, exps, c0, 4)
                picked = work[2][:, :, 4:8]
                top_two(link, nc, g, exps, picked, work[0][:, :, 0:4], work[1][:, :, 0:4], c0, 4, 2.0)
                link(nc.vector.tensor_tensor(exps, exps, picked, ALU.mult))
                divide_by_sum(link, nc, exps, c0, 4, 1e-8)
                for i, group in enumerate((first, second)):
                    link(nc.vector.tensor_tensor(weights[:, :, 4 * i:4 * i + 4], exps, over(group, 4), ALU.mult))
                    link(nc.vector.tensor_tensor(mask[:, :, 4 * i:4 * i + 4], picked, over(group, 4), ALU.mult))
                return
            scale = D ** -0.5 if rule == "keys" else 1.0
            link(nc.vector.tensor_scalar(logits[:], ps[:], scale, None, ALU.mult))
            a, b2 = work[0][:, :, 0:width], work[1][:, :, 0:width]
            softmax_to(link, nc, dve, logits[:], weights[:], c0, width, exp_asked, exp_done, 1)
            if rule == "logits":
                top_two(link, nc, g, logits[:], mask[:], a, b2, c0, width, BIG)
                link(nc.vector.tensor_tensor(weights[:], weights[:], mask[:], ALU.mult))
                divide_by_sum(link, nc, weights[:], c0, width)
                return
            divide_by_sum(link, nc, weights[:], c0, width)
            top_two(link, nc, g, weights[:], mask[:], a, b2, c0, width, 2.0)
            if rule == "keys":
                link(nc.vector.tensor_tensor(weights[:], weights[:], mask[:], ALU.mult))
                divide_by_sum(link, nc, weights[:], c0, width, 1e-9)


def stage_spread(nc, g, tag, coefficients, width, table_dram, acc, add, mask=None, mask_dram=None):
    with ExitStack() as ctx:
        s = Pool(nc, ctx, tag)
        table = s.sb("table", [width, D])
        turned_sb = s.sb("turned_sb", [width, NP])
        mask_sb = s.sb("mask_sb", [width, NP])
        turned = s.ps("turned", [width, CH, BANK])
        mask_ps = s.ps("mask_ps", [width, CH, BANK])
        row = [s.ps(f"row{i}", [P, BANK]) for i in range(2)]
        loaded, turned_full, turned_read = s.sem("loaded"), s.sem("turned_full"), s.sem("turned_read")
        row_full, row_read, stored = s.sem("row_full"), s.sem("row_read"), s.sem("stored")
        block = ctx.enter_context(nc.Block())

        @block.sync
        def _(sync):
            sync.dma_start(table[:], table_dram).then_inc(loaded, 16)
            if mask is not None:
                sync.wait_ge(turned_read, 2 * CH)
                sync.dma_start(mask_dram[0:width, :], mask_sb[:, 0:NT]).then_inc(stored, 16)
                sync.wait_ge(stored, 16)

        @block.tensor
        def _(pe):
            for src, into in ((coefficients, turned), (mask, mask_ps)):
                if src is None:
                    continue
                for c, (b0, n) in enumerate(TG):
                    for b in range(b0, b0 + n):
                        last = nc.tensor.transpose(into[:, c, (b - b0) * P:(b - b0 + 1) * P], src[:, b, :], g.ident[:])
                    last.then_inc(turned_full, 1)
            pe.wait_ge(turned_read, CH)
            pe.wait_ge(loaded, 16)
            for b in range(NB):
                if b >= 2:
                    pe.wait_ge(row_read, b - 1)
                nc.tensor.matmul(row[b % 2][:, 0:D], turned_sb[:, b * P:(b + 1) * P], table[:], start=True, stop=True)\
                    .then_inc(row_full, 1)

        @block.scalar
        def _(act):
            n_read = 0
            for src, into, sb in ((coefficients, turned, turned_sb), (mask, mask_ps, mask_sb)):
                if src is None:
                    continue
                for c, (b0, n) in enumerate(TG):
                    n_read += 1
                    act.wait_ge(turned_full, n_read)
                    nc.scalar.activation(sb[:, b0 * P:(b0 + n) * P], into[:, c, 0:n * P], ACT.Copy).then_inc(turned_read, 1)

        @block.vector
        def _(dve):
            for b in range(NB):
                dve.wait_ge(row_full, b + 1)
                if add:
                    nc.vector.tensor_tensor(acc[:, b, :], row[b % 2][:, 0:D], acc[:, b, :], ALU.add).then_inc(row_read, 1)
                else:
                    nc.vector.tensor_copy(acc[:, b, :], row[b % 2][:, 0:D]).then_inc(row_read, 1)



def stage_experts(nc, g, tag, src_t, w1_dram, b1_dram, w2_dram, weights, acc, mask_dram=None, norm=None):
    experts, _, hidden = w1_dram.shape
    ht = hidden // P
    with ExitStack() as ctx:
        s = Pool(nc, ctx, tag)
        w1, w2 = s.sb("w1", [P, KD, hidden]), s.sb("w2", [P, ht, D])
        b1 = s.sb("b1", [P, experts * ht])
        h = s.sb("h", [P, ht, NP])
        wide = [s.ps(f"wide{i}", [P, CH, BANK]) for i in range(2)]
        row = [s.ps(f"row{i}", [P, BANK]) for i in range(2)]
        w1_loaded, w2_loaded, b1_loaded = s.sem("w1_loaded"), s.sem("w2_loaded"), s.sem("b1_loaded")
        h_pad, wide_full, wide_read = s.sem("h_pad"), s.sem("wide_full"), s.sem("wide_read")
        row_full, row_read = s.sem("row_full"), s.sem("row_read")
        if mask_dram is not None:
            mask = s.sb("mask", [P, NT])
            xm = s.sb("xm", [P, KD, NT])
            mask_loaded, masked = s.sem("mask_loaded"), s.sem("masked")
        if norm is not None:
            b2, gamma = s.sb("b2", [P, D]), s.sb("gamma", [P, D])
            y = s.sb("y", [P, NB, D])
            z = [s.sb(f"z{i}", [P, D]) for i in range(2)]
            stats, mean_var = s.sb("stats", [P, NB, 6]), s.sb("mean_var", [P, NB, 2])
            std, scale, shift = s.sb("std", [P, NB]), s.sb("scale", [P, NB]), s.sb("shift", [P, NB])
            rows_loaded, std_done, scaled, z_full, z_used = (
                s.sem("rows_loaded"), s.sem("std_done"), s.sem("scaled"), s.sem("z_full"), s.sem("z_used"))
            tiles_seen = s.sem("tiles_seen")
            stats_done, v_step, added = s.sem("stats_done"), s.sem("v_step"), s.sem("added")
        x_in = src_t if mask_dram is None else xm
        w1_v = w1_dram.rearrange("e (k p) o -> e p k o", p=P)
        w2_v = w2_dram.rearrange("e (f p) o -> e p f o", p=P)
        block = ctx.enter_context(nc.Block())

        @block.sync
        def _(sync):
            def load_mask(e):
                if mask_dram is not None:
                    sync.dma_start(mask[:], mask_dram[e].partition_broadcast(P)).then_inc(mask_loaded, 16)

            def load_rows(e):
                if norm is not None:
                    sync.dma_start(b2[:], norm[0][e].partition_broadcast(P)).then_inc(rows_loaded, 16)
                    sync.dma_start(gamma[:], norm[1][e].partition_broadcast(P)).then_inc(rows_loaded, 16)

            load_mask(0)
            sync.dma_start(w1[:], w1_v[0]).then_inc(w1_loaded, 16)
            sync.dma_start(b1[:], b1_dram).then_inc(b1_loaded, 16)
            sync.dma_start(w2[:], w2_v[0]).then_inc(w2_loaded, 16)
            load_rows(0)
            with sync.Fori(1, experts) as e:
                if mask_dram is not None:
                    sync.wait_ge(masked, KD * e)
                    load_mask(e)
                sync.wait_ge(wide_full, ht * e)
                sync.dma_start(w1[:], w1_v[e]).then_inc(w1_loaded, 16)
                sync.wait_ge(row_full, NB * e)
                sync.dma_start(w2[:], w2_v[e]).then_inc(w2_loaded, 16)
                if norm is not None:
                    sync.wait_ge(added, NB * e)
                    load_rows(e)

        @block.gpsimd
        def _(pool):
            nc.gpsimd.memset(h[:, :, NT:NP], 0.0).then_inc(h_pad, 1)
            if mask_dram is not None:
                def apply_mask():
                    for k in range(KD):
                        nc.gpsimd.tensor_tensor(xm[:, k, :], src_t[:, k, 0:NT], mask[:], ALU.mult).then_inc(masked, 1)

                pool.wait_ge(mask_loaded, 16)
                apply_mask()
                with pool.Fori(1, experts) as e:
                    pool.wait_ge(mask_loaded, 16 * e + 16)
                    pool.wait_ge(wide_full, ht * e)
                    apply_mask()
            if norm is not None:
                pool.sem_inc(z_used, 2)
                with pool.Fori(0, experts) as e:
                    pool.wait_ge(rows_loaded, 32 * e + 32)
                    for b in range(NB):
                        z_b = z[b % 2]
                        pool.wait_ge(z_full, e * NB + (b + 1))
                        nc.gpsimd.tensor_tensor(z_b[:], z_b[:], gamma[:], ALU.mult).then_inc(z_used, 1)
                        pool.wait_ge(z_used, e * 2 * NB + (2 * b + 3))
                        nc.gpsimd.tensor_tensor(acc[:, b, :], acc[:, b, :], z_b[:], ALU.add).then_inc(z_used, 1)
                        pool.wait_ge(z_used, e * 2 * NB + (2 * b + 4))
                    pool.sem_inc(added, NB)

        @block.tensor
        def _(pe):
            pe.wait_ge(h_pad, 1)
            with pe.Fori(0, experts) as e:
                pe.wait_ge(w1_loaded, 16 * e + 16)
                if mask_dram is not None:
                    pe.wait_ge(masked, KD * e + KD)
                for f in range(ht):
                    pe.wait_ge(wide_read, ht * e + (f + 1))
                    for c in range(CH):
                        for k in range(KD):
                            last = nc.tensor.matmul(wide[f % 2][:, c, 0:CW], w1[:, k, f * P:(f + 1) * P],
                                                    x_in[:, k, c * CW:(c + 1) * CW], start=(k == 0), stop=(k == KD - 1))
                    last.then_inc(wide_full, 1)
                pe.wait_ge(wide_read, ht * e + (ht + 2))
                pe.wait_ge(w2_loaded, 16 * e + 16)
                for b in range(NB):
                    slot = row[b % 2]
                    pe.wait_ge(row_read, NB * e + max(b + 1, 2))
                    for f in range(ht):
                        last = nc.tensor.matmul(slot[:, 0:D], h[:, f, b * P:(b + 1) * P], w2[:, f, :],
                                                start=(f == 0), stop=(f == ht - 1))
                    last.then_inc(row_full, 1)

        @block.scalar
        def _(act):
            act.sem_inc(wide_read, 2)
            act.wait_ge(b1_loaded, 16)
            with act.Fori(0, experts) as e:
                for f in range(ht):
                    act.wait_ge(wide_full, ht * e + (f + 1))
                    nc.scalar.activation(h[:, f, 0:NT].rearrange("p (c n) -> p c n", c=CH), wide[f % 2][:, :, 0:CW],
                                         ACT.Relu, bias=b1[:, bass.ds(e * ht + f, 1)]).then_inc(wide_read, 1)
                if norm is not None:
                    act.wait_ge(stats_done, e + 1)
                    nc.scalar.activation(std[:], mean_var[:, :, 1], ACT.Sqrt, bias=g.eps[:]).then_inc(std_done, 1)
                    act.wait_ge(scaled, e + 1)
                    for b in range(NB):
                        act.wait_ge(z_used, e * 2 * NB + max(2 * b, 2))
                        nc.scalar.activation(z[b % 2][:], y[:, b, :], ACT.Identity, scale=scale[:, b:b + 1],
                                             bias=shift[:, b:b + 1]).then_inc(z_full, 1)

        @block.vector
        def _(dve):
            dve.sem_inc(row_read, 2)
            with dve.Fori(0, experts) as e:
                if norm is None:
                    for b in range(NB):
                        dve.wait_ge(row_full, NB * e + (b + 1))
                        dve.wait_ge(row_read, NB * e + (b + 1))
                        nc.vector.scalar_tensor_tensor(out=acc[:, b, :], in0=row[b % 2][:, 0:D],
                                                       scalar=weights[:, b, bass.ds(e, 1)], in1=acc[:, b, :],
                                                       op0=ALU.mult, op1=ALU.add).then_inc(row_read, 1)
                else:
                    dve.wait_ge(rows_loaded, 32 * e + 32)
                    for b in range(NB):
                        dve.wait_ge(row_full, NB * e + (b + 1))
                        if b == 0:
                            dve.wait_ge(z_used, e * 2 * NB + 1)
                        nc.vector.tensor_tensor(y[:, b, :], row[b % 2][:, 0:D], b2[:], ALU.add).then_inc(row_read, 1)
                        dve.wait_ge(row_read, NB * e + (b + 3))
                        nc.vector.bn_stats(stats[:, b, :], y[:, b, :]).then_inc(v_step, 1)
                    dve.wait_ge(v_step, e * (2 * NB + 3) + NB)
                    dve.sem_inc(tiles_seen, 1)
                    for b in range(NB):
                        last = nc.vector.bn_aggr(mean_var[:, b, :], stats[:, b, :])
                        last.then_inc(v_step, 1)
                    dve.wait_ge(v_step, e * (2 * NB + 3) + 2 * NB)
                    dve.sem_inc(stats_done, 1)
                    dve.wait_ge(std_done, e + 1)
                    nc.vector.reciprocal(std[:], std[:]).then_inc(v_step, 1)
                    dve.wait_ge(v_step, e * (2 * NB + 3) + (2 * NB + 1))
                    nc.vector.tensor_tensor(scale[:], std[:], weights[:, :, bass.ds(e, 1)].rearrange("p b o -> p (b o)"),
                                            ALU.mult).then_inc(v_step, 1)
                    dve.wait_ge(v_step, e * (2 * NB + 3) + (2 * NB + 2))
                    nc.vector.scalar_tensor_tensor(out=shift[:], in0=mean_var[:, :, 0], scalar=-1.0, in1=scale[:],
                                                   op0=ALU.mult, op1=ALU.mult).then_inc(v_step, 1)
                    dve.wait_ge(v_step, e * (2 * NB + 3) + (2 * NB + 3))
                    dve.sem_inc(scaled, 1)


def two_level_experts(nc, g, a):
    with ExitStack() as ctx:
        s = Pool(nc, ctx, "lv")
        h0 = s.sb("h0", [P, NB, D])
        for level, experts in enumerate((a["L0_ffn_Wr0"].shape[1], a["L0_ffn_Wr1"].shape[1])):
            with ExitStack() as inner:
                t = Pool(nc, inner, f"lv{level}")
                probs, mask = t.sb("probs", [P, NB, experts]), t.sb("mask", [P, NB, experts])
                acc = (h0, g.x)[level]
                stage_route(nc, g, f"lv{level}r", g.xn_t, a[f"L0_ffn_Wr{level}"], experts, "probs", probs, mask)
                stage_spread(nc, g, f"lv{level}s", probs, experts, a[f"L0_ffn_b2_{level}"], acc, level == 1,
                             mask, g.mask_dram)
                stage_experts(nc, g, f"lv{level}e", g.xn_t, a[f"L0_ffn_W1_{level}"], a[f"L0_ffn_b1_{level}"],
                              a[f"L0_ffn_W2_{level}"], probs, acc, g.mask_dram)
            if level == 0:
                stage_norm(nc, g, "lvt", h0, None, g.xn_t)


def normalised_experts(nc, g, a):
    with ExitStack() as ctx:
        s = Pool(nc, ctx, "ne")
        experts = a["L3_ffn_Wg"].shape[1]
        weights, mask = s.sb("weights", [P, NB, experts]), s.sb("mask", [P, NB, experts])
        stage_route(nc, g, "ner", g.xn_t, a["L3_ffn_Wg"], experts, "logits", weights, mask)
        stage_spread(nc, g, "nes", weights, experts, a["L3_ffn_beta"], g.x, True)
        stage_experts(nc, g, "nee", g.xn_t, a["L3_ffn_W1"], a["L3_ffn_b1"], a["L3_ffn_W2"], weights, g.x,
                      norm=(a["L3_ffn_b2"], a["L3_ffn_gamma"]))



def stage_aggregate(nc, g, tag, values, width, finish):
    with ExitStack() as ctx:
        s = Pool(nc, ctx, tag)
        part = [s.sb(f"part{i}", [P, NB, width], BF16) for i in range(3)]
        rest = s.sb("rest", [P, NB, width])
        out = [s.ps(f"out{i}", [P, BANK]) for i in range(4)]
        split, v_step, out_full, out_read = s.sem("split"), s.sem("v_step"), s.sem("out_full"), s.sem("out_read")
        block = ctx.enter_context(nc.Block())

        @block.vector
        def _(dve):
            link = chain(dve, v_step)
            for b0, n in TG:
                v, r = values[:, b0:b0 + n, :], rest[:, b0:b0 + n, :]
                hi, mid, lo = (p[:, b0:b0 + n, :] for p in part)
                link(nc.vector.tensor_copy(hi, v))
                link(nc.vector.tensor_tensor(r, v, hi, ALU.subtract))
                link(nc.vector.tensor_copy(mid, r))
                nc.vector.tensor_tensor(lo, r, mid, ALU.subtract).then_inc(split, 1)
            for b in range(NB):
                dve.wait_ge(out_full, b + 1)
                finish(b, out[b % 4][:, 0:width]).then_inc(out_read, 1)

        @block.tensor
        def _(pe):
            for b in range(NB):
                if b >= 4:
                    pe.wait_ge(out_read, b - 3)
                for t in range(NB):
                    if b == 0:
                        pe.wait_ge(split, t // 4 + 1)
                        pe.wait_ge(v_step, 3 * (t // 4 + 1))
                    for i in range(3):
                        last = nc.tensor.matmul(out[b % 4][:, 0:width], g.adj_t[:, t, b * P:(b + 1) * P],
                                                part[i][:, t, :], start=(t == 0 and i == 0),
                                                stop=(t == NB - 1 and i == 2))
                last.then_inc(out_full, 1)


def aggregate_only(nc, g, a):
    with ExitStack() as ctx:
        s = Pool(nc, ctx, "agg")
        w, hidden = s.sb("w", [P, D]), s.sb("hidden", [P, NB, D])
        with ExitStack() as inner:
            t = Pool(nc, inner, "aggw")
            w_loaded, scaled = t.sem("w_loaded"), t.sem("scaled")
            block = inner.enter_context(nc.Block())

            @block.sync
            def _(sync):
                sync.dma_start(w[:], a["L2_gnn_W"].partition_broadcast(P)).then_inc(w_loaded, 16)

            @block.vector
            def _(dve):
                dve.wait_ge(w_loaded, 16)
                nc.vector.tensor_tensor(hidden[:], g.xn[:], w[:].unsqueeze(1).to_broadcast([P, NB, D]), ALU.mult)\
                    .then_inc(scaled, 1)
                dve.wait_ge(scaled, 1)

        def finish(b, out):
            return nc.vector.tensor_tensor(g.x[:, b, :], out, g.x[:, b, :], ALU.add)

        stage_aggregate(nc, g, "agga", hidden, D, finish)



TINY = 1e-10
ARTANH_TOP = 1.0 - 1e-7
SERIES_BELOW = 0.25


def hyperbolic(nc, g, a):
    with ExitStack() as ctx:
        s = Pool(nc, ctx, "hyp")
        mx = s.sb("mx", [P, NB, D + 2])
        gathered = s.sb("gathered", [P, NB, D + 2])
        prod = s.sb("prod", [P, NB, D])
        stage_project(nc, g, "hypw", g.xn_t, a["L3_gnn_W"], [], (0, prod))
        stage_hyperbolic_values(nc, g, prod, mx)

        def finish(b, out):
            return nc.vector.tensor_copy(gathered[:, b, :], out)

        stage_aggregate(nc, g, "hypa", mx, D + 2, finish)
        stage_hyperbolic_end(nc, g, gathered)


def artanh(link, nc, x, log_plus, log_minus, series, square, out):
    link(nc.vector.tensor_tensor(out, log_plus, log_minus, ALU.subtract))
    link(nc.vector.tensor_scalar(out, out, 0.5, None, ALU.mult))
    link(nc.vector.tensor_tensor(square, x, x, ALU.mult))
    link(nc.vector.tensor_scalar(series, square, 1 / 11, 1 / 9, ALU.mult, ALU.add))
    for c in (1 / 7, 1 / 5, 1 / 3, 1.0):
        link(nc.vector.tensor_tensor(series, series, square, ALU.mult))
        link(nc.vector.tensor_scalar(series, series, c, None, ALU.add))
    link(nc.vector.tensor_tensor(series, series, x, ALU.mult))
    link(nc.vector.tensor_tensor(series, series, out, ALU.subtract))
    link(nc.vector.tensor_scalar(square, x, SERIES_BELOW, None, ALU.is_lt))
    link(nc.vector.tensor_tensor(series, series, square, ALU.mult))
    link(nc.vector.tensor_tensor(out, out, series, ALU.add))


def turns(eng, own, other):
    n = [0, 0]

    def hand(instruction):
        n[0] += 1
        instruction.then_inc(own, 1)

    def take():
        n[1] += 1
        eng.wait_ge(other, n[1])
    return hand, take


def stage_hyperbolic_values(nc, g, prod, values):
    with ExitStack() as ctx:
        s = Pool(nc, ctx, "hypv")
        x_norm, m_norm, clipped, log_plus, log_minus, series, square, at, factor, gamma = (
            s.sb(n, [P, NB]) for n in ("x_norm", "m_norm", "clipped", "log_plus", "log_minus", "series", "square",
                                       "at", "factor", "gamma"))
        squares = s.sb("squares", [P, 3 * NB, D], BF16)
        v_step, v_turn, a_turn, a_step = s.sem("v_step"), s.sem("v_turn"), s.sem("a_turn"), s.sem("a_step")
        block = ctx.enter_context(nc.Block())

        @block.scalar
        def _(act):
            hand, take = turns(act, a_turn, v_turn)
            for b in range(NB):
                nc.scalar.activation(squares[:, b, :], g.xn[:, b, :], ACT.Square, accum_out=x_norm[:, b:b + 1])\
                    .then_inc(a_step, 1)
                nc.scalar.activation(squares[:, NB + b, :], prod[:, b, :], ACT.Square, accum_out=m_norm[:, b:b + 1])\
                    .then_inc(a_step, 1)
            take()
            nc.scalar.activation(m_norm[:], m_norm[:], ACT.Sqrt).then_inc(a_step, 1)
            act.wait_ge(a_step, 2 * NB + 1)
            hand(nc.scalar.activation(x_norm[:], x_norm[:], ACT.Sqrt))
            take()
            nc.scalar.activation(log_plus[:], clipped[:], ACT.Ln, bias=g.one[:]).then_inc(a_step, 1)
            act.wait_ge(a_step, 2 * NB + 2)
            hand(nc.scalar.activation(log_minus[:], clipped[:], ACT.Ln, bias=g.one[:], scale=-1.0))
            take()
            hand(nc.scalar.activation(at[:], at[:], ACT.Tanh))
            take()
            for b in range(NB):
                nc.scalar.activation(squares[:, 2 * NB + b, :], prod[:, b, :], ACT.Square,
                                     accum_out=square[:, b:b + 1]).then_inc(a_step, 1)

        @block.vector
        def _(dve):
            link = chain(dve, v_step)
            hand, take = turns(dve, v_turn, a_turn)
            dve.wait_ge(a_step, 2 * NB)
            link(nc.vector.tensor_scalar(x_norm[:], x_norm[:], TINY * TINY, None, ALU.max))
            hand(nc.vector.tensor_scalar(m_norm[:], m_norm[:], TINY * TINY, None, ALU.max))
            take()
            link(nc.vector.reciprocal(factor[:], x_norm[:]))
            link(nc.vector.tensor_tensor(factor[:], factor[:], m_norm[:], ALU.mult))
            hand(nc.vector.tensor_scalar(clipped[:], x_norm[:], ARTANH_TOP, None, ALU.min))
            take()
            artanh(link, nc, clipped[:], log_plus[:], log_minus[:], series[:], square[:], at[:])
            hand(nc.vector.tensor_tensor(at[:], at[:], factor[:], ALU.mult))
            take()
            link(nc.vector.reciprocal(factor[:], m_norm[:]))
            link(nc.vector.tensor_tensor(factor[:], factor[:], at[:], ALU.mult))
            link(nc.vector.tensor_scalar(series[:], m_norm[:], TINY, None, ALU.is_gt))
            link(nc.vector.tensor_tensor(factor[:], factor[:], series[:], ALU.mult))
            for b in range(NB - 1):
                link(nc.vector.tensor_scalar(prod[:, b, :], prod[:, b, :], factor[:, b:b + 1], None, ALU.mult))
            hand(nc.vector.tensor_scalar(prod[:, NB - 1, :], prod[:, NB - 1, :], factor[:, NB - 1:NB], None, ALU.mult))
            dve.wait_ge(a_step, 3 * NB + 2)
            link(nc.vector.tensor_scalar(gamma[:], square[:], -1.0, 1.0, ALU.mult, ALU.add))
            link(nc.vector.reciprocal(gamma[:], gamma[:]))
            link(nc.vector.tensor_scalar(gamma[:], gamma[:], 2.0, 1e-15, ALU.mult, ALU.max))
            for b in range(NB):
                link(nc.vector.tensor_scalar(values[:, b, 0:D], prod[:, b, :], gamma[:, b:b + 1], None, ALU.mult))
            link(nc.vector.tensor_scalar(values[:, :, D], gamma[:], -1.0, None, ALU.add))
            link(nc.vector.memset(values[:, :, D + 1], 1.0))


def stage_hyperbolic_end(nc, g, gathered):
    with ExitStack() as ctx:
        s = Pool(nc, ctx, "hype")
        inv, sq, root, n, clipped, log_plus, log_minus, series, square, at, factor, scale = (
            s.sb(nm, [P, NB]) for nm in ("inv", "sq", "root", "n", "clipped", "log_plus", "log_minus", "series",
                                         "square", "at", "factor", "scale"))
        squares = s.sb("squares", [P, 2 * NB, D], BF16)
        r = s.sb("r", [P, NB, D])
        v_step, v_turn, a_turn, a_step = s.sem("v_step"), s.sem("v_turn"), s.sem("a_turn"), s.sem("a_step")
        denom, alpha = gathered[:, :, D], gathered[:, :, D + 1]
        block = ctx.enter_context(nc.Block())

        @block.scalar
        def _(act):
            hand, take = turns(act, a_turn, v_turn)
            take()
            for b in range(NB):
                last = nc.scalar.activation(squares[:, b, :], gathered[:, b, 0:D], ACT.Square, scale=inv[:, b:b + 1],
                                            accum_out=sq[:, b:b + 1])
                if b < NB - 1:
                    last.then_inc(a_step, 1)
            hand(last)
            for col in (root, n):
                take()
                hand(nc.scalar.activation(col[:], col[:], ACT.Sqrt))

            def logs():
                take()
                nc.scalar.activation(log_plus[:], clipped[:], ACT.Ln, bias=g.one[:]).then_inc(a_step, 1)
                hand(nc.scalar.activation(log_minus[:], clipped[:], ACT.Ln, bias=g.one[:], scale=-1.0))

            logs()
            take()
            hand(nc.scalar.activation(at[:], at[:], ACT.Tanh))
            take()
            hand(nc.scalar.activation(root[:], root[:], ACT.Sqrt))
            logs()
            take()
            for b in range(NB):
                nc.scalar.activation(r[:, b, :], gathered[:, b, 0:D], ACT.Relu, scale=scale[:, b:b + 1])\
                    .then_inc(a_step, 1)
            act.wait_ge(a_step, NB - 1 + 2 + NB)
            for b in range(NB):
                last = nc.scalar.activation(squares[:, NB + b, :], r[:, b, :], ACT.Square, accum_out=sq[:, b:b + 1])
                if b < NB - 1:
                    last.then_inc(a_step, 1)
            hand(last)
            take()
            nc.scalar.activation(root[:], sq[:], ACT.Sqrt).then_inc(a_step, 1)
            act.wait_ge(a_step, 3 * NB + 1)
            hand(nc.scalar.activation(at[:], root[:], ACT.Tanh))

        @block.vector
        def _(dve):
            link = chain(dve, v_step)
            hand, take = turns(dve, v_turn, a_turn)
            link(nc.vector.tensor_scalar(sq[:], denom, 0.0, None, ALU.is_ge))
            link(nc.vector.tensor_scalar(sq[:], sq[:], 2.0, -1.0, ALU.mult, ALU.add))
            link(nc.vector.tensor_tensor(inv[:], denom, sq[:], ALU.mult))
            link(nc.vector.tensor_scalar(inv[:], inv[:], TINY, None, ALU.max))
            link(nc.vector.tensor_tensor(inv[:], inv[:], sq[:], ALU.mult))
            hand(nc.vector.reciprocal(inv[:], inv[:]))
            take()
            dve.wait_ge(a_step, NB - 1)
            link(nc.vector.tensor_scalar(root[:], sq[:], -1.0, 1.0, ALU.mult, ALU.add))
            hand(nc.vector.tensor_scalar(root[:], root[:], TINY, None, ALU.max))
            take()
            link(nc.vector.tensor_scalar(root[:], root[:], 1.0, None, ALU.add))
            link(nc.vector.reciprocal(factor[:], root[:]))
            link(nc.vector.tensor_tensor(sq[:], sq[:], factor[:], ALU.mult))
            link(nc.vector.tensor_tensor(sq[:], sq[:], factor[:], ALU.mult))
            hand(nc.vector.tensor_scalar(n[:], sq[:], TINY * TINY, None, ALU.max))
            take()
            hand(nc.vector.tensor_scalar(clipped[:], n[:], ARTANH_TOP, None, ALU.min))
            take()
            artanh(link, nc, clipped[:], log_plus[:], log_minus[:], series[:], square[:], at[:])
            hand(nc.vector.tensor_tensor(at[:], at[:], alpha, ALU.mult))
            take()
            link(nc.vector.reciprocal(n[:], n[:]))
            link(nc.vector.tensor_tensor(at[:], at[:], n[:], ALU.mult))
            link(nc.vector.tensor_tensor(factor[:], factor[:], at[:], ALU.mult))
            link(nc.vector.tensor_tensor(root[:], sq[:], at[:], ALU.mult))
            link(nc.vector.tensor_tensor(root[:], root[:], at[:], ALU.mult))
            hand(nc.vector.tensor_scalar(root[:], root[:], TINY * TINY, None, ALU.max))
            take()
            hand(nc.vector.tensor_scalar(clipped[:], root[:], ARTANH_TOP, None, ALU.min))
            take()
            artanh(link, nc, clipped[:], log_plus[:], log_minus[:], series[:], square[:], at[:])
            link(nc.vector.reciprocal(root[:], root[:]))
            link(nc.vector.tensor_tensor(at[:], at[:], root[:], ALU.mult))
            link(nc.vector.tensor_tensor(scale[:], factor[:], at[:], ALU.mult))
            hand(nc.vector.tensor_tensor(scale[:], scale[:], inv[:], ALU.mult))
            take()
            dve.wait_ge(a_step, 3 * NB)
            hand(nc.vector.tensor_scalar(sq[:], sq[:], TINY * TINY, None, ALU.max))
            take()
            link(nc.vector.reciprocal(root[:], root[:]))
            link(nc.vector.tensor_tensor(at[:], at[:], root[:], ALU.mult))
            for b in range(NB):
                link(nc.vector.scalar_tensor_tensor(out=g.x[:, b, :], in0=r[:, b, :], scalar=at[:, b:b + 1],
                                                    in1=g.x[:, b, :], op0=ALU.mult, op1=ALU.add))



HID = 512
HT = HID // P


def stage_gated_hidden(nc, g, tag, src_t, w_drams, h):
    pairs = [(i, j) for i in range(len(w_drams)) for j in range(HT)]
    with ExitStack() as ctx:
        s = Pool(nc, ctx, tag)
        w = [s.sb(f"w{i}", [P, KD, 2 * HID]) for i in range(len(w_drams))]
        gate = [s.sb(f"gate{i}", [P, NT]) for i in range(2)]
        wide = [s.ps(f"wide{i}", [P, CH, BANK]) for i in range(2)]
        w_loaded = [s.sem(f"w_loaded{i}") for i in range(len(w_drams))]
        pad, a_full, b_full, gate_done, h_done = (s.sem("pad"), s.sem("a_full"), s.sem("b_full"), s.sem("gate_done"),
                                                  s.sem("h_done"))
        block = ctx.enter_context(nc.Block())

        @block.sync
        def _(sync):
            for i, dram in enumerate(w_drams):
                sync.dma_start(w[i][:], dram.rearrange("(k p) o -> p k o", p=P)).then_inc(w_loaded[i], 16)

        @block.gpsimd
        def _(pool):
            nc.gpsimd.memset(h[:, :, NT:NP], 0.0).then_inc(pad, 1)
            pool.wait_ge(pad, 1)

        @block.tensor
        def _(pe):
            for t, (i, j) in enumerate(pairs):
                if j == 0:
                    pe.wait_ge(w_loaded[i], 16)
                for half, (full, read) in enumerate(((a_full, gate_done), (b_full, h_done))):
                    if t:
                        pe.wait_ge(read, t)
                    for c in range(CH):
                        for k in range(KD):
                            last = nc.tensor.matmul(wide[half][:, c, 0:CW],
                                                    w[i][:, k, half * HID + j * P:half * HID + (j + 1) * P],
                                                    src_t[:, k, c * CW:(c + 1) * CW], start=(k == 0), stop=(k == KD - 1))
                    last.then_inc(full, 1)

        @block.scalar
        def _(act):
            for t in range(len(pairs)):
                act.wait_ge(a_full, t + 1)
                if t >= 2:
                    act.wait_ge(h_done, t - 1)
                nc.scalar.activation(gate[t % 2][:].rearrange("p (c n) -> p c n", c=CH), wide[0][:, :, 0:CW], ACT.Silu)\
                    .then_inc(gate_done, 1)

        @block.vector
        def _(dve):
            for t in range(len(pairs)):
                dve.wait_ge(b_full, t + 1)
                dve.wait_ge(gate_done, t + 1)
                nc.vector.tensor_tensor(h[:, t, 0:NT].rearrange("p (c n) -> p c n", c=CH), wide[1][:, :, 0:CW],
                                        gate[t % 2][:].rearrange("p (c n) -> p c n", c=CH), ALU.mult).then_inc(h_done, 1)


def stage_routed_out(nc, g, tag, h, shared_dram, expert_dram, weights, experts):
    pairs = experts // 2
    with ExitStack() as ctx:
        s = Pool(nc, ctx, tag)
        ws = s.sb("ws", [P, HT, D])
        we = s.sb("we", [P, HT, experts * D])
        ring = [s.ps(f"ring{i}", [P, BANK]) for i in range(8)]
        ws_loaded, we_loaded, full, read = s.sem("ws_loaded"), s.sem("we_loaded"), s.sem("full"), s.sem("read")
        v_step = s.sem("v_step")
        block = ctx.enter_context(nc.Block())

        @block.sync
        def _(sync):
            sync.dma_start(ws[:], shared_dram.rearrange("(k p) o -> p k o", p=P)).then_inc(ws_loaded, 16)
            sync.dma_start(we[:], expert_dram.rearrange("(k p) o -> p k o", p=P)).then_inc(we_loaded, 16)

        @block.tensor
        def _(pe):
            pe.wait_ge(ws_loaded, 16)
            n = 0
            for b in range(NB):
                for j in range(1 + pairs):
                    if n >= 8:
                        pe.wait_ge(read, n - 7)
                    if n == 1:
                        pe.wait_ge(we_loaded, 16)
                    width = D if j == 0 else 2 * D
                    for f in range(HT):
                        lhs = h[:, f + (HT if j else 0), b * P:(b + 1) * P]
                        rhs = ws[:, f, :] if j == 0 else we[:, f, (j - 1) * 2 * D:j * 2 * D]
                        last = nc.tensor.matmul(ring[n % 8][:, 0:width], lhs, rhs, start=(f == 0), stop=(f == HT - 1))
                    last.then_inc(full, 1)
                    n += 1

        @block.vector
        def _(dve):
            link = chain(dve, v_step)
            n = 0
            for b in range(NB):
                for j in range(1 + pairs):
                    dve.wait_ge(full, n + 1)
                    if j == 0:
                        last = nc.vector.tensor_tensor(g.x[:, b, :], ring[n % 8][:, 0:D], g.x[:, b, :], ALU.add)
                    else:
                        e = 2 * (j - 1)
                        link(nc.vector.scalar_tensor_tensor(out=g.x[:, b, :], in0=ring[n % 8][:, 0:D],
                                                            scalar=weights[:, b, e:e + 1], in1=g.x[:, b, :],
                                                            op0=ALU.mult, op1=ALU.add))
                        last = nc.vector.scalar_tensor_tensor(out=g.x[:, b, :], in0=ring[n % 8][:, D:2 * D],
                                                              scalar=weights[:, b, e + 1:e + 2], in1=g.x[:, b, :],
                                                              op0=ALU.mult, op1=ALU.add)
                    last.then_inc(read, 1)
                    n += 1
                    dve.wait_ge(read, n)


def shared_and_routed(nc, g, a):
    experts = a["L1_ffn_expert_gate_w"].shape[0]
    with ExitStack() as ctx:
        s = Pool(nc, ctx, "sr")
        weights = s.sb("weights", [P, NB, experts])
        counts = s.sb("counts", [P, NB, experts + 1])
        affine = s.sb("affine", [P, 2 * KD])
        with ExitStack() as inner:
            t = Pool(nc, inner, "srl")
            loaded, ones = t.sem("loaded"), t.sem("ones")
            block = inner.enter_context(nc.Block())

            @block.sync
            def _(sync):
                sync.dma_start(affine[:], a["L1_ffn_affine"]).then_inc(loaded, 16)
                sync.wait_ge(loaded, 16)

            @block.gpsimd
            def _(pool):
                nc.gpsimd.memset(counts[:, :, experts], 1.0).then_inc(ones, 1)
                pool.wait_ge(ones, 1)

        stage_norm(nc, g, "srn", g.xn, g.xn, g.xn_t, affine[:, 0:KD], affine[:, KD:2 * KD])
        stage_route(nc, g, "srr", g.xn_t, a["L1_ffn_gates"], experts + 2, "grouped", weights, counts,
                    bias=a["L1_ffn_gate_bias"])
        stage_spread(nc, g, "srs", counts, experts + 1, a["L1_ffn_out_bias"], g.x, True)
        h = s.sb("h", [P, 2 * HT, NP])
        stage_gated_hidden(nc, g, "srh", g.xn_t, [a["L1_ffn_shared_in_w"], a["L1_ffn_expert_in_w"]], h)
        stage_routed_out(nc, g, "sro", h, a["L1_ffn_shared_out_w"], a["L1_ffn_expert_out_weight"], weights, experts)



HEADS = 8
HD = D // HEADS
PAIRS = HEADS // 2
QR = 3 * HD
STEPS = CH * NB
UNITS = 2 * STEPS
RING = 3
PRING = 4
MAX_TILES = 2 * NB
ROWS = ("bv", "bo", "bf2", "g2")
MAX_AT = [9 + k * 20 // MAX_TILES for k in range(MAX_TILES)]
TURN_STEP = STEPS - 3
V_LINKS = CH * PAIRS * 3 + 2 * NB + 1 + 2 * NB + 2


def slab(nc, s, name, width):
    at = -(-nc.sbuf_base // 32) * 32
    s.sb(name, [P, width])
    assert nc.sbuf_base == at + 4 * width, (nc.sbuf_base, at, width)
    return at


def stage_transformer_experts(nc, g, a, weights, acc):
    experts = a["L2_ffn_Wqkv"].shape[0]
    with ExitStack() as ctx:
        s = Pool(nc, ctx, "tx")
        wqkv, wo = s.sb("wqkv", [P, KD, 3 * D]), s.sb("wo", [P, KD, D])
        w1, w2 = s.sb("w1", [P, KD, FF]), s.sb("w2", [P, FT, D])
        rows = s.sb("rows", [P, len(ROWS) + 1, D])
        bv, bo, bf2, g2, be1_row = (rows[:, i, :] for i in range(5))
        g1_row = s.sb("g1_row", [P, D])
        cols = s.sb("cols", [P, experts, 2 * KD + FT + 2 * KD])
        at = slab(nc, s, "slab", FT * NP)
        hi = nc.alloc_sbuf_tensor_at("tx_hi", [P, 2 * KD, NT], F32R, offset=at)
        lo = nc.alloc_sbuf_tensor_at("tx_lo", [P, 2 * KD, NT], F32R, offset=at + 2 * KD * NT * 4)
        h = nc.alloc_sbuf_tensor_at("tx_h", [P, FT, NP], F32, offset=at)
        ops = s.sb("ops", [P, 4, 2, NP], F32R)
        v = s.sb("v", [P, NB, D])
        at2 = slab(nc, s, "slab2", KD * NP)
        plain = nc.alloc_sbuf_tensor_at("tx_plain", [P, 2, NT], F32, offset=at2)
        ctx_t = nc.alloc_sbuf_tensor_at("tx_ctx", [P, KD, NP], F32, offset=at2)
        x1_t = nc.alloc_sbuf_tensor_at("tx_x1t", [P, KD, NP], F32, offset=at2)
        p = s.sb("p", [P, PRING, CW])
        x1 = s.sb("x1", [P, NB, D])
        inv_sum = s.sb("inv_sum", [P, 2, CW])
        neg_max = s.sb("neg_max", [P, 2, NB])
        m_hi, m_lo = s.sb("m_hi", [MAX_TILES, P], F32R), s.sb("m_lo", [MAX_TILES, P], F32R)
        ones = s.sb("ones", [P, HD])
        key_bias = s.sb("key_bias", [P, 1])
        tmp = [s.sb(f"tmp{i}", [P, D]) for i in range(2)]
        z = [s.sb(f"z{i}", [P, D]) for i in range(2)]
        stats, mean_var = s.sb("stats", [P, NB, 6]), s.sb("mean_var", [P, NB, 2])
        std, scale, shift = s.sb("std", [P, NB]), s.sb("scale", [P, NB]), s.sb("shift", [P, NB])

        bank = s.ps("bank", [P, 8, BANK])
        wide = [bank[:, 0:3, :], bank[:, 3:6, :]]
        row = [bank[:, 6, :], bank[:, 7, :]]
        max_ps = bank[:, 3:6, :].rearrange("p c n -> p (c n)")

        wqkv_loaded, w_loaded, cols_loaded = s.sem("wqkv_loaded"), s.sem("w_loaded"), s.sem("cols_loaded")
        ops_loaded = [s.sem("ops_loaded_even"), s.sem("ops_loaded_odd")]
        max_loaded, const_made = s.sem("max_loaded"), s.sem("const_made")
        qk_full, v_full, max_full, turned_max, s_full, pv_done = (
            s.sem(n) for n in ("qk_full", "v_full", "max_full", "turned_max", "s_full", "pv_done"))
        wo_full, x1t_full, f1_full, f2_full = (s.sem(n) for n in ("wo_full", "x1t_full", "f1_full", "f2_full"))
        plain_done, m_hi_done, exp_done, std_done, x1t_done, h_done, gelu_done, z_full = (
            s.sem(n) for n in ("plain_done", "m_hi_done", "exp_done", "std_done", "x1t_done", "h_done", "gelu_done",
                               "z_full"))
        split_done, max_done, m_lo_done, ctx_done, row_read, y_done, stats_done, scaled, v_step, v_seen, f2_added = (
            s.sem(n) for n in ("split_done", "max_done", "m_lo_done", "ctx_done", "row_read", "y_done", "stats_done",
                               "scaled", "v_step", "v_seen", "f2_added"))
        aggr_step = s.sem("aggr_step")
        x1_done, z_used, rows_used = s.sem("x1_done"), s.sem("z_used"), s.sem("rows_used")
        pool_step, key_zero, pads_zero = s.sem("pool_step"), s.sem("key_zero"), s.sem("pads_zero")
        pool_seen, act_seen = s.sem("pool_seen"), s.sem("act_seen")

        block = ctx.enter_context(nc.Block())

        @block.sync
        def _(sync):
            sync.dma_start(cols[:], a["L2_ffn_cols"]).then_inc(cols_loaded, 16)
            with sync.Fori(0, experts) as e:
                def load_pair(pair):
                    sem = ops_loaded[pair % 2]
                    for head in (2 * pair, 2 * pair + 1):
                        lanes = slice(HD * (head % 4), HD * (head % 4) + HD)
                        tile = 2 * (head // 4)
                        for kind, parts in enumerate(((hi, lo, hi), (hi, hi, lo))):
                            for i, part in enumerate(parts):
                                sync.dma_start(ops[HD * i:HD * (i + 1), head % 4, kind, 0:NT].bitcast(F32),
                                               part[lanes, tile + kind, :].bitcast(F32)).then_inc(sem, 16)

                def load_max(pair):
                    sync.wait_ge(m_hi_done, PAIRS * e + (pair + 1))
                    sync.wait_ge(m_lo_done, PAIRS * e + (pair + 1))
                    for i in range(2):
                        head = 2 * pair + i
                        for r, part in enumerate((m_hi, m_lo)):
                            sync.dma_start(ops[QR + r:QR + r + 1, head % 4, 0, :].bitcast(F32),
                                           part[i * NB:(i + 1) * NB, :].bitcast(F32)).then_inc(max_loaded, 16)

                sync.wait_ge(v_full, NB * e + 1)
                sync.dma_start(wqkv[:], a["L2_ffn_Wqkv"][e].rearrange("(k p) o -> p k o", p=P)).then_inc(wqkv_loaded, 16)
                sync.wait_ge(rows_used, e + 1)
                sync.dma_start(rows[:], a["L2_ffn_rows"][e].partition_broadcast(P)).then_inc(w_loaded, 16)
                sync.dma_start(g1_row[:], a["L2_ffn_g1"][e].partition_broadcast(P)).then_inc(w_loaded, 16)
                sync.dma_start(wo[:], a["L2_ffn_Wo"][e].rearrange("(k p) o -> p k o", p=P)).then_inc(w_loaded, 16)
                sync.dma_start(w1[:], a["L2_ffn_W1"][e].rearrange("(k p) o -> p k o", p=P)).then_inc(w_loaded, 16)
                sync.dma_start(w2[:], a["L2_ffn_W2"][e].rearrange("(f p) o -> p f o", p=P)).then_inc(w_loaded, 16)
                sync.wait_ge(const_made, 4)
                sync.wait_ge(split_done, 8 * e + 4)
                load_pair(0)
                load_pair(1)
                load_max(0)
                load_max(1)
                sync.wait_ge(split_done, 8 * e + 8)
                sync.wait_ge(pv_done, PAIRS * STEPS * e + STEPS)
                load_pair(2)
                load_max(2)
                sync.wait_ge(pv_done, PAIRS * STEPS * e + 2 * STEPS)
                load_pair(3)
                load_max(3)

        @block.gpsimd
        def _(pool):
            nc.gpsimd.memset(ones[:], 1.0).then_inc(const_made, 1)
            pool.wait_ge(const_made, 1)
            nc.gpsimd.memset(ops[QR:QR + 2, :, 1, :].bitcast(F32), 1.0).then_inc(const_made, 1)
            pool.wait_ge(const_made, 2)
            nc.gpsimd.memset(ops[0:QR, :, :, NT:NP].bitcast(F32), 0.0).then_inc(const_made, 1)
            pool.wait_ge(const_made, 3)
            nc.gpsimd.memset(key_bias[:], 0.0).then_inc(key_zero, 1)
            pool.wait_ge(key_zero, 1)
            nc.gpsimd.affine_select(out=key_bias[:], in_=key_bias[:], compare_op=ALU.is_gt, fill=-BIG,
                                    base=N - (NB - 1) * P, pattern=[[0, 1]], channel_multiplier=-1)\
                .then_inc(const_made, 1)
            pool.sem_inc(z_used, 2)
            pool.sem_inc(rows_used, 1)
            with pool.Fori(0, experts) as e:
                pool.wait_ge(split_done, 8 * e + 8)
                pool.sem_inc(pool_seen, 1)
                nc.gpsimd.memset(ctx_t[:, :, NT:NP], 0.0).then_inc(pads_zero, 1)
                pool.wait_ge(w_loaded, 80 * e + 80)
                pool.wait_ge(x1t_full, 6 * e + KD)
                pool.sem_inc(pool_seen, 1)
                nc.gpsimd.memset(h[:, :, NT:NP], 0.0).then_inc(pads_zero, 1)
                for b in range(NB):
                    pool.wait_ge(x1t_full, 6 * e + KD * (b // 4 + 1))
                    nc.gpsimd.tensor_tensor(x1[:, b, :], x1[:, b, :], g1_row[:], ALU.mult).then_inc(pool_step, 1)
                    pool.wait_ge(pool_step, NB * e + (b + 1))
                    nc.gpsimd.tensor_tensor(x1[:, b, :], x1[:, b, :], be1_row, ALU.add).then_inc(x1_done, 1)
                for b in range(NB):
                    z_b = z[b % 2]
                    pool.wait_ge(z_full, NB * e + (b + 1))
                    nc.gpsimd.tensor_tensor(z_b[:], z_b[:], g2, ALU.mult).then_inc(z_used, 1)
                    pool.wait_ge(z_used, 2 * NB * e + (2 * b + 3))
                    nc.gpsimd.tensor_tensor(acc[:, b, :], acc[:, b, :], z_b[:], ALU.add).then_inc(z_used, 1)
                    pool.wait_ge(z_used, 2 * NB * e + (2 * b + 4))
                pool.sem_inc(rows_used, 1)

        @block.tensor
        def _(pe):
            pe.sem_inc(v_full, 1)
            pe.wait_ge(const_made, 4)
            with pe.Fori(0, experts) as e:
                def project(tile):
                    if tile >= 2:
                        pe.wait_ge(plain_done, 4 * e + (tile - 1))
                    c0 = (tile % 2) * D + (tile // 2) * P
                    for c in range(CH):
                        for k in range(KD):
                            last = nc.tensor.matmul(wide[tile % 2][:, c, 0:CW], wqkv[:, k, c0:c0 + P],
                                                    g.xn_t[:, k, c * CW:(c + 1) * CW], start=(k == 0), stop=(k == KD - 1))
                    last.then_inc(qk_full, 1)

                def rows_free(section, b):
                    if section < 2:
                        pe.wait_ge(row_read, 2 * NB * e + (1 + section * NB + max(b - 1, 0)))
                    if section == 2 and b < 2:
                        pe.wait_ge(row_read, 2 * NB * e + (1 + 2 * NB))
                    if section == 2 and b >= 2:
                        pe.wait_ge(f2_added, NB * e + b)

                def max_scores(pair, k):
                    head, b = 2 * pair + k // NB, k % NB
                    if pair == 0 and k == 0:
                        pe.wait_ge(plain_done, 4 * e + 4)
                    if k == 0:
                        pe.wait_ge(ops_loaded[pair % 2], 384 * e + 192 * (pair // 2 + 1))
                    if pair and k == 0:
                        pe.wait_ge(m_lo_done, PAIRS * e + pair)
                    if k:
                        pe.wait_ge(max_done, PAIRS * MAX_TILES * e + (MAX_TILES * pair + k))
                    for k0, w in KCH:
                        last = nc.tensor.matmul(max_ps[:, k0:k0 + w], ops[0:QR, head % 4, 0, b * P:(b + 1) * P],
                                                ops[0:QR, head % 4, 1, k0:k0 + w], start=True, stop=True)
                    last.then_inc(max_full, 1)

                def turn_max(pair):
                    pe.wait_ge(max_done, PAIRS * MAX_TILES * e + MAX_TILES * (pair + 1))
                    nc.tensor.transpose(max_ps[0:MAX_TILES, 0:P], neg_max[:].rearrange("p i b -> p (i b)"), g.ident[:])\
                        .then_inc(turned_max, 1)

                def scores(pair, step):
                    c, t = step // NB, step % NB
                    if step == 0:
                        pe.wait_ge(max_loaded, 64 * PAIRS * e + 64 * (pair + 1))
                    for i in range(2):
                        u = UNITS * pair + 2 * step + i
                        if u >= RING:
                            pe.wait_ge(exp_done, PAIRS * UNITS * e + (u - RING + 1))
                        slot = (2 * pair + i) % 4
                        nc.tensor.matmul(bank[:, u % RING, 0:CW], ops[0:QR + 2, slot, 1, t * P:(t + 1) * P],
                                         ops[0:QR + 2, slot, 0, c * CW:(c + 1) * CW], start=True, stop=True)\
                            .then_inc(s_full, 1)

                def mix(pair, step):
                    c, t = step // NB, step % NB
                    chunk = CH * pair + c
                    out = row[chunk % 2]
                    u = UNITS * pair + 2 * step
                    if t == 0 and chunk >= 2:
                        pe.wait_ge(ctx_done, CH * PAIRS * e + (chunk - 1))
                    if t == 0 and chunk == 0:
                        pe.wait_ge(row_read, 2 * NB * e + (1 + NB))
                    pe.wait_ge(exp_done, PAIRS * UNITS * e + (u + 2))
                    for i in range(2):
                        head = 2 * pair + i
                        for j, lhs in enumerate((v[:, t, head * HD:(head + 1) * HD], ones[:])):
                            lane = 2 * HD * i + HD * j
                            last = nc.tensor.matmul(out[lane:lane + HD, 0:CW], lhs, p[:, (u + i) % PRING, :],
                                                    start=(t == 0), stop=(t == NB - 1), tile_position=(0, lane))
                    last.then_inc(pv_done, 1)

                pe.wait_ge(wqkv_loaded, 16 * e + 16)
                for tile in range(4):
                    project(tile)
                pe.wait_ge(f2_added, NB * e + 1)
                for b in range(NB):
                    rows_free(0, b)
                    for k in range(KD):
                        last = nc.tensor.matmul(row[b % 2][:, 0:D], g.xn_t[:, k, b * P:(b + 1) * P],
                                                wqkv[:, k, 2 * D:3 * D], start=(k == 0), stop=(k == KD - 1))
                    last.then_inc(v_full, 1)
                for k in range(MAX_TILES):
                    max_scores(0, k)
                turn_max(0)
                scores(0, 0)
                for pair in range(PAIRS):
                    for step in range(STEPS):
                        if step + 1 < STEPS:
                            scores(pair, step + 1)
                        elif pair + 1 < PAIRS:
                            scores(pair + 1, 0)
                        mix(pair, step)
                        if pair + 1 < PAIRS:
                            for k in range(MAX_TILES):
                                if MAX_AT[k] == step:
                                    max_scores(pair + 1, k)
                            if step == TURN_STEP:
                                turn_max(pair + 1)

                pe.wait_ge(w_loaded, 80 * e + 80)
                pe.wait_ge(ctx_done, CH * PAIRS * e + CH * PAIRS)
                pe.wait_ge(pads_zero, 2 * e + 1)
                for b in range(NB):
                    rows_free(1, b)
                    for k in range(KD):
                        last = nc.tensor.matmul(row[b % 2][:, 0:D], ctx_t[:, k, b * P:(b + 1) * P], wo[:, k, :],
                                                start=(k == 0), stop=(k == KD - 1))
                    last.then_inc(wo_full, 1)
                n = 0
                for b0, nb in TG:
                    for k in range(KD):
                        for b in range(b0, b0 + nb):
                            pe.wait_ge(y_done, NB * e + (b + 1))
                            last = nc.tensor.transpose(bank[:, n, (b - b0) * P:(b - b0 + 1) * P],
                                                       x1[:, b, k * P:(k + 1) * P], g.ident[:])
                        last.then_inc(x1t_full, 1)
                        n += 1
                pe.wait_ge(x1t_done, 6 * e + 6)
                for f in range(FT):
                    if f >= 2:
                        pe.wait_ge(h_done, FT * e + (f - 1))
                    for c in range(CH):
                        for k in range(KD):
                            last = nc.tensor.matmul(wide[f % 2][:, c, 0:CW], w1[:, k, f * P:(f + 1) * P],
                                                    x1_t[:, k, c * CW:(c + 1) * CW], start=(k == 0), stop=(k == KD - 1))
                    last.then_inc(f1_full, 1)
                pe.wait_ge(h_done, FT * e + FT)
                pe.wait_ge(pads_zero, 2 * e + 2)
                for b in range(NB):
                    rows_free(2, b)
                    for f in range(FT):
                        last = nc.tensor.matmul(row[b % 2][:, 0:D], h[:, f, b * P:(b + 1) * P], w2[:, f, :],
                                                start=(f == 0), stop=(f == FT - 1))
                    last.then_inc(f2_full, 1)

        @block.scalar
        def _(act):
            act.wait_ge(cols_loaded, 16)
            act.wait_ge(const_made, 4)
            with act.Fori(0, experts) as e:
                def exponent(pair, step, i):
                    u = UNITS * pair + 2 * step + i
                    act.wait_ge(s_full, PAIRS * UNITS * e + (u + 1))
                    if u >= PRING:
                        act.wait_ge(pv_done, PAIRS * STEPS * e + (u // 2 - 1))
                    last_tile = step % NB == NB - 1
                    bias = dict(bias=key_bias[:]) if last_tile else {}
                    nc.scalar.activation(p[:, u % PRING, :], bank[:, u % RING, 0:CW], ACT.Exp, **bias).then_inc(exp_done, 1)

                def high_max(pair):
                    act.wait_ge(turned_max, PAIRS * e + (pair + 1))
                    if pair:
                        act.wait_ge(max_loaded, 64 * PAIRS * e + 64 * pair)
                    nc.scalar.activation(m_hi[:], max_ps[0:MAX_TILES, 0:P], ACT.Copy).then_inc(m_hi_done, 1)

                for tile in range(4):
                    act.wait_ge(qk_full, 4 * e + (tile + 1))
                    if tile >= 2:
                        act.wait_ge(split_done, 8 * e + 2 * (tile - 1))
                    act.sem_inc(act_seen, 1)
                    nc.scalar.activation(plain[:, tile % 2, :].rearrange("p (c n) -> p c n", c=CH),
                                         wide[tile % 2][:, :, 0:CW], ACT.Identity,
                                         bias=cols[:, bass.ds(e, 1), (tile % 2) * KD + tile // 2]).then_inc(plain_done, 1)
                high_max(0)
                for pair in range(PAIRS):
                    for step in range(STEPS):
                        for i in range(2):
                            exponent(pair, step, i)
                        if step == TURN_STEP and pair + 1 < PAIRS:
                            high_max(pair + 1)
                act.wait_ge(stats_done, 2 * e + 1)
                nc.scalar.activation(std[:], mean_var[:, :, 1], ACT.Sqrt, bias=g.eps[:]).then_inc(std_done, 1)
                n = 0
                for b0, nb in TG:
                    for k in range(KD):
                        act.wait_ge(x1t_full, 6 * e + (n + 1))
                        act.sem_inc(act_seen, 1)
                        c = 2 * KD + FT + k
                        nc.scalar.activation(x1_t[:, k, b0 * P:(b0 + nb) * P], bank[:, n, 0:nb * P], ACT.Identity,
                                             scale=cols[:, bass.ds(e, 1), c], bias=cols[:, bass.ds(e, 1), c + KD])\
                            .then_inc(x1t_done, 1)
                        n += 1
                for f in range(FT):
                    act.wait_ge(f1_full, FT * e + (f + 1))
                    act.sem_inc(act_seen, 1)
                    nc.scalar.activation(h[:, f, 0:NT].rearrange("p (c n) -> p c n", c=CH), wide[f % 2][:, :, 0:CW],
                                         ACT.Gelu, bias=cols[:, bass.ds(e, 1), 2 * KD + f]).then_inc(h_done, 1)
                for b in range(NB):
                    act.wait_ge(f2_added, NB * e + (b + 2))
                    nc.scalar.activation(tmp[b % 2][:], tmp[b % 2][:], ACT.Gelu).then_inc(gelu_done, 1)
                act.wait_ge(stats_done, 2 * e + 2)
                nc.scalar.activation(std[:], mean_var[:, :, 1], ACT.Sqrt, bias=g.eps[:]).then_inc(std_done, 1)
                act.wait_ge(scaled, e + 1)
                for b in range(NB):
                    act.wait_ge(z_used, 2 * NB * e + max(2 * b, 2))
                    nc.scalar.activation(z[b % 2][:], x1[:, b, :], ACT.Identity, scale=scale[:, b:b + 1],
                                         bias=shift[:, b:b + 1]).then_inc(z_full, 1)

        @block.vector
        def _(dve):
            dve.sem_inc(row_read, 1)
            dve.sem_inc(f2_added, 1)
            with dve.Fori(0, experts) as e:
                n = [0]

                def link(instruction):
                    n[0] += 1
                    instruction.then_inc(v_step, 1)
                    dve.wait_ge(v_step, V_LINKS * e + n[0])

                def settle():
                    dve.sem_inc(v_seen, 1)

                def row_max(pair, k):
                    dve.wait_ge(max_full, PAIRS * MAX_TILES * e + (MAX_TILES * pair + k + 1))
                    nc.vector.tensor_reduce(neg_max[:, k // NB, k % NB:k % NB + 1], max_ps[:, 0:N], AX_X, ALU.max,
                                            negate=True).then_inc(max_done, 1)

                def low_max(pair):
                    dve.wait_ge(m_hi_done, PAIRS * e + (pair + 1))
                    nc.vector.tensor_tensor(m_lo[:], max_ps[0:MAX_TILES, 0:P], m_hi[:], ALU.subtract)\
                        .then_inc(m_lo_done, 1)

                def normalise(pair, c):
                    chunk = CH * pair + c
                    out = row[chunk % 2]
                    dve.wait_ge(pv_done, PAIRS * STEPS * e + NB * (chunk + 1))
                    for i in range(2):
                        head = 2 * pair + i
                        base = 2 * HD * i
                        link(nc.vector.reciprocal(inv_sum[base:base + HD, i, :], out[base + HD:base + 2 * HD, 0:CW]))
                        into = ctx_t[HD * (head % 4):HD * (head % 4) + HD, head // 4, c * CW:(c + 1) * CW]
                        last = nc.vector.tensor_tensor(into, out[base:base + HD, 0:CW], inv_sum[base:base + HD, i, :],
                                                       ALU.mult)
                        if i == 0:
                            link(last)
                    last.then_inc(ctx_done, 1)

                for tile in range(4):
                    dve.wait_ge(plain_done, 4 * e + (tile + 1))
                    factor = HD ** -0.5 if tile % 2 == 0 else 1.0
                    src = plain[:, tile % 2, :]
                    nc.vector.tensor_scalar(hi[:, tile, :], src, factor, None, ALU.mult).then_inc(split_done, 1)
                    dve.wait_ge(split_done, 8 * e + (2 * tile + 1))
                    nc.vector.scalar_tensor_tensor(out=lo[:, tile, :], in0=src, scalar=factor, in1=hi[:, tile, :],
                                                   op0=ALU.mult, op1=ALU.subtract).then_inc(split_done, 1)
                dve.wait_ge(w_loaded, 80 * e + 80)
                for b in range(NB):
                    dve.wait_ge(v_full, NB * e + (b + 2))
                    nc.vector.tensor_tensor(v[:, b, :], row[b % 2][:, 0:D], bv, ALU.add).then_inc(row_read, 1)
                for k in range(MAX_TILES):
                    row_max(0, k)
                low_max(0)
                for pair in range(PAIRS):
                    for step in range(STEPS):
                        if pair + 1 < PAIRS:
                            for k in range(MAX_TILES):
                                if MAX_AT[k] == step:
                                    row_max(pair + 1, k)
                        if step % NB == NB - 1:
                            normalise(pair, step // NB)
                        if step == TURN_STEP and pair + 1 < PAIRS:
                            low_max(pair + 1)

                for b in range(NB):
                    dve.wait_ge(wo_full, NB * e + (b + 1))
                    if b == 0:
                        dve.wait_ge(z_used, 2 * NB * e + 1)
                    nc.vector.tensor_tensor(x1[:, b, :], row[b % 2][:, 0:D], bo, ALU.add).then_inc(row_read, 1)
                    dve.wait_ge(row_read, 2 * NB * e + (1 + NB + b + 1))
                    link(nc.vector.tensor_tensor(x1[:, b, :], x1[:, b, :], g.xn[:, b, :], ALU.add))
                    link(nc.vector.bn_stats(stats[:, b, :], x1[:, b, :]))
                settle()
                for b in range(NB - 1):
                    nc.vector.bn_aggr(mean_var[:, b, :], stats[:, b, :]).then_inc(aggr_step, 1)
                nc.vector.bn_aggr(mean_var[:, NB - 1, :], stats[:, NB - 1, :]).then_inc(stats_done, 1)
                dve.wait_ge(std_done, 2 * e + 1)
                link(nc.vector.reciprocal(std[:], std[:]))
                for b in range(NB):
                    nc.vector.tensor_scalar(x1[:, b, :], x1[:, b, :], mean_var[:, b, 0:1], std[:, b:b + 1],
                                            ALU.subtract, ALU.mult).then_inc(y_done, 1)

                def add_bias(b):
                    dve.wait_ge(f2_full, NB * e + (b + 1))
                    nc.vector.tensor_tensor(tmp[b % 2][:], row[b % 2][:, 0:D], bf2, ALU.add).then_inc(f2_added, 1)

                add_bias(0)
                for b in range(NB):
                    if b + 1 < NB:
                        add_bias(b + 1)
                    dve.wait_ge(gelu_done, NB * e + (b + 1))
                    dve.wait_ge(x1_done, NB * e + (b + 1))
                    link(nc.vector.tensor_tensor(x1[:, b, :], tmp[b % 2][:], x1[:, b, :], ALU.add))
                    link(nc.vector.bn_stats(stats[:, b, :], x1[:, b, :]))
                settle()
                for b in range(NB - 1):
                    nc.vector.bn_aggr(mean_var[:, b, :], stats[:, b, :]).then_inc(aggr_step, 1)
                nc.vector.bn_aggr(mean_var[:, NB - 1, :], stats[:, NB - 1, :]).then_inc(stats_done, 1)
                dve.wait_ge(std_done, 2 * e + 2)
                link(nc.vector.reciprocal(std[:], std[:]))
                link(nc.vector.tensor_tensor(scale[:], std[:], weights[:, :, bass.ds(e, 1)].rearrange("p b o -> p (b o)"),
                                             ALU.mult))
                nc.vector.scalar_tensor_tensor(out=shift[:], in0=mean_var[:, :, 0], scalar=-1.0, in1=scale[:],
                                               op0=ALU.mult, op1=ALU.mult).then_inc(scaled, 1)
                assert n[0] == V_LINKS, n[0]


def transformer_experts(nc, g, a):
    with ExitStack() as ctx:
        s = Pool(nc, ctx, "te")
        experts = a["L2_ffn_Wqkv"].shape[0]
        weights, mask = s.sb("weights", [P, NB, experts]), s.sb("mask", [P, NB, experts])
        stage_route(nc, g, "ter", g.xn_t, a["L2_ffn_expert_queries"], experts, "keys", weights, mask,
                    keys=(a["L2_ffn_gate_Wk"], a["L2_ffn_gate_bk"]))
        stage_spread(nc, g, "tes", weights, experts, a["L2_ffn_be2"], g.x, True)
        stage_transformer_experts(nc, g, a, weights, g.x)



class Global:
    pass


def stage_clear(nc):
    used = sorted(nc.released_uncleared_semaphores)
    block_ctx = ExitStack()
    with block_ctx:
        block = block_ctx.enter_context(nc.Block())

        @block.gpsimd
        def _(pool):
            pool.sem_clear(range(used[0], used[-1] + 1))


def stage_store(nc, g, out):
    with ExitStack() as ctx:
        s = Pool(nc, ctx, "store")
        stored = s.sem("stored")
        block = ctx.enter_context(nc.Block())

        @block.sync
        def _(sync):
            full = N // P
            sync.dma_start(out[0:full * P, :].rearrange("(b p) d -> p b d", p=P), g.x[:, 0:full, :]).then_inc(stored, 16)
            sync.dma_start(out[full * P:N, :], g.x[0:N - full * P, full, :]).then_inc(stored, 16)
            sync.wait_ge(stored, 32)


def program(nc, a, out, start=0, stop=8):
    with ExitStack() as ctx:
        s = Pool(nc, ctx, "g")
        g = Global()
        g.adj_loaded, g.adj_loads = s.sem("adj_loaded"), 0
        g.x = s.sb("x", [P, NB, D])
        g.xn = s.sb("xn", [P, NB, D])
        g.xn_t = s.sb("xn_t", [P, KD, NP])
        g.ident = s.sb("ident", [P, P])
        g.eps = s.sb("eps", [P, 1])
        g.one = s.sb("one", [P, 1])
        g.ramp = s.sb("ramp", [P, NB, 8])
        g.mask_dram = nc.dram_tensor("expert_masks", [8, NT], F32, kind="Internal").ap()
        stage_load(nc, g, a["x"])
        blocks = [lambda: gat_layers(nc, g, a["L0_gnn_W_stack"]),
                  lambda: two_level_experts(nc, g, a),
                  lambda: masked_attention(nc, g, a["L1_gnn_W"], a["L1_gnn_U"], a["adj"]),
                  lambda: shared_and_routed(nc, g, a),
                  lambda: aggregate_only(nc, g, a),
                  lambda: transformer_experts(nc, g, a),
                  lambda: hyperbolic(nc, g, a),
                  lambda: normalised_experts(nc, g, a)]
        for i in range(start, stop):
            stage_clear(nc)
            stage_norm(nc, g, f"ln{i}", g.x, g.xn, g.xn_t)
            if i % 2 == 0:
                with ExitStack() as inner:
                    g.adj_t = Pool(nc, inner, f"g{i}").sb("adj_t", [P, NB, NP], BF16)
                    stage_adjacency(nc, g, f"adj{i}", a["adj_t"])
                    blocks[i]()
            else:
                blocks[i]()
        stage_store(nc, g, out)


def columns(b):
    return np.ascontiguousarray(b.reshape(-1, P).T)


def lay_out(inputs):
    a = {name: np.ascontiguousarray(np.asarray(v)) for name, v in inputs.items()}
    x, adj = a.pop("x"), a.pop("adj")
    a["x"] = np.zeros((NP, D), x.dtype)
    a["x"][:N] = x
    a["adj"] = np.zeros((NP, N), adj.dtype)
    a["adj"][:N] = adj
    a["adj_t"] = np.zeros((NP, NP), adj.dtype)
    a["adj_t"][:N, :N] = adj.T
    a["L0_ffn_b1_0"], a["L0_ffn_b1_1"], a["L3_ffn_b1"] = (columns(a[k]) for k in ("L0_ffn_b1_0", "L0_ffn_b1_1", "L3_ffn_b1"))
    a["L1_ffn_gates"] = np.concatenate([a["L1_ffn_expert_gate_w"], a.pop("L1_ffn_group_gate_w")]).T.copy()
    a["L1_ffn_gate_bias"] = np.concatenate([a.pop("L1_ffn_expert_bias"), a.pop("L1_ffn_group_bias")])
    a["L1_ffn_out_bias"] = np.concatenate([a.pop("L1_ffn_expert_out_bias"), a.pop("L1_ffn_shared_out_b")[None]])
    a["L1_ffn_affine"] = np.concatenate([columns(a.pop("L1_ffn_ln_scale")), columns(a.pop("L1_ffn_ln_bias"))], 1)
    for k in ("L1_ffn_shared_in_w", "L1_ffn_expert_in_w", "L1_ffn_shared_out_w"):
        a[k] = a[k].T.copy()
    a["L1_ffn_expert_out_weight"] = a["L1_ffn_expert_out_weight"].transpose(2, 0, 1).reshape(HID, -1).copy()
    for k in ("L2_ffn_Wqkv", "L2_ffn_Wo", "L2_ffn_W1", "L2_ffn_W2"):
        a[k] = a[k].transpose(0, 2, 1).copy()
    a["L2_ffn_gate_Wk"] = a["L2_ffn_gate_Wk"].T.copy()
    a["L2_ffn_expert_queries"] = a["L2_ffn_expert_queries"].T.copy()
    a["L2_ffn_gate_bk"] = columns(a["L2_ffn_gate_bk"])
    bqkv, g1, be1 = a.pop("L2_ffn_bqkv"), a["L2_ffn_g1"], a.pop("L2_ffn_be1")
    per_feature = np.concatenate([bqkv[:, :2 * D], a.pop("L2_ffn_bf1"), g1, be1], 1)
    a["L2_ffn_cols"] = columns(per_feature).reshape(P, len(g1), -1)
    a["L2_ffn_rows"] = np.stack([bqkv[:, 2 * D:], a.pop("L2_ffn_bo"), a.pop("L2_ffn_bf2"), a.pop("L2_ffn_g2"), be1], 1)
    return a



def kernel(**inputs):
    import concourse.bacc as bacc
    from concourse.bass_utils import run_bass_kernel_spmd

    nc = bacc.Bacc("TRN2", target_bir_lowering=False, num_devices=1)
    arrays, args = {}, {}
    for name, array in lay_out(inputs).items():
        arrays[f"in_{name}"] = array
        args[name] = nc.dram_tensor(f"in_{name}", array.shape, mybir.dt.from_np(array.dtype), kind="ExternalInput").ap()
    out = nc.dram_tensor("out_x", (N, D), F32, kind="ExternalOutput").ap()
    program(nc, args, out)
    result = run_bass_kernel_spmd(nc, [arrays], core_ids=[0])
    return result.results[0]["out_x"]
```

```python
from contextlib import ExitStack

import numpy as np

import concourse.bass as bass
from concourse import mybir

F32 = mybir.dt.float32
F32R = mybir.dt.float32r
BF16 = mybir.dt.bfloat16
ALU = mybir.AluOpType
ACT = mybir.ActivationFunctionType
AX_X = mybir.AxisListType.X

P = 128
N = 1354
D = 256
KD = D // P
NB = -(-N // P)
NP = NB * P
CH = 3
CW = -(-N // CH)
NT = CH * CW
TG = [(0, 4), (4, 4), (8, 3)]
KCH = [(0, 512), (512, 512), (1024, N - 1024)]
BANK = 512
LN_EPS = 1e-5
BIG = 1e30
FF = 1024
FT = FF // P
LOG2_HALF_ULP = 1.1920929e-07


class Pool:

    def __init__(self, nc, ctx, tag):
        self.nc, self.ctx, self.tag = nc, ctx, tag

    def sb(self, name, shape, dt=F32):
        return self.ctx.enter_context(self.nc.sbuf_tensor(f"{self.tag}_{name}", shape, dt))

    def ps(self, name, shape, dt=F32):
        return self.ctx.enter_context(self.nc.psum_tensor(f"{self.tag}_{name}", shape, dt))

    def sem(self, name):
        return self.ctx.enter_context(self.nc.semaphore(f"{self.tag}_{name}"))


def chain(eng, sem, count=0):
    n = [count]

    def link(instruction):
        n[0] += 1
        instruction.then_inc(sem, 1)
        eng.wait_ge(sem, n[0])
    return link


def over(col, width):
    return col.unsqueeze(2).to_broadcast([P, NB, width])



def stage_load(nc, g, x):
    with ExitStack() as ctx:
        s = Pool(nc, ctx, "load")
        x_loaded, zeroed, made = s.sem("x_loaded"), s.sem("zeroed"), s.sem("made")
        block = ctx.enter_context(nc.Block())

        @block.sync
        def _(sync):
            sync.dma_start(g.x[:], x.rearrange("(b p) d -> p b d", p=P)).then_inc(x_loaded, 16)
            sync.wait_ge(x_loaded, 16)

        @block.gpsimd
        def _(pool):
            nc.gpsimd.memset(g.ident[:], 0.0).then_inc(zeroed, 1)
            pool.wait_ge(zeroed, 1)
            nc.gpsimd.affine_select(out=g.ident[:], in_=g.ident[:], compare_op=ALU.not_equal, fill=1.0, base=0,
                                    pattern=[[-1, P]], channel_multiplier=1).then_inc(made, 1)
            nc.gpsimd.memset(g.eps[:], LN_EPS).then_inc(made, 1)
            nc.gpsimd.memset(g.one[:], 1.0).then_inc(made, 1)
            for e in range(8):
                nc.gpsimd.memset(g.ramp[:, :, e], float(8 - e)).then_inc(made, 1)
            pool.wait_ge(made, 11)


def stage_adjacency(nc, g, tag, adj_t):
    g.adj_loads += 1
    with ExitStack() as ctx:
        block = ctx.enter_context(nc.Block())

        @block.gpsimd
        def _(pool):
            pool.dma_start(g.adj_t[:], adj_t.rearrange("(b p) q -> p b q", p=P)).then_inc(g.adj_loaded, 16)
            pool.wait_ge(g.adj_loaded, 16 * g.adj_loads)



def stage_norm(nc, g, tag, src, dst, dst_t, gain=None, shift=None):
    with ExitStack() as ctx:
        s = Pool(nc, ctx, tag)
        stats = s.sb("stats", [P, NB, 6])
        mean_var = s.sb("mean_var", [P, NB, 2])
        std = s.sb("std", [P, NB])
        rstd = s.sb("rstd", [P, NB])
        turned = [s.ps(f"turned{i}", [P, BANK]) for i in range(4)]
        v_step, std_done, normed = s.sem("v_step"), s.sem("std_done"), s.sem("normed")
        turned_full, turned_read = s.sem("turned_full"), s.sem("turned_read")
        normalise = dst is not None
        out = dst if normalise else src
        block = ctx.enter_context(nc.Block())

        if normalise:
            @block.vector
            def _(dve):
                for b in range(NB):
                    nc.vector.bn_stats(stats[:, b, :], src[:, b, :]).then_inc(v_step, 1)
                dve.wait_ge(v_step, NB)
                for b in range(NB):
                    nc.vector.bn_aggr(mean_var[:, b, :], stats[:, b, :]).then_inc(v_step, 1)
                dve.wait_ge(std_done, 1)
                nc.vector.reciprocal(rstd[:], std[:]).then_inc(v_step, 1)
                dve.wait_ge(v_step, 2 * NB + 1)
                for b in range(NB):
                    nc.vector.tensor_scalar(dst[:, b, :], src[:, b, :], mean_var[:, b, 0:1], rstd[:, b:b + 1],
                                            ALU.subtract, ALU.mult).then_inc(normed, 1)

        @block.tensor
        def _(pe):
            t = 0
            for b0, nb in TG:
                for k in range(KD):
                    if t >= 4:
                        pe.wait_ge(turned_read, t - 3)
                    for b in range(b0, b0 + nb):
                        if normalise:
                            pe.wait_ge(normed, b + 1)
                        last = nc.tensor.transpose(turned[t % 4][:, (b - b0) * P:(b - b0 + 1) * P],
                                                   out[:, b, k * P:(k + 1) * P], g.ident[:])
                    last.then_inc(turned_full, 1)
                    t += 1

        @block.scalar
        def _(act):
            if normalise:
                act.wait_ge(v_step, 2 * NB)
                nc.scalar.activation(std[:], mean_var[:, :, 1], ACT.Sqrt, bias=g.eps[:]).then_inc(std_done, 1)
            t = 0
            for b0, nb in TG:
                for k in range(KD):
                    act.wait_ge(turned_full, t + 1)
                    into = dst_t[:, k, b0 * P:(b0 + nb) * P]
                    if gain is None:
                        nc.scalar.activation(into, turned[t % 4][:, 0:nb * P], ACT.Copy).then_inc(turned_read, 1)
                    else:
                        nc.scalar.activation(into, turned[t % 4][:, 0:nb * P], ACT.Identity, scale=gain[:, k:k + 1],
                                             bias=shift[:, k:k + 1]).then_inc(turned_read, 1)
                    t += 1



def stage_project(nc, g, tag, src_t, w_dram, feature_major, token_major):
    cols = w_dram.shape[1]
    tiles = [(c0 + j * P, target, j) for c0, target in feature_major for j in range(KD)]
    with ExitStack() as ctx:
        s = Pool(nc, ctx, tag)
        w = s.sb("w", [P, KD, cols])
        wide = [s.ps(f"wide{i}", [P, CH, BANK]) for i in range(2)]
        row = [s.ps(f"row{i}", [P, BANK]) for i in range(2)]
        w_loaded, pads_zero = s.sem("w_loaded"), s.sem("pads_zero")
        wide_full, row_full = s.sem("wide_full"), s.sem("row_full")
        wide_read_act, wide_read_dve = s.sem("wide_read_act"), s.sem("wide_read_dve")
        row_read_act, row_read_dve = s.sem("row_read_act"), s.sem("row_read_dve")
        block = ctx.enter_context(nc.Block())

        @block.sync
        def _(sync):
            sync.dma_start(w[:], w_dram.rearrange("(k p) o -> p k o", p=P)).then_inc(w_loaded, 16)

        @block.gpsimd
        def _(pool):
            for _, target in feature_major:
                nc.gpsimd.memset(target[:, :, NT:NP], 0.0).then_inc(pads_zero, 1)
            pool.wait_ge(pads_zero, len(feature_major))

        @block.tensor
        def _(pe):
            pe.wait_ge(w_loaded, 16)
            for t, (c0, _, _) in enumerate(tiles):
                if t >= 2:
                    pe.wait_ge([wide_read_act, wide_read_dve][t % 2], t // 2)
                for c in range(CH):
                    for k in range(KD):
                        last = nc.tensor.matmul(wide[t % 2][:, c, 0:CW], w[:, k, c0:c0 + P],
                                                src_t[:, k, c * CW:(c + 1) * CW], start=(k == 0), stop=(k == KD - 1))
                last.then_inc(wide_full, 1)
            if token_major:
                c0 = token_major[0]
                for b in range(NB):
                    if b >= 2:
                        pe.wait_ge([row_read_act, row_read_dve][b % 2], b // 2)
                    for k in range(KD):
                        last = nc.tensor.matmul(row[b % 2][:, 0:D], src_t[:, k, b * P:(b + 1) * P],
                                                w[:, k, c0:c0 + D], start=(k == 0), stop=(k == KD - 1))
                    last.then_inc(row_full, 1)

        def drain(eng, copy, parity, wide_read, row_read):
            for t, (_, target, j) in enumerate(tiles):
                if t % 2 == parity:
                    eng.wait_ge(wide_full, t + 1)
                    copy(target[:, j, 0:NT].rearrange("p (c n) -> p c n", c=CH), wide[t % 2][:, :, 0:CW])\
                        .then_inc(wide_read, 1)
            if token_major:
                for b in range(parity, NB, 2):
                    eng.wait_ge(row_full, b + 1)
                    copy(token_major[1][:, b, :], row[b % 2][:, 0:D]).then_inc(row_read, 1)

        @block.scalar
        def _(act):
            drain(act, lambda o, i: nc.scalar.activation(o, i, ACT.Copy), 0, wide_read_act, row_read_act)

        @block.vector
        def _(dve):
            drain(dve, nc.vector.tensor_copy, 1, wide_read_dve, row_read_dve)



def stage_graph_attention(nc, g, tag, q_t, k_t, v, finish, masked_rows=None):
    with ExitStack() as ctx:
        s = Pool(nc, ctx, tag)
        e = [s.sb(f"e{i}", [P, NP]) for i in range(2)]
        e_t = s.sb("e_t", [P, NB, P])
        neg_max = s.sb("neg_max", [P, NB])
        row_sum = s.sb("row_sum", [P, NB])
        inv = s.sb("inv", [P, NB])
        scratch = s.sb("scratch", [P, D])
        scores = [s.ps(f"scores{i}", [P, CH * BANK]) for i in range(2)]
        turned = s.ps("turned", [P, BANK])
        out = s.ps("out", [P, BANK])
        scores_full, turned_full, out_full = s.sem("scores_full"), s.sem("turned_full"), s.sem("out_full")
        max_done, exp_done, e_pad = s.sem("max_done"), s.sem("exp_done"), s.sem("e_pad")
        e_t_done, finished, v_step = s.sem("e_t_done"), s.sem("finished"), s.sem("v_step")
        if masked_rows is not None:
            rows = [s.sb(f"rows{i}", [P, N]) for i in range(2)]
            kept = [s.sb(f"kept{i}", [P, N]) for i in range(2)]
            rows_loaded, bias_done = [s.sem(f"rows_loaded{i}") for i in range(2)], s.sem("bias_done")
            pool_step, self_added = s.sem("pool_step"), s.sem("self_added")
        block = ctx.enter_context(nc.Block())

        if masked_rows is not None:
            @block.sync
            def _(sync):
                for b in range(NB):
                    if b >= 2:
                        sync.wait_ge(max_done, b - 1)
                    sync.dma_start(rows[b % 2][:], masked_rows[b * P:(b + 1) * P, 0:N]).then_inc(rows_loaded[b % 2], 16)

        @block.gpsimd
        def _(pool):
            for i in range(2):
                nc.gpsimd.memset(e[i][:, N:NP], 0.0).then_inc(e_pad, 1)
            if masked_rows is not None:
                link = chain(pool, pool_step)
                for b in range(NB):
                    own = g.adj_t[:, b, b * P:(b + 1) * P]
                    nc.gpsimd.tensor_tensor(own, own, g.ident[:], ALU.add).then_inc(self_added, 1)
                for b in range(NB):
                    pool.wait_ge(rows_loaded[b % 2], 16 * (b // 2 + 1))
                    r = rows[b % 2]
                    nc_last = nc.gpsimd.tensor_scalar(r[:], r[:], -1.0, BIG, ALU.add, ALU.mult)
                    link(nc_last)
                    w = min(P, N - b * P)
                    own = r[:, b * P:b * P + w]
                    nc.gpsimd.affine_select(out=own, in_=own, compare_op=ALU.not_equal, fill=0.0, base=0,
                                            pattern=[[-1, w]], channel_multiplier=1).then_inc(bias_done, 1)
                pool.wait_ge(e_t_done, CH * NB)
                for b in range(NB):
                    own = g.adj_t[:, b, b * P:(b + 1) * P]
                    nc.gpsimd.tensor_tensor(own, own, g.ident[:], ALU.subtract).then_inc(self_added, 1)
                pool.wait_ge(self_added, 2 * NB)
            pool.wait_ge(e_pad, 2)

        @block.tensor
        def _(pe):
            def score(b, c):
                if c == 0 and b >= 2:
                    pe.wait_ge(max_done if masked_rows is not None else exp_done, b - 1)
                k0, w = KCH[c]
                for k in range(KD):
                    last = nc.tensor.matmul(scores[b % 2][:, k0:k0 + w], q_t[:, k, b * P:(b + 1) * P],
                                            k_t[:, k, k0:k0 + w], start=(k == 0), stop=(k == KD - 1))
                if c == CH - 1:
                    last.then_inc(scores_full, 1)

            def turn(b, c):
                if c == 0:
                    pe.wait_ge(exp_done, b + 1)
                    pe.wait_ge(e_pad, 2)
                if b + c:
                    pe.wait_ge(e_t_done, CH * b + c)
                t0, n = TG[c]
                for t in range(t0, t0 + n):
                    last = nc.tensor.transpose(turned[:, (t - t0) * P:(t - t0 + 1) * P],
                                               e[b % 2][:, t * P:(t + 1) * P], g.ident[:])
                last.then_inc(turned_full, 1)

            def mix(b):
                pe.wait_ge(e_t_done, CH * (b + 1))
                if b:
                    pe.wait_ge(finished, b)
                for t in range(NB):
                    last = nc.tensor.matmul(out[:, 0:D], e_t[:, t, :], v[:, t, :], start=(t == 0), stop=(t == NB - 1))
                last.then_inc(out_full, 1)

            for c in range(CH):
                score(0, c)
            for b in range(NB):
                for c in range(CH):
                    turn(b, c)
                    if b + 1 < NB:
                        score(b + 1, c)
                mix(b)

        @block.scalar
        def _(act):
            for b in range(NB):
                act.wait_ge(max_done, b + 1)
                if b >= 2:
                    act.wait_ge(turned_full, CH * (b - 1))
                seen = scores[b % 2][:, 0:N] if masked_rows is None else kept[b % 2][:]
                nc.scalar.activation(e[b % 2][:, 0:N], seen, ACT.Exp, bias=neg_max[:, b:b + 1],
                                     accum_out=row_sum[:, b:b + 1]).then_inc(exp_done, 1)

        @block.vector
        def _(dve):
            link = chain(dve, v_step)

            def row_max(b):
                dve.wait_ge(scores_full, b + 1)
                if masked_rows is None:
                    nc.vector.tensor_reduce(neg_max[:, b:b + 1], scores[b % 2][:, 0:N], AX_X, ALU.max, negate=True)\
                        .then_inc(max_done, 1)
                    return
                dve.wait_ge(bias_done, b + 1)
                if b >= 2:
                    dve.wait_ge(exp_done, b - 1)
                link(nc.vector.tensor_tensor(kept[b % 2][:], scores[b % 2][:, 0:N], rows[b % 2][:], ALU.add))
                nc.vector.tensor_reduce(neg_max[:, b:b + 1], kept[b % 2][:], AX_X, ALU.max, negate=True)\
                    .then_inc(max_done, 1)

            row_max(0)
            if masked_rows is not None:
                dve.wait_ge(self_added, NB)
            for b in range(NB):
                for c, (t0, n) in enumerate(TG):
                    dve.wait_ge(turned_full, CH * b + c + 1)
                    if b:
                        dve.wait_ge(out_full, b)
                    nc.vector.tensor_tensor(e_t[:, t0:t0 + n, :],
                                            turned[:, 0:n * P].rearrange("p (t q) -> p t q", q=P),
                                            g.adj_t[:, t0:t0 + n, b * P:(b + 1) * P], ALU.mult).then_inc(e_t_done, 1)
                if b + 1 < NB:
                    row_max(b + 1)
                link(nc.vector.reciprocal(inv[:, b:b + 1], row_sum[:, b:b + 1]))
                dve.wait_ge(out_full, b + 1)
                finish(link, b, out[:, 0:D], inv[:, b:b + 1], scratch).then_inc(finished, 1)
            dve.wait_ge(finished, NB)


def gat_layers(nc, g, w_stack):
    layers = w_stack.shape[0]
    for layer in range(layers):
        with ExitStack() as ctx:
            s = Pool(nc, ctx, f"gat{layer}")
            wh_t, ws_t, wh = s.sb("wh_t", [P, KD, NP]), s.sb("ws_t", [P, KD, NP]), s.sb("wh", [P, NB, D])
            stage_project(nc, g, f"gat{layer}p", g.xn_t, w_stack[layer], [(0, wh_t), (D, ws_t)], (0, wh))
            last_layer = layer == layers - 1

            def finish(link, b, out, inv, scratch):
                link(nc.vector.scalar_tensor_tensor(out=scratch[:], in0=out, scalar=inv, in1=g.xn[:, b, :],
                                                    op0=ALU.mult, op1=ALU.add))
                leaky = nc.vector.scalar_tensor_tensor(out=g.xn[:, b, :], in0=scratch[:], scalar=0.01, in1=scratch[:],
                                                       op0=ALU.mult, op1=ALU.max)
                if not last_layer:
                    return leaky
                link(leaky)
                return nc.vector.tensor_tensor(g.x[:, b, :], g.x[:, b, :], g.xn[:, b, :], ALU.add)

            stage_graph_attention(nc, g, f"gat{layer}a", wh_t, ws_t, wh, finish)
        if not last_layer:
            stage_norm(nc, g, f"gat{layer}t", g.xn, None, g.xn_t)


def masked_attention(nc, g, w, u, adj):
    with ExitStack() as ctx:
        s = Pool(nc, ctx, "nbr")
        h_t, hu_t, h = s.sb("h_t", [P, KD, NP]), s.sb("hu_t", [P, KD, NP]), s.sb("h", [P, NB, D])
        stage_project(nc, g, "nbrh", g.xn_t, w, [(0, h_t)], (0, h))
        stage_project(nc, g, "nbru", h_t, u, [(0, hu_t)], None)

        def finish(link, b, out, inv, scratch):
            return nc.vector.scalar_tensor_tensor(out=g.x[:, b, :], in0=out, scalar=inv, in1=g.x[:, b, :],
                                                  op0=ALU.mult, op1=ALU.add)

        stage_graph_attention(nc, g, "nbra", hu_t, h_t, h, finish, masked_rows=adj)



def top_two(link, nc, g, values, mask, work, work2, col, width, below):
    ramp = g.ramp[:, :, 0:width]
    left = values
    for turn in range(2):
        link(nc.vector.tensor_reduce(col, left, AX_X, ALU.max))
        link(nc.vector.tensor_tensor(work, left, over(col, width), ALU.is_equal))
        link(nc.vector.tensor_tensor(work, work, ramp, ALU.mult))
        link(nc.vector.tensor_reduce(col, work, AX_X, ALU.max))
        link(nc.vector.tensor_tensor(work, work, over(col, width), ALU.is_equal))
        if turn == 0:
            link(nc.vector.tensor_copy(mask, work))
            link(nc.vector.tensor_scalar(work2, work, -below, None, ALU.mult))
            link(nc.vector.tensor_tensor(work2, work2, values, ALU.add))
            left = work2
        else:
            link(nc.vector.tensor_tensor(mask, mask, work, ALU.add))


def softmax_to(link, nc, dve, values, probs, col, width, exp_asked, exp_done, n):
    link(nc.vector.tensor_reduce(col, values, AX_X, ALU.max))
    nc.vector.tensor_tensor(probs, values, over(col, width), ALU.subtract).then_inc(exp_asked, 1)
    dve.wait_ge(exp_done, n)


def divide_by_sum(link, nc, values, col, width, eps=None):
    link(nc.vector.tensor_reduce(col, values, AX_X, ALU.add))
    if eps is not None:
        link(nc.vector.tensor_scalar(col, col, eps, None, ALU.add))
    link(nc.vector.reciprocal(col, col))
    link(nc.vector.tensor_tensor(values, values, over(col, width), ALU.mult))


def stage_route(nc, g, tag, src_t, gate, width, rule, weights, mask, bias=None, keys=None):
    with ExitStack() as ctx:
        s = Pool(nc, ctx, tag)
        w = s.sb("w", [P, KD, width])
        logits = s.sb("logits", [P, NB, width])
        work = [s.sb(f"work{i}", [P, NB, 8]) for i in range(4)]
        cols = [s.sb(f"col{i}", [P, NB]) for i in range(3)]
        ps = s.ps("ps", [P, NB, width])
        w_loaded, full, v_step = s.sem("w_loaded"), s.sem("full"), s.sem("v_step")
        exp_asked, exp_done = s.sem("exp_asked"), s.sem("exp_done")
        if bias is not None:
            bias_all = s.sb("bias_all", [P, width])
        if keys is not None:
            wk = s.sb("wk", [P, KD, D])
            bk = s.sb("bk", [P, KD])
            keys_t = s.sb("keys_t", [P, KD, NP])
            wide = [s.ps(f"wide{i}", [P, CH, BANK]) for i in range(2)]
            keys_full, keys_done, pads = s.sem("keys_full"), s.sem("keys_done"), s.sem("pads")
        weights_view = weights[:] if rule != "grouped" else work[3][:, :, 0:4]
        loads = 1 + (bias is not None) + 2 * (keys is not None)
        block = ctx.enter_context(nc.Block())

        @block.sync
        def _(sync):
            sync.dma_start(w[:], gate.rearrange("(k p) e -> p k e", p=P)).then_inc(w_loaded, 16)
            if bias is not None:
                sync.dma_start(bias_all[:], bias.partition_broadcast(P)).then_inc(w_loaded, 16)
            if keys is not None:
                sync.dma_start(wk[:], keys[0].rearrange("(k p) o -> p k o", p=P)).then_inc(w_loaded, 16)
                sync.dma_start(bk[:], keys[1]).then_inc(w_loaded, 16)

        if keys is not None:
            @block.gpsimd
            def _(pool):
                nc.gpsimd.memset(keys_t[:, :, NT:NP], 0.0).then_inc(pads, 1)

        @block.tensor
        def _(pe):
            pe.wait_ge(w_loaded, 16 * loads)
            seen = src_t
            if keys is not None:
                for j in range(KD):
                    for c in range(CH):
                        for k in range(KD):
                            last = nc.tensor.matmul(wide[j][:, c, 0:CW], wk[:, k, j * P:(j + 1) * P],
                                                    src_t[:, k, c * CW:(c + 1) * CW], start=(k == 0), stop=(k == KD - 1))
                    last.then_inc(keys_full, 1)
                pe.wait_ge(keys_done, KD)
                pe.wait_ge(pads, 1)
                seen = keys_t
            for b in range(NB):
                for k in range(KD):
                    last = nc.tensor.matmul(ps[:, b, :], seen[:, k, b * P:(b + 1) * P], w[:, k, :],
                                            start=(k == 0), stop=(k == KD - 1))
            last.then_inc(full, 1)

        @block.scalar
        def _(act):
            if keys is not None:
                act.wait_ge(w_loaded, 16 * loads)
                for j in range(KD):
                    act.wait_ge(keys_full, j + 1)
                    nc.scalar.activation(keys_t[:, j, 0:NT].rearrange("p (c n) -> p c n", c=CH), wide[j][:, :, 0:CW],
                                         ACT.Identity, bias=bk[:, j:j + 1]).then_inc(keys_done, 1)
            act.wait_ge(exp_asked, 1)
            nc.scalar.activation(weights_view, weights_view, ACT.Exp).then_inc(exp_done, 1)

        @block.vector
        def _(dve):
            link = chain(dve, v_step)
            dve.wait_ge(full, 1)
            c0, c1, c2 = (c[:] for c in cols)
            if rule == "grouped":
                dve.wait_ge(w_loaded, 16 * loads)
                link(nc.vector.tensor_tensor(logits[:], ps[:], bias_all[:].unsqueeze(1).to_broadcast([P, NB, width]),
                                             ALU.add))
                first, second = c1, c2
                link(nc.vector.tensor_tensor(first, logits[:, :, 8], logits[:, :, 9], ALU.is_ge))
                link(nc.vector.tensor_scalar(second, first, -1.0, 1.0, ALU.mult, ALU.add))
                chosen, other, exps = work[0][:, :, 0:4], work[1][:, :, 0:4], work[3][:, :, 0:4]
                link(nc.vector.tensor_tensor(chosen, logits[:, :, 0:4], over(first, 4), ALU.mult))
                link(nc.vector.tensor_tensor(other, logits[:, :, 4:8], over(second, 4), ALU.mult))
                link(nc.vector.tensor_tensor(chosen, chosen, other, ALU.add))
                softmax_to(link, nc, dve, chosen, exps, c0, 4, exp_asked, exp_done, 1)
                divide_by_sum(link, nc, exps, c0, 4)
                picked = work[2][:, :, 4:8]
                top_two(link, nc, g, exps, picked, work[0][:, :, 0:4], work[1][:, :, 0:4], c0, 4, 2.0)
                link(nc.vector.tensor_tensor(exps, exps, picked, ALU.mult))
                divide_by_sum(link, nc, exps, c0, 4, 1e-8)
                for i, group in enumerate((first, second)):
                    link(nc.vector.tensor_tensor(weights[:, :, 4 * i:4 * i + 4], exps, over(group, 4), ALU.mult))
                    link(nc.vector.tensor_tensor(mask[:, :, 4 * i:4 * i + 4], picked, over(group, 4), ALU.mult))
                return
            scale = D ** -0.5 if rule == "keys" else 1.0
            link(nc.vector.tensor_scalar(logits[:], ps[:], scale, None, ALU.mult))
            a, b2 = work[0][:, :, 0:width], work[1][:, :, 0:width]
            softmax_to(link, nc, dve, logits[:], weights[:], c0, width, exp_asked, exp_done, 1)
            if rule == "logits":
                top_two(link, nc, g, logits[:], mask[:], a, b2, c0, width, BIG)
                link(nc.vector.tensor_tensor(weights[:], weights[:], mask[:], ALU.mult))
                divide_by_sum(link, nc, weights[:], c0, width)
                return
            divide_by_sum(link, nc, weights[:], c0, width)
            top_two(link, nc, g, weights[:], mask[:], a, b2, c0, width, 2.0)
            if rule == "keys":
                link(nc.vector.tensor_tensor(weights[:], weights[:], mask[:], ALU.mult))
                divide_by_sum(link, nc, weights[:], c0, width, 1e-9)


def stage_spread(nc, g, tag, coefficients, width, table_dram, acc, add, mask=None, mask_dram=None):
    with ExitStack() as ctx:
        s = Pool(nc, ctx, tag)
        table = s.sb("table", [width, D])
        turned_sb = s.sb("turned_sb", [width, NP])
        mask_sb = s.sb("mask_sb", [width, NP])
        turned = s.ps("turned", [width, CH, BANK])
        mask_ps = s.ps("mask_ps", [width, CH, BANK])
        row = [s.ps(f"row{i}", [P, BANK]) for i in range(2)]
        loaded, turned_full, turned_read = s.sem("loaded"), s.sem("turned_full"), s.sem("turned_read")
        row_full, row_read, stored = s.sem("row_full"), s.sem("row_read"), s.sem("stored")
        block = ctx.enter_context(nc.Block())

        @block.sync
        def _(sync):
            sync.dma_start(table[:], table_dram).then_inc(loaded, 16)
            if mask is not None:
                sync.wait_ge(turned_read, 2 * CH)
                sync.dma_start(mask_dram[0:width, :], mask_sb[:, 0:NT]).then_inc(stored, 16)
                sync.wait_ge(stored, 16)

        @block.tensor
        def _(pe):
            for src, into in ((coefficients, turned), (mask, mask_ps)):
                if src is None:
                    continue
                for c, (b0, n) in enumerate(TG):
                    for b in range(b0, b0 + n):
                        last = nc.tensor.transpose(into[:, c, (b - b0) * P:(b - b0 + 1) * P], src[:, b, :], g.ident[:])
                    last.then_inc(turned_full, 1)
            pe.wait_ge(turned_read, CH)
            pe.wait_ge(loaded, 16)
            for b in range(NB):
                if b >= 2:
                    pe.wait_ge(row_read, b - 1)
                nc.tensor.matmul(row[b % 2][:, 0:D], turned_sb[:, b * P:(b + 1) * P], table[:], start=True, stop=True)\
                    .then_inc(row_full, 1)

        @block.scalar
        def _(act):
            n_read = 0
            for src, into, sb in ((coefficients, turned, turned_sb), (mask, mask_ps, mask_sb)):
                if src is None:
                    continue
                for c, (b0, n) in enumerate(TG):
                    n_read += 1
                    act.wait_ge(turned_full, n_read)
                    nc.scalar.activation(sb[:, b0 * P:(b0 + n) * P], into[:, c, 0:n * P], ACT.Copy).then_inc(turned_read, 1)

        @block.vector
        def _(dve):
            for b in range(NB):
                dve.wait_ge(row_full, b + 1)
                if add:
                    nc.vector.tensor_tensor(acc[:, b, :], row[b % 2][:, 0:D], acc[:, b, :], ALU.add).then_inc(row_read, 1)
                else:
                    nc.vector.tensor_copy(acc[:, b, :], row[b % 2][:, 0:D]).then_inc(row_read, 1)



def stage_experts(nc, g, tag, src_t, w1_dram, b1_dram, w2_dram, weights, acc, mask_dram=None, norm=None):
    experts, _, hidden = w1_dram.shape
    ht = hidden // P
    with ExitStack() as ctx:
        s = Pool(nc, ctx, tag)
        w1, w2 = s.sb("w1", [P, KD, hidden]), s.sb("w2", [P, ht, D])
        b1 = s.sb("b1", [P, experts * ht])
        h = s.sb("h", [P, ht, NP])
        wide = [s.ps(f"wide{i}", [P, CH, BANK]) for i in range(2)]
        row = [s.ps(f"row{i}", [P, BANK]) for i in range(2)]
        w1_loaded, w2_loaded, b1_loaded = s.sem("w1_loaded"), s.sem("w2_loaded"), s.sem("b1_loaded")
        h_pad, wide_full, wide_read = s.sem("h_pad"), s.sem("wide_full"), s.sem("wide_read")
        row_full, row_read = s.sem("row_full"), s.sem("row_read")
        if mask_dram is not None:
            mask = s.sb("mask", [P, NT])
            xm = s.sb("xm", [P, KD, NT])
            mask_loaded, masked = s.sem("mask_loaded"), s.sem("masked")
        if norm is not None:
            b2, gamma = s.sb("b2", [P, D]), s.sb("gamma", [P, D])
            y = s.sb("y", [P, NB, D])
            z = [s.sb(f"z{i}", [P, D]) for i in range(2)]
            stats, mean_var = s.sb("stats", [P, NB, 6]), s.sb("mean_var", [P, NB, 2])
            std, scale, shift = s.sb("std", [P, NB]), s.sb("scale", [P, NB]), s.sb("shift", [P, NB])
            rows_loaded, std_done, scaled, z_full, z_used = (
                s.sem("rows_loaded"), s.sem("std_done"), s.sem("scaled"), s.sem("z_full"), s.sem("z_used"))
            tiles_seen = s.sem("tiles_seen")
            stats_done, v_step, added = s.sem("stats_done"), s.sem("v_step"), s.sem("added")
        x_in = src_t if mask_dram is None else xm
        w1_v = w1_dram.rearrange("e (k p) o -> e p k o", p=P)
        w2_v = w2_dram.rearrange("e (f p) o -> e p f o", p=P)
        block = ctx.enter_context(nc.Block())

        @block.sync
        def _(sync):
            def load_mask(e):
                if mask_dram is not None:
                    sync.dma_start(mask[:], mask_dram[e].partition_broadcast(P)).then_inc(mask_loaded, 16)

            def load_rows(e):
                if norm is not None:
                    sync.dma_start(b2[:], norm[0][e].partition_broadcast(P)).then_inc(rows_loaded, 16)
                    sync.dma_start(gamma[:], norm[1][e].partition_broadcast(P)).then_inc(rows_loaded, 16)

            load_mask(0)
            sync.dma_start(w1[:], w1_v[0]).then_inc(w1_loaded, 16)
            sync.dma_start(b1[:], b1_dram).then_inc(b1_loaded, 16)
            sync.dma_start(w2[:], w2_v[0]).then_inc(w2_loaded, 16)
            load_rows(0)
            with sync.Fori(1, experts) as e:
                if mask_dram is not None:
                    sync.wait_ge(masked, KD * e)
                    load_mask(e)
                sync.wait_ge(wide_full, ht * e)
                sync.dma_start(w1[:], w1_v[e]).then_inc(w1_loaded, 16)
                sync.wait_ge(row_full, NB * e)
                sync.dma_start(w2[:], w2_v[e]).then_inc(w2_loaded, 16)
                if norm is not None:
                    sync.wait_ge(added, NB * e)
                    load_rows(e)

        @block.gpsimd
        def _(pool):
            nc.gpsimd.memset(h[:, :, NT:NP], 0.0).then_inc(h_pad, 1)
            if mask_dram is not None:
                def apply_mask():
                    for k in range(KD):
                        nc.gpsimd.tensor_tensor(xm[:, k, :], src_t[:, k, 0:NT], mask[:], ALU.mult).then_inc(masked, 1)

                pool.wait_ge(mask_loaded, 16)
                apply_mask()
                with pool.Fori(1, experts) as e:
                    pool.wait_ge(mask_loaded, 16 * e + 16)
                    pool.wait_ge(wide_full, ht * e)
                    apply_mask()
            if norm is not None:
                pool.sem_inc(z_used, 2)
                with pool.Fori(0, experts) as e:
                    pool.wait_ge(rows_loaded, 32 * e + 32)
                    for b in range(NB):
                        z_b = z[b % 2]
                        pool.wait_ge(z_full, e * NB + (b + 1))
                        nc.gpsimd.tensor_tensor(z_b[:], z_b[:], gamma[:], ALU.mult).then_inc(z_used, 1)
                        pool.wait_ge(z_used, e * 2 * NB + (2 * b + 3))
                        nc.gpsimd.tensor_tensor(acc[:, b, :], acc[:, b, :], z_b[:], ALU.add).then_inc(z_used, 1)
                        pool.wait_ge(z_used, e * 2 * NB + (2 * b + 4))
                    pool.sem_inc(added, NB)

        @block.tensor
        def _(pe):
            pe.wait_ge(h_pad, 1)
            with pe.Fori(0, experts) as e:
                pe.wait_ge(w1_loaded, 16 * e + 16)
                if mask_dram is not None:
                    pe.wait_ge(masked, KD * e + KD)
                for f in range(ht):
                    pe.wait_ge(wide_read, ht * e + (f + 1))
                    for c in range(CH):
                        for k in range(KD):
                            last = nc.tensor.matmul(wide[f % 2][:, c, 0:CW], w1[:, k, f * P:(f + 1) * P],
                                                    x_in[:, k, c * CW:(c + 1) * CW], start=(k == 0), stop=(k == KD - 1))
                    last.then_inc(wide_full, 1)
                pe.wait_ge(wide_read, ht * e + (ht + 2))
                pe.wait_ge(w2_loaded, 16 * e + 16)
                for b in range(NB):
                    slot = row[b % 2]
                    pe.wait_ge(row_read, NB * e + max(b + 1, 2))
                    for f in range(ht):
                        last = nc.tensor.matmul(slot[:, 0:D], h[:, f, b * P:(b + 1) * P], w2[:, f, :],
                                                start=(f == 0), stop=(f == ht - 1))
                    last.then_inc(row_full, 1)

        @block.scalar
        def _(act):
            act.sem_inc(wide_read, 2)
            act.wait_ge(b1_loaded, 16)
            with act.Fori(0, experts) as e:
                for f in range(ht):
                    act.wait_ge(wide_full, ht * e + (f + 1))
                    nc.scalar.activation(h[:, f, 0:NT].rearrange("p (c n) -> p c n", c=CH), wide[f % 2][:, :, 0:CW],
                                         ACT.Relu, bias=b1[:, bass.ds(e * ht + f, 1)]).then_inc(wide_read, 1)
                if norm is not None:
                    act.wait_ge(stats_done, e + 1)
                    nc.scalar.activation(std[:], mean_var[:, :, 1], ACT.Sqrt, bias=g.eps[:]).then_inc(std_done, 1)
                    act.wait_ge(scaled, e + 1)
                    for b in range(NB):
                        act.wait_ge(z_used, e * 2 * NB + max(2 * b, 2))
                        nc.scalar.activation(z[b % 2][:], y[:, b, :], ACT.Identity, scale=scale[:, b:b + 1],
                                             bias=shift[:, b:b + 1]).then_inc(z_full, 1)

        @block.vector
        def _(dve):
            dve.sem_inc(row_read, 2)
            with dve.Fori(0, experts) as e:
                if norm is None:
                    for b in range(NB):
                        dve.wait_ge(row_full, NB * e + (b + 1))
                        dve.wait_ge(row_read, NB * e + (b + 1))
                        nc.vector.scalar_tensor_tensor(out=acc[:, b, :], in0=row[b % 2][:, 0:D],
                                                       scalar=weights[:, b, bass.ds(e, 1)], in1=acc[:, b, :],
                                                       op0=ALU.mult, op1=ALU.add).then_inc(row_read, 1)
                else:
                    dve.wait_ge(rows_loaded, 32 * e + 32)
                    for b in range(NB):
                        dve.wait_ge(row_full, NB * e + (b + 1))
                        if b == 0:
                            dve.wait_ge(z_used, e * 2 * NB + 1)
                        nc.vector.tensor_tensor(y[:, b, :], row[b % 2][:, 0:D], b2[:], ALU.add).then_inc(row_read, 1)
                        dve.wait_ge(row_read, NB * e + (b + 3))
                        nc.vector.bn_stats(stats[:, b, :], y[:, b, :]).then_inc(v_step, 1)
                    dve.wait_ge(v_step, e * (2 * NB + 3) + NB)
                    dve.sem_inc(tiles_seen, 1)
                    for b in range(NB):
                        last = nc.vector.bn_aggr(mean_var[:, b, :], stats[:, b, :])
                        last.then_inc(v_step, 1)
                    dve.wait_ge(v_step, e * (2 * NB + 3) + 2 * NB)
                    dve.sem_inc(stats_done, 1)
                    dve.wait_ge(std_done, e + 1)
                    nc.vector.reciprocal(std[:], std[:]).then_inc(v_step, 1)
                    dve.wait_ge(v_step, e * (2 * NB + 3) + (2 * NB + 1))
                    nc.vector.tensor_tensor(scale[:], std[:], weights[:, :, bass.ds(e, 1)].rearrange("p b o -> p (b o)"),
                                            ALU.mult).then_inc(v_step, 1)
                    dve.wait_ge(v_step, e * (2 * NB + 3) + (2 * NB + 2))
                    nc.vector.scalar_tensor_tensor(out=shift[:], in0=mean_var[:, :, 0], scalar=-1.0, in1=scale[:],
                                                   op0=ALU.mult, op1=ALU.mult).then_inc(v_step, 1)
                    dve.wait_ge(v_step, e * (2 * NB + 3) + (2 * NB + 3))
                    dve.sem_inc(scaled, 1)


def two_level_experts(nc, g, a):
    with ExitStack() as ctx:
        s = Pool(nc, ctx, "lv")
        h0 = s.sb("h0", [P, NB, D])
        for level, experts in enumerate((a["L0_ffn_Wr0"].shape[1], a["L0_ffn_Wr1"].shape[1])):
            with ExitStack() as inner:
                t = Pool(nc, inner, f"lv{level}")
                probs, mask = t.sb("probs", [P, NB, experts]), t.sb("mask", [P, NB, experts])
                acc = (h0, g.x)[level]
                stage_route(nc, g, f"lv{level}r", g.xn_t, a[f"L0_ffn_Wr{level}"], experts, "probs", probs, mask)
                stage_spread(nc, g, f"lv{level}s", probs, experts, a[f"L0_ffn_b2_{level}"], acc, level == 1,
                             mask, g.mask_dram)
                stage_experts(nc, g, f"lv{level}e", g.xn_t, a[f"L0_ffn_W1_{level}"], a[f"L0_ffn_b1_{level}"],
                              a[f"L0_ffn_W2_{level}"], probs, acc, g.mask_dram)
            if level == 0:
                stage_norm(nc, g, "lvt", h0, None, g.xn_t)


def normalised_experts(nc, g, a):
    with ExitStack() as ctx:
        s = Pool(nc, ctx, "ne")
        experts = a["L3_ffn_Wg"].shape[1]
        weights, mask = s.sb("weights", [P, NB, experts]), s.sb("mask", [P, NB, experts])
        stage_route(nc, g, "ner", g.xn_t, a["L3_ffn_Wg"], experts, "logits", weights, mask)
        stage_spread(nc, g, "nes", weights, experts, a["L3_ffn_beta"], g.x, True)
        stage_experts(nc, g, "nee", g.xn_t, a["L3_ffn_W1"], a["L3_ffn_b1"], a["L3_ffn_W2"], weights, g.x,
                      norm=(a["L3_ffn_b2"], a["L3_ffn_gamma"]))



def stage_aggregate(nc, g, tag, values, width, finish):
    with ExitStack() as ctx:
        s = Pool(nc, ctx, tag)
        part = [s.sb(f"part{i}", [P, NB, width], BF16) for i in range(3)]
        rest = s.sb("rest", [P, NB, width])
        out = [s.ps(f"out{i}", [P, BANK]) for i in range(4)]
        split, v_step, out_full, out_read = s.sem("split"), s.sem("v_step"), s.sem("out_full"), s.sem("out_read")
        block = ctx.enter_context(nc.Block())

        @block.vector
        def _(dve):
            link = chain(dve, v_step)
            for b0, n in TG:
                v, r = values[:, b0:b0 + n, :], rest[:, b0:b0 + n, :]
                hi, mid, lo = (p[:, b0:b0 + n, :] for p in part)
                link(nc.vector.tensor_copy(hi, v))
                link(nc.vector.tensor_tensor(r, v, hi, ALU.subtract))
                link(nc.vector.tensor_copy(mid, r))
                nc.vector.tensor_tensor(lo, r, mid, ALU.subtract).then_inc(split, 1)
            for b in range(NB):
                dve.wait_ge(out_full, b + 1)
                finish(b, out[b % 4][:, 0:width]).then_inc(out_read, 1)

        @block.tensor
        def _(pe):
            for b in range(NB):
                if b >= 4:
                    pe.wait_ge(out_read, b - 3)
                for t in range(NB):
                    if b == 0:
                        pe.wait_ge(split, t // 4 + 1)
                        pe.wait_ge(v_step, 3 * (t // 4 + 1))
                    for i in range(3):
                        last = nc.tensor.matmul(out[b % 4][:, 0:width], g.adj_t[:, t, b * P:(b + 1) * P],
                                                part[i][:, t, :], start=(t == 0 and i == 0),
                                                stop=(t == NB - 1 and i == 2))
                last.then_inc(out_full, 1)


def aggregate_only(nc, g, a):
    with ExitStack() as ctx:
        s = Pool(nc, ctx, "agg")
        w, hidden = s.sb("w", [P, D]), s.sb("hidden", [P, NB, D])
        with ExitStack() as inner:
            t = Pool(nc, inner, "aggw")
            w_loaded, scaled = t.sem("w_loaded"), t.sem("scaled")
            block = inner.enter_context(nc.Block())

            @block.sync
            def _(sync):
                sync.dma_start(w[:], a["L2_gnn_W"].partition_broadcast(P)).then_inc(w_loaded, 16)

            @block.vector
            def _(dve):
                dve.wait_ge(w_loaded, 16)
                nc.vector.tensor_tensor(hidden[:], g.xn[:], w[:].unsqueeze(1).to_broadcast([P, NB, D]), ALU.mult)\
                    .then_inc(scaled, 1)
                dve.wait_ge(scaled, 1)

        def finish(b, out):
            return nc.vector.tensor_tensor(g.x[:, b, :], out, g.x[:, b, :], ALU.add)

        stage_aggregate(nc, g, "agga", hidden, D, finish)



TINY = 1e-10
ARTANH_TOP = 1.0 - 1e-7
SERIES_BELOW = 0.25


def hyperbolic(nc, g, a):
    with ExitStack() as ctx:
        s = Pool(nc, ctx, "hyp")
        mx = s.sb("mx", [P, NB, D + 2])
        gathered = s.sb("gathered", [P, NB, D + 2])
        prod = s.sb("prod", [P, NB, D])
        stage_project(nc, g, "hypw", g.xn_t, a["L3_gnn_W"], [], (0, prod))
        stage_hyperbolic_values(nc, g, prod, mx)

        def finish(b, out):
            return nc.vector.tensor_copy(gathered[:, b, :], out)

        stage_aggregate(nc, g, "hypa", mx, D + 2, finish)
        stage_hyperbolic_end(nc, g, gathered)


def artanh(link, nc, x, log_plus, log_minus, series, square, out):
    link(nc.vector.tensor_tensor(out, log_plus, log_minus, ALU.subtract))
    link(nc.vector.tensor_scalar(out, out, 0.5, None, ALU.mult))
    link(nc.vector.tensor_tensor(square, x, x, ALU.mult))
    link(nc.vector.tensor_scalar(series, square, 1 / 11, 1 / 9, ALU.mult, ALU.add))
    for c in (1 / 7, 1 / 5, 1 / 3, 1.0):
        link(nc.vector.tensor_tensor(series, series, square, ALU.mult))
        link(nc.vector.tensor_scalar(series, series, c, None, ALU.add))
    link(nc.vector.tensor_tensor(series, series, x, ALU.mult))
    link(nc.vector.tensor_tensor(series, series, out, ALU.subtract))
    link(nc.vector.tensor_scalar(square, x, SERIES_BELOW, None, ALU.is_lt))
    link(nc.vector.tensor_tensor(series, series, square, ALU.mult))
    link(nc.vector.tensor_tensor(out, out, series, ALU.add))


def turns(eng, own, other):
    n = [0, 0]

    def hand(instruction):
        n[0] += 1
        instruction.then_inc(own, 1)

    def take():
        n[1] += 1
        eng.wait_ge(other, n[1])
    return hand, take


def stage_hyperbolic_values(nc, g, prod, values):
    with ExitStack() as ctx:
        s = Pool(nc, ctx, "hypv")
        x_norm, m_norm, clipped, log_plus, log_minus, series, square, at, factor, gamma = (
            s.sb(n, [P, NB]) for n in ("x_norm", "m_norm", "clipped", "log_plus", "log_minus", "series", "square",
                                       "at", "factor", "gamma"))
        squares = s.sb("squares", [P, 3 * NB, D], BF16)
        v_step, v_turn, a_turn, a_step = s.sem("v_step"), s.sem("v_turn"), s.sem("a_turn"), s.sem("a_step")
        block = ctx.enter_context(nc.Block())

        @block.scalar
        def _(act):
            hand, take = turns(act, a_turn, v_turn)
            for b in range(NB):
                nc.scalar.activation(squares[:, b, :], g.xn[:, b, :], ACT.Square, accum_out=x_norm[:, b:b + 1])\
                    .then_inc(a_step, 1)
                nc.scalar.activation(squares[:, NB + b, :], prod[:, b, :], ACT.Square, accum_out=m_norm[:, b:b + 1])\
                    .then_inc(a_step, 1)
            take()
            nc.scalar.activation(m_norm[:], m_norm[:], ACT.Sqrt).then_inc(a_step, 1)
            act.wait_ge(a_step, 2 * NB + 1)
            hand(nc.scalar.activation(x_norm[:], x_norm[:], ACT.Sqrt))
            take()
            nc.scalar.activation(log_plus[:], clipped[:], ACT.Ln, bias=g.one[:]).then_inc(a_step, 1)
            act.wait_ge(a_step, 2 * NB + 2)
            hand(nc.scalar.activation(log_minus[:], clipped[:], ACT.Ln, bias=g.one[:], scale=-1.0))
            take()
            hand(nc.scalar.activation(at[:], at[:], ACT.Tanh))
            take()
            for b in range(NB):
                nc.scalar.activation(squares[:, 2 * NB + b, :], prod[:, b, :], ACT.Square,
                                     accum_out=square[:, b:b + 1]).then_inc(a_step, 1)

        @block.vector
        def _(dve):
            link = chain(dve, v_step)
            hand, take = turns(dve, v_turn, a_turn)
            dve.wait_ge(a_step, 2 * NB)
            link(nc.vector.tensor_scalar(x_norm[:], x_norm[:], TINY * TINY, None, ALU.max))
            hand(nc.vector.tensor_scalar(m_norm[:], m_norm[:], TINY * TINY, None, ALU.max))
            take()
            link(nc.vector.reciprocal(factor[:], x_norm[:]))
            link(nc.vector.tensor_tensor(factor[:], factor[:], m_norm[:], ALU.mult))
            hand(nc.vector.tensor_scalar(clipped[:], x_norm[:], ARTANH_TOP, None, ALU.min))
            take()
            artanh(link, nc, clipped[:], log_plus[:], log_minus[:], series[:], square[:], at[:])
            hand(nc.vector.tensor_tensor(at[:], at[:], factor[:], ALU.mult))
            take()
            link(nc.vector.reciprocal(factor[:], m_norm[:]))
            link(nc.vector.tensor_tensor(factor[:], factor[:], at[:], ALU.mult))
            link(nc.vector.tensor_scalar(series[:], m_norm[:], TINY, None, ALU.is_gt))
            link(nc.vector.tensor_tensor(factor[:], factor[:], series[:], ALU.mult))
            for b in range(NB - 1):
                link(nc.vector.tensor_scalar(prod[:, b, :], prod[:, b, :], factor[:, b:b + 1], None, ALU.mult))
            hand(nc.vector.tensor_scalar(prod[:, NB - 1, :], prod[:, NB - 1, :], factor[:, NB - 1:NB], None, ALU.mult))
            dve.wait_ge(a_step, 3 * NB + 2)
            link(nc.vector.tensor_scalar(gamma[:], square[:], -1.0, 1.0, ALU.mult, ALU.add))
            link(nc.vector.reciprocal(gamma[:], gamma[:]))
            link(nc.vector.tensor_scalar(gamma[:], gamma[:], 2.0, 1e-15, ALU.mult, ALU.max))
            for b in range(NB):
                link(nc.vector.tensor_scalar(values[:, b, 0:D], prod[:, b, :], gamma[:, b:b + 1], None, ALU.mult))
            link(nc.vector.tensor_scalar(values[:, :, D], gamma[:], -1.0, None, ALU.add))
            link(nc.vector.memset(values[:, :, D + 1], 1.0))


def stage_hyperbolic_end(nc, g, gathered):
    with ExitStack() as ctx:
        s = Pool(nc, ctx, "hype")
        inv, sq, root, n, clipped, log_plus, log_minus, series, square, at, factor, scale = (
            s.sb(nm, [P, NB]) for nm in ("inv", "sq", "root", "n", "clipped", "log_plus", "log_minus", "series",
                                         "square", "at", "factor", "scale"))
        squares = s.sb("squares", [P, 2 * NB, D], BF16)
        r = s.sb("r", [P, NB, D])
        v_step, v_turn, a_turn, a_step = s.sem("v_step"), s.sem("v_turn"), s.sem("a_turn"), s.sem("a_step")
        denom, alpha = gathered[:, :, D], gathered[:, :, D + 1]
        block = ctx.enter_context(nc.Block())

        @block.scalar
        def _(act):
            hand, take = turns(act, a_turn, v_turn)
            take()
            for b in range(NB):
                last = nc.scalar.activation(squares[:, b, :], gathered[:, b, 0:D], ACT.Square, scale=inv[:, b:b + 1],
                                            accum_out=sq[:, b:b + 1])
                if b < NB - 1:
                    last.then_inc(a_step, 1)
            hand(last)
            for col in (root, n):
                take()
                hand(nc.scalar.activation(col[:], col[:], ACT.Sqrt))

            def logs():
                take()
                nc.scalar.activation(log_plus[:], clipped[:], ACT.Ln, bias=g.one[:]).then_inc(a_step, 1)
                hand(nc.scalar.activation(log_minus[:], clipped[:], ACT.Ln, bias=g.one[:], scale=-1.0))

            logs()
            take()
            hand(nc.scalar.activation(at[:], at[:], ACT.Tanh))
            take()
            hand(nc.scalar.activation(root[:], root[:], ACT.Sqrt))
            logs()
            take()
            for b in range(NB):
                nc.scalar.activation(r[:, b, :], gathered[:, b, 0:D], ACT.Relu, scale=scale[:, b:b + 1])\
                    .then_inc(a_step, 1)
            act.wait_ge(a_step, NB - 1 + 2 + NB)
            for b in range(NB):
                last = nc.scalar.activation(squares[:, NB + b, :], r[:, b, :], ACT.Square, accum_out=sq[:, b:b + 1])
                if b < NB - 1:
                    last.then_inc(a_step, 1)
            hand(last)
            take()
            nc.scalar.activation(root[:], sq[:], ACT.Sqrt).then_inc(a_step, 1)
            act.wait_ge(a_step, 3 * NB + 1)
            hand(nc.scalar.activation(at[:], root[:], ACT.Tanh))

        @block.vector
        def _(dve):
            link = chain(dve, v_step)
            hand, take = turns(dve, v_turn, a_turn)
            link(nc.vector.tensor_scalar(sq[:], denom, 0.0, None, ALU.is_ge))
            link(nc.vector.tensor_scalar(sq[:], sq[:], 2.0, -1.0, ALU.mult, ALU.add))
            link(nc.vector.tensor_tensor(inv[:], denom, sq[:], ALU.mult))
            link(nc.vector.tensor_scalar(inv[:], inv[:], TINY, None, ALU.max))
            link(nc.vector.tensor_tensor(inv[:], inv[:], sq[:], ALU.mult))
            hand(nc.vector.reciprocal(inv[:], inv[:]))
            take()
            dve.wait_ge(a_step, NB - 1)
            link(nc.vector.tensor_scalar(root[:], sq[:], -1.0, 1.0, ALU.mult, ALU.add))
            hand(nc.vector.tensor_scalar(root[:], root[:], TINY, None, ALU.max))
            take()
            link(nc.vector.tensor_scalar(root[:], root[:], 1.0, None, ALU.add))
            link(nc.vector.reciprocal(factor[:], root[:]))
            link(nc.vector.tensor_tensor(sq[:], sq[:], factor[:], ALU.mult))
            link(nc.vector.tensor_tensor(sq[:], sq[:], factor[:], ALU.mult))
            hand(nc.vector.tensor_scalar(n[:], sq[:], TINY * TINY, None, ALU.max))
            take()
            hand(nc.vector.tensor_scalar(clipped[:], n[:], ARTANH_TOP, None, ALU.min))
            take()
            artanh(link, nc, clipped[:], log_plus[:], log_minus[:], series[:], square[:], at[:])
            hand(nc.vector.tensor_tensor(at[:], at[:], alpha, ALU.mult))
            take()
            link(nc.vector.reciprocal(n[:], n[:]))
            link(nc.vector.tensor_tensor(at[:], at[:], n[:], ALU.mult))
            link(nc.vector.tensor_tensor(factor[:], factor[:], at[:], ALU.mult))
            link(nc.vector.tensor_tensor(root[:], sq[:], at[:], ALU.mult))
            link(nc.vector.tensor_tensor(root[:], root[:], at[:], ALU.mult))
            hand(nc.vector.tensor_scalar(root[:], root[:], TINY * TINY, None, ALU.max))
            take()
            hand(nc.vector.tensor_scalar(clipped[:], root[:], ARTANH_TOP, None, ALU.min))
            take()
            artanh(link, nc, clipped[:], log_plus[:], log_minus[:], series[:], square[:], at[:])
            link(nc.vector.reciprocal(root[:], root[:]))
            link(nc.vector.tensor_tensor(at[:], at[:], root[:], ALU.mult))
            link(nc.vector.tensor_tensor(scale[:], factor[:], at[:], ALU.mult))
            hand(nc.vector.tensor_tensor(scale[:], scale[:], inv[:], ALU.mult))
            take()
            dve.wait_ge(a_step, 3 * NB)
            hand(nc.vector.tensor_scalar(sq[:], sq[:], TINY * TINY, None, ALU.max))
            take()
            link(nc.vector.reciprocal(root[:], root[:]))
            link(nc.vector.tensor_tensor(at[:], at[:], root[:], ALU.mult))
            for b in range(NB):
                link(nc.vector.scalar_tensor_tensor(out=g.x[:, b, :], in0=r[:, b, :], scalar=at[:, b:b + 1],
                                                    in1=g.x[:, b, :], op0=ALU.mult, op1=ALU.add))



HID = 512
HT = HID // P


def stage_gated_hidden(nc, g, tag, src_t, w_drams, h):
    pairs = [(i, j) for i in range(len(w_drams)) for j in range(HT)]
    with ExitStack() as ctx:
        s = Pool(nc, ctx, tag)
        w = [s.sb(f"w{i}", [P, KD, 2 * HID]) for i in range(len(w_drams))]
        gate = [s.sb(f"gate{i}", [P, NT]) for i in range(2)]
        wide = [s.ps(f"wide{i}", [P, CH, BANK]) for i in range(2)]
        w_loaded = [s.sem(f"w_loaded{i}") for i in range(len(w_drams))]
        pad, a_full, b_full, gate_done, h_done = (s.sem("pad"), s.sem("a_full"), s.sem("b_full"), s.sem("gate_done"),
                                                  s.sem("h_done"))
        block = ctx.enter_context(nc.Block())

        @block.sync
        def _(sync):
            for i, dram in enumerate(w_drams):
                sync.dma_start(w[i][:], dram.rearrange("(k p) o -> p k o", p=P)).then_inc(w_loaded[i], 16)

        @block.gpsimd
        def _(pool):
            nc.gpsimd.memset(h[:, :, NT:NP], 0.0).then_inc(pad, 1)
            pool.wait_ge(pad, 1)

        @block.tensor
        def _(pe):
            for t, (i, j) in enumerate(pairs):
                if j == 0:
                    pe.wait_ge(w_loaded[i], 16)
                for half, (full, read) in enumerate(((a_full, gate_done), (b_full, h_done))):
                    if t:
                        pe.wait_ge(read, t)
                    for c in range(CH):
                        for k in range(KD):
                            last = nc.tensor.matmul(wide[half][:, c, 0:CW],
                                                    w[i][:, k, half * HID + j * P:half * HID + (j + 1) * P],
                                                    src_t[:, k, c * CW:(c + 1) * CW], start=(k == 0), stop=(k == KD - 1))
                    last.then_inc(full, 1)

        @block.scalar
        def _(act):
            for t in range(len(pairs)):
                act.wait_ge(a_full, t + 1)
                if t >= 2:
                    act.wait_ge(h_done, t - 1)
                nc.scalar.activation(gate[t % 2][:].rearrange("p (c n) -> p c n", c=CH), wide[0][:, :, 0:CW], ACT.Silu)\
                    .then_inc(gate_done, 1)

        @block.vector
        def _(dve):
            for t in range(len(pairs)):
                dve.wait_ge(b_full, t + 1)
                dve.wait_ge(gate_done, t + 1)
                nc.vector.tensor_tensor(h[:, t, 0:NT].rearrange("p (c n) -> p c n", c=CH), wide[1][:, :, 0:CW],
                                        gate[t % 2][:].rearrange("p (c n) -> p c n", c=CH), ALU.mult).then_inc(h_done, 1)


def stage_routed_out(nc, g, tag, h, shared_dram, expert_dram, weights, experts):
    pairs = experts // 2
    with ExitStack() as ctx:
        s = Pool(nc, ctx, tag)
        ws = s.sb("ws", [P, HT, D])
        we = s.sb("we", [P, HT, experts * D])
        ring = [s.ps(f"ring{i}", [P, BANK]) for i in range(8)]
        ws_loaded, we_loaded, full, read = s.sem("ws_loaded"), s.sem("we_loaded"), s.sem("full"), s.sem("read")
        v_step = s.sem("v_step")
        block = ctx.enter_context(nc.Block())

        @block.sync
        def _(sync):
            sync.dma_start(ws[:], shared_dram.rearrange("(k p) o -> p k o", p=P)).then_inc(ws_loaded, 16)
            sync.dma_start(we[:], expert_dram.rearrange("(k p) o -> p k o", p=P)).then_inc(we_loaded, 16)

        @block.tensor
        def _(pe):
            pe.wait_ge(ws_loaded, 16)
            n = 0
            for b in range(NB):
                for j in range(1 + pairs):
                    if n >= 8:
                        pe.wait_ge(read, n - 7)
                    if n == 1:
                        pe.wait_ge(we_loaded, 16)
                    width = D if j == 0 else 2 * D
                    for f in range(HT):
                        lhs = h[:, f + (HT if j else 0), b * P:(b + 1) * P]
                        rhs = ws[:, f, :] if j == 0 else we[:, f, (j - 1) * 2 * D:j * 2 * D]
                        last = nc.tensor.matmul(ring[n % 8][:, 0:width], lhs, rhs, start=(f == 0), stop=(f == HT - 1))
                    last.then_inc(full, 1)
                    n += 1

        @block.vector
        def _(dve):
            link = chain(dve, v_step)
            n = 0
            for b in range(NB):
                for j in range(1 + pairs):
                    dve.wait_ge(full, n + 1)
                    if j == 0:
                        last = nc.vector.tensor_tensor(g.x[:, b, :], ring[n % 8][:, 0:D], g.x[:, b, :], ALU.add)
                    else:
                        e = 2 * (j - 1)
                        link(nc.vector.scalar_tensor_tensor(out=g.x[:, b, :], in0=ring[n % 8][:, 0:D],
                                                            scalar=weights[:, b, e:e + 1], in1=g.x[:, b, :],
                                                            op0=ALU.mult, op1=ALU.add))
                        last = nc.vector.scalar_tensor_tensor(out=g.x[:, b, :], in0=ring[n % 8][:, D:2 * D],
                                                              scalar=weights[:, b, e + 1:e + 2], in1=g.x[:, b, :],
                                                              op0=ALU.mult, op1=ALU.add)
                    last.then_inc(read, 1)
                    n += 1
                    dve.wait_ge(read, n)


def shared_and_routed(nc, g, a):
    experts = a["L1_ffn_expert_gate_w"].shape[0]
    with ExitStack() as ctx:
        s = Pool(nc, ctx, "sr")
        weights = s.sb("weights", [P, NB, experts])
        counts = s.sb("counts", [P, NB, experts + 1])
        affine = s.sb("affine", [P, 2 * KD])
        with ExitStack() as inner:
            t = Pool(nc, inner, "srl")
            loaded, ones = t.sem("loaded"), t.sem("ones")
            block = inner.enter_context(nc.Block())

            @block.sync
            def _(sync):
                sync.dma_start(affine[:], a["L1_ffn_affine"]).then_inc(loaded, 16)
                sync.wait_ge(loaded, 16)

            @block.gpsimd
            def _(pool):
                nc.gpsimd.memset(counts[:, :, experts], 1.0).then_inc(ones, 1)
                pool.wait_ge(ones, 1)

        stage_norm(nc, g, "srn", g.xn, g.xn, g.xn_t, affine[:, 0:KD], affine[:, KD:2 * KD])
        stage_route(nc, g, "srr", g.xn_t, a["L1_ffn_gates"], experts + 2, "grouped", weights, counts,
                    bias=a["L1_ffn_gate_bias"])
        stage_spread(nc, g, "srs", counts, experts + 1, a["L1_ffn_out_bias"], g.x, True)
        h = s.sb("h", [P, 2 * HT, NP])
        stage_gated_hidden(nc, g, "srh", g.xn_t, [a["L1_ffn_shared_in_w"], a["L1_ffn_expert_in_w"]], h)
        stage_routed_out(nc, g, "sro", h, a["L1_ffn_shared_out_w"], a["L1_ffn_expert_out_weight"], weights, experts)



HEADS = 8
HD = D // HEADS
PAIRS = HEADS // 2
QR = 3 * HD
STEPS = CH * NB
UNITS = 2 * STEPS
RING = 3
PRING = 4
MAX_TILES = 2 * NB
MAX_CHUNKS = MAX_TILES * CH
TURN_STEP = STEPS - 3
MAX_STEPS = [s for s in range(4, TURN_STEP + 1) if s % NB > 1]
MAX_AT = {s: [m for m in range(MAX_CHUNKS) if m * len(MAX_STEPS) // MAX_CHUNKS == i] for i, s in enumerate(MAX_STEPS)}
HALVES = [(0, 6), (6, 5)]
F_UNITS = 2 * FT
V_LINKS = CH * PAIRS + 2 * NB + 1 + 2 * NB + 2


def shares(items, slots):
    items = list(items)
    return [[m for n, m in enumerate(items) if n * slots // len(items) == i] for i in range(slots)]


FRONT_F2 = shares(range(0, 24), 6) + shares(range(46, MAX_CHUNKS), 5)
FRONT_F1 = shares(range(24, 46), F_UNITS)


def slab(nc, s, name, width):
    at = -(-nc.sbuf_base // 32) * 32
    s.sb(name, [P, width])
    assert nc.sbuf_base == at + 4 * width, (nc.sbuf_base, at, width)
    return at


def stage_transformer_experts(nc, g, a, weights, acc):
    experts = a["L2_ffn_Wqkv"].shape[0]
    with ExitStack() as ctx:
        s = Pool(nc, ctx, "tx")
        wqkv, wo = s.sb("wqkv", [P, KD, 3 * D]), s.sb("wo", [P, KD, D])
        w1, w2 = s.sb("w1", [P, KD, FF]), s.sb("w2", [P, FT, D])
        bv = s.sb("bv", [P, D])
        rows = s.sb("rows", [P, 5, D])
        bo, bf2, g2, be1_row, g1_row = (rows[:, i, :] for i in range(5))
        cols = s.sb("cols", [P, experts, 2 * KD + FT + 2 * KD])
        hi_a, lo_a = s.sb("hi_a", [P, 2, NT], F32R), s.sb("lo_a", [P, 2, NT], F32R)
        half = HALVES[0][1] * P
        at = slab(nc, s, "slab", FT * half)
        hi_b = nc.alloc_sbuf_tensor_at("tx_hi_b", [P, 2, NT], F32R, offset=at)
        lo_b = nc.alloc_sbuf_tensor_at("tx_lo_b", [P, 2, NT], F32R, offset=at + 2 * NT * 4)
        h = nc.alloc_sbuf_tensor_at("tx_h", [P, FT, half], F32, offset=at)
        ops = s.sb("ops", [P, 4, 2, NP], F32R)
        v = s.sb("v", [P, NB, D])
        at2 = slab(nc, s, "slab2", KD * NP)
        ctx_t = nc.alloc_sbuf_tensor_at("tx_ctx", [P, KD, NP], F32, offset=at2)
        x1_t = nc.alloc_sbuf_tensor_at("tx_x1t", [P, KD, NP], F32, offset=at2)
        p = s.sb("p", [P, PRING, CW])
        x1 = s.sb("x1", [P, NB, D])
        inv_sum = s.sb("inv_sum", [2 * HD, 2, CW])
        chunk_max = s.sb("chunk_max", [P, MAX_TILES, CH])
        neg_max = s.sb("neg_max", [P, MAX_TILES])
        m_hi, m_lo = s.sb("m_hi", [MAX_TILES, P], F32R), s.sb("m_lo", [MAX_TILES, P], F32R)
        ones = s.sb("ones", [P, HD])
        key_bias = s.sb("key_bias", [P, 1])
        tmp = [s.sb(f"tmp{i}", [P, D]) for i in range(2)]
        z = [s.sb(f"z{i}", [P, D]) for i in range(2)]
        stats, mean_var = s.sb("stats", [P, NB, 6]), s.sb("mean_var", [P, NB, 2])
        std, scale, shift = s.sb("std", [P, NB]), s.sb("scale", [P, NB]), s.sb("shift", [P, NB])

        bank = s.ps("bank", [P, 8, BANK])
        wide = [bank[:, 0:3, :], bank[:, 3:6, :]]
        row = [bank[:, 6, :], bank[:, 7, :]]

        front_loaded, w_loaded, cols_loaded = s.sem("front_loaded"), s.sem("w_loaded"), s.sem("cols_loaded")
        ops_loaded = [s.sem("ops_loaded_even"), s.sem("ops_loaded_odd")]
        max_loaded, const_made = s.sem("max_loaded"), s.sem("const_made")
        qk_full, v_full, max_full, turned_max, s_full, pv_done = (
            s.sem(n) for n in ("qk_full", "v_full", "max_full", "turned_max", "s_full", "pv_done"))
        wo_full, x1t_full, f1_full, f2_full = (s.sem(n) for n in ("wo_full", "x1t_full", "f1_full", "f2_full"))
        hi_done, m_hi_done, exp_done, std_done, x1t_done, h_done, gelu_done, z_full, act_seen = (
            s.sem(n) for n in ("hi_done", "m_hi_done", "exp_done", "std_done", "x1t_done", "h_done", "gelu_done",
                               "z_full", "act_seen"))
        lo_done, v_read, max_done, m_lo_done, ctx_done, wo_read, y_done, stats_done, scaled, v_step, v_seen, f2_added = (
            s.sem(n) for n in ("lo_done", "v_read", "max_done", "m_lo_done", "ctx_done", "wo_read", "y_done",
                               "stats_done", "scaled", "v_step", "v_seen", "f2_added"))
        aggr_step, joined_max = s.sem("aggr_step"), s.sem("joined_max")
        x1_done, z_used, rows_used, pool_step, key_zero, pads_zero, pool_seen = (
            s.sem(n) for n in ("x1_done", "z_used", "rows_used", "pool_step", "key_zero", "pads_zero", "pool_seen"))

        def over_experts(eng, body):
            body(0, False, True)
            with eng.Fori(1, experts - 1) as e:
                body(e, True, True)
            body(experts - 1, True, False)

        block = ctx.enter_context(nc.Block())
        nc.disable_value_cache = True

        @block.sync
        def _(sync):
            def load_front(e):
                sync.dma_start(wqkv[:], a["L2_ffn_Wqkv"][e].rearrange("(k p) o -> p k o", p=P)).then_inc(front_loaded, 16)
                sync.dma_start(bv[:], a["L2_ffn_bv"][e].partition_broadcast(P)).then_inc(front_loaded, 16)

            def load_pair(pair):
                hi, lo = (hi_a, lo_a) if pair < 2 else (hi_b, lo_b)
                for head in (2 * pair, 2 * pair + 1):
                    lanes = slice(HD * (head % 4), HD * (head % 4) + HD)
                    for kind, parts in enumerate(((hi, lo, hi), (hi, hi, lo))):
                        for i, part in enumerate(parts):
                            sync.dma_start(ops[HD * i:HD * (i + 1), head % 4, kind, 0:NT].bitcast(F32),
                                           part[lanes, kind, :].bitcast(F32)).then_inc(ops_loaded[pair % 2], 16)

            def load_first_pairs(e):
                sync.wait_ge(lo_done, 4 * e + 2)
                load_pair(0)
                load_pair(1)

            def load_max(e, pair):
                sync.wait_ge(m_hi_done, PAIRS * e + (pair + 1))
                sync.wait_ge(m_lo_done, PAIRS * e + (pair + 1))
                for i in range(2):
                    head = 2 * pair + i
                    for r, part in enumerate((m_hi, m_lo)):
                        sync.dma_start(ops[QR + r:QR + r + 1, head % 4, 0, :].bitcast(F32),
                                       part[i * NB:(i + 1) * NB, :].bitcast(F32)).then_inc(max_loaded, 16)

            def body(e, before, after):
                load_max(e, 0)
                if after:
                    sync.wait_ge(qk_full, 4 * e + 4)
                    load_front(e + 1)
                if before:
                    sync.wait_ge(f2_full, NB * e)
                sync.dma_start(wo[:], a["L2_ffn_Wo"][e].rearrange("(k p) o -> p k o", p=P)).then_inc(w_loaded, 16)
                sync.dma_start(w1[:], a["L2_ffn_W1"][e].rearrange("(k p) o -> p k o", p=P)).then_inc(w_loaded, 16)
                sync.dma_start(w2[:], a["L2_ffn_W2"][e].rearrange("(f p) o -> p f o", p=P)).then_inc(w_loaded, 16)
                if before:
                    sync.wait_ge(rows_used, e)
                sync.dma_start(rows[:], a["L2_ffn_rows"][e].partition_broadcast(P)).then_inc(w_loaded, 16)
                load_max(e, 1)
                sync.wait_ge(lo_done, 4 * e + 4)
                for pair in (2, 3):
                    sync.wait_ge(pv_done, PAIRS * STEPS * e + (pair - 1) * STEPS)
                    load_pair(pair)
                    load_max(e, pair)
                if after:
                    load_first_pairs(e + 1)

            load_front(0)
            sync.dma_start(cols[:], a["L2_ffn_cols"]).then_inc(cols_loaded, 16)
            sync.wait_ge(const_made, 4)
            load_first_pairs(0)
            over_experts(sync, body)

        @block.gpsimd
        def _(pool):
            nc.gpsimd.memset(ones[:], 1.0).then_inc(const_made, 1)
            pool.wait_ge(const_made, 1)
            nc.gpsimd.memset(ops[QR:QR + 2, :, 1, :].bitcast(F32), 1.0).then_inc(const_made, 1)
            pool.wait_ge(const_made, 2)
            nc.gpsimd.memset(ops[0:QR, :, :, NT:NP].bitcast(F32), 0.0).then_inc(const_made, 1)
            pool.wait_ge(const_made, 3)
            nc.gpsimd.memset(key_bias[:], 0.0).then_inc(key_zero, 1)
            pool.wait_ge(key_zero, 1)
            nc.gpsimd.affine_select(out=key_bias[:], in_=key_bias[:], compare_op=ALU.is_gt, fill=-BIG,
                                    base=N - (NB - 1) * P, pattern=[[0, 1]], channel_multiplier=-1)\
                .then_inc(const_made, 1)
            pool.sem_inc(z_used, 2)

            def add_result(e):
                for b in range(NB):
                    z_b = z[b % 2]
                    pool.wait_ge(z_full, NB * e + (b + 1))
                    nc.gpsimd.tensor_tensor(z_b[:], z_b[:], g2, ALU.mult).then_inc(z_used, 1)
                    pool.wait_ge(z_used, 2 * NB * e + (2 * b + 3))
                    nc.gpsimd.tensor_tensor(acc[:, b, :], acc[:, b, :], z_b[:], ALU.add).then_inc(z_used, 1)
                    pool.wait_ge(z_used, 2 * NB * e + (2 * b + 4))
                pool.sem_inc(rows_used, 1)

            def body(e, before, after):
                pool.wait_ge(qk_full, 4 * e + 3)
                pool.sem_inc(pool_seen, 1)
                nc.gpsimd.memset(ctx_t[:, :, NT:NP], 0.0).then_inc(pads_zero, 1)
                if before:
                    add_result(e - 1)
                pool.wait_ge(w_loaded, 64 * e + 64)
                for b in range(NB):
                    pool.wait_ge(x1t_full, 6 * e + KD * (b // 4 + 1))
                    nc.gpsimd.tensor_tensor(x1[:, b, :], x1[:, b, :], g1_row, ALU.mult).then_inc(pool_step, 1)
                    pool.wait_ge(pool_step, NB * e + (b + 1))
                    nc.gpsimd.tensor_tensor(x1[:, b, :], x1[:, b, :], be1_row, ALU.add).then_inc(x1_done, 1)

            over_experts(pool, body)
            add_result(experts - 1)

        @block.tensor
        def _(pe):
            def project(e, tile):
                c0 = (tile % 2) * D + (tile // 2) * P
                for c in range(CH):
                    for k in range(KD):
                        last = nc.tensor.matmul(wide[tile % 2][:, c, 0:CW], wqkv[:, k, c0:c0 + P],
                                                g.xn_t[:, k, c * CW:(c + 1) * CW], start=(k == 0), stop=(k == KD - 1))
                last.then_inc(qk_full, 1)

            def project_v(e, b):
                if b >= 2:
                    pe.wait_ge(v_read, NB * e + (b - 1))
                for k in range(KD):
                    last = nc.tensor.matmul(row[b % 2][:, 0:D], g.xn_t[:, k, b * P:(b + 1) * P],
                                            wqkv[:, k, 2 * D:3 * D], start=(k == 0), stop=(k == KD - 1))
                last.then_inc(v_full, 1)

            def max_scores(e, pair, m):
                tile, c = m // CH, m % CH
                head, b = 2 * pair + tile // NB, tile % NB
                if m == 0:
                    pe.wait_ge(ops_loaded[pair % 2], 384 * e + 192 * (pair // 2 + 1))
                    if pair == 0:
                        pe.wait_ge(lo_done, 4 * e + 2)
                    elif pair == 1:
                        pe.wait_ge(lo_done, 4 * e + 4)
                    else:
                        pe.wait_ge(m_lo_done, PAIRS * e + pair)
                if m >= RING:
                    pe.wait_ge(max_done, PAIRS * MAX_CHUNKS * e + (MAX_CHUNKS * pair + m - RING + 1))
                k0, w = KCH[c]
                nc.tensor.matmul(bank[:, 3 + m % RING, 0:w], ops[0:QR, head % 4, 0, b * P:(b + 1) * P],
                                 ops[0:QR, head % 4, 1, k0:k0 + w], start=True, stop=True).then_inc(max_full, 1)

            def turn_max(e, pair):
                pe.wait_ge(joined_max, PAIRS * e + (pair + 1))
                nc.tensor.transpose(bank[0:MAX_TILES, 3, 0:P], neg_max[:], g.ident[:]).then_inc(turned_max, 1)

            def scores(e, pair, step):
                c, t = step // NB, step % NB
                if step == 0:
                    pe.wait_ge(max_loaded, 64 * PAIRS * e + 64 * (pair + 1))
                    if pair == 0:
                        pe.wait_ge(lo_done, 4 * e + 3)
                for i in range(2):
                    u = UNITS * pair + 2 * step + i
                    if u >= RING:
                        pe.wait_ge(exp_done, PAIRS * UNITS * e + (u - RING + 1))
                    slot = (2 * pair + i) % 4
                    nc.tensor.matmul(bank[:, u % RING, 0:CW], ops[0:QR + 2, slot, 1, t * P:(t + 1) * P],
                                     ops[0:QR + 2, slot, 0, c * CW:(c + 1) * CW], start=True, stop=True)\
                        .then_inc(s_full, 1)

            def mix(e, pair, step, before):
                c, t = step // NB, step % NB
                chunk = CH * pair + c
                u = UNITS * pair + 2 * step
                if t == 0 and chunk >= 2:
                    pe.wait_ge(ctx_done, CH * PAIRS * e + (chunk - 1))
                if t == 0 and chunk == 0:
                    pe.wait_ge(v_read, NB * e + NB)
                    if before:
                        pe.wait_ge(f2_added, NB * e)
                pe.wait_ge(exp_done, PAIRS * UNITS * e + (u + 2))
                for i in range(2):
                    head = 2 * pair + i
                    for j, lhs in enumerate((v[:, t, head * HD:(head + 1) * HD], ones[:])):
                        lane = HD * (i + 2 * j)
                        last = nc.tensor.matmul(row[chunk % 2][lane:lane + HD, 0:CW], lhs, p[:, (u + i) % PRING, :],
                                                start=(t == 0), stop=(t == NB - 1), tile_position=(0, lane))
                last.then_inc(pv_done, 1)

            def body(e, before, after):
                pe.wait_ge(m_lo_done, PAIRS * e + 1)
                project(e, 2)
                project(e, 3)
                scores(e, 0, 0)
                for pair in range(PAIRS):
                    for step in range(STEPS):
                        if step + 1 < STEPS:
                            scores(e, pair, step + 1)
                        elif pair + 1 < PAIRS:
                            scores(e, pair + 1, 0)
                        chunks = MAX_AT.get(step, []) if pair + 1 < PAIRS else []
                        for m in chunks[:1]:
                            max_scores(e, pair + 1, m)
                        mix(e, pair, step, before)
                        for m in chunks[1:]:
                            max_scores(e, pair + 1, m)
                        if step == TURN_STEP + 1 and pair + 1 < PAIRS:
                            turn_max(e, pair + 1)

                pe.wait_ge(w_loaded, 64 * e + 64)
                pe.wait_ge(ctx_done, CH * PAIRS * e + CH * PAIRS)
                pe.wait_ge(pads_zero, e + 1)
                for b in range(NB):
                    if b >= 2:
                        pe.wait_ge(wo_read, NB * e + (b - 1))
                    for k in range(KD):
                        last = nc.tensor.matmul(row[b % 2][:, 0:D], ctx_t[:, k, b * P:(b + 1) * P], wo[:, k, :],
                                                start=(k == 0), stop=(k == KD - 1))
                    last.then_inc(wo_full, 1)
                if after:
                    pe.wait_ge(front_loaded, 32 * (e + 1) + 32)
                    project(e + 1, 0)
                    project(e + 1, 1)
                pe.wait_ge(wo_read, NB * e + NB)
                n = 0
                for b0, nb in TG:
                    for k in range(KD):
                        if n >= 2:
                            pe.wait_ge(x1t_done, 6 * e + (n - 1))
                        for b in range(b0, b0 + nb):
                            if k == 0:
                                pe.wait_ge(y_done, NB * e + (b + 1))
                            last = nc.tensor.transpose(row[n % 2][:, (b - b0) * P:(b - b0 + 1) * P],
                                                       x1[:, b, k * P:(k + 1) * P], g.ident[:])
                        last.then_inc(x1t_full, 1)
                        n += 1
                pe.wait_ge(x1t_done, 6 * e + 6)
                if after:
                    pe.wait_ge(lo_done, 4 * (e + 1) + 1)
                f = 0
                done = 0
                for i, (b0, nb) in enumerate(HALVES):
                    w = nb * P // 2
                    for n in range(F_UNITS):
                        t, c = n // 2, n % 2
                        if f >= RING:
                            pe.wait_ge(h_done, 2 * F_UNITS * e + (f - RING + 1))
                        for k in range(KD):
                            c0 = b0 * P + c * w
                            last = nc.tensor.matmul(bank[:, f % RING, 0:w], w1[:, k, t * P:(t + 1) * P],
                                                    x1_t[:, k, c0:c0 + w], start=(k == 0), stop=(k == KD - 1))
                        last.then_inc(f1_full, 1)
                        f += 1
                        if after and i == 0 and 3 <= n < 3 + NB:
                            project_v(e + 1, n - 3)
                        if after and i == 1:
                            for m in FRONT_F1[n]:
                                max_scores(e + 1, 0, m)
                    pe.wait_ge(h_done, 2 * F_UNITS * e + f)
                    for b in range(b0, b0 + nb):
                        if b == 0 and after:
                            pe.wait_ge(v_read, NB * (e + 1) + NB)
                        if b >= 2:
                            pe.wait_ge(f2_added, NB * e + (b - 1))
                        for t in range(FT):
                            last = nc.tensor.matmul(row[b % 2][:, 0:D], h[:, t, (b - b0) * P:(b - b0 + 1) * P],
                                                    w2[:, t, :], start=(t == 0), stop=(t == FT - 1))
                        last.then_inc(f2_full, 1)
                        if after:
                            for m in FRONT_F2[b]:
                                max_scores(e + 1, 0, m)
                if after:
                    turn_max(e + 1, 0)

            pe.wait_ge(const_made, 4)
            pe.wait_ge(front_loaded, 32)
            project(0, 0)
            project(0, 1)
            for b in range(NB):
                project_v(0, b)
            for m in range(MAX_CHUNKS):
                max_scores(0, 0, m)
            turn_max(0, 0)
            over_experts(pe, body)

        @block.scalar
        def _(act):
            def high(e, tile):
                into = (hi_a, hi_b)[tile // 2]
                act.wait_ge(qk_full, 4 * e + (tile + 1))
                act.sem_inc(act_seen, 1)
                nc.scalar.activation(into[:, tile % 2, :].rearrange("p (c n) -> p c n", c=CH),
                                     wide[tile % 2][:, :, 0:CW], ACT.Identity,
                                     bias=cols[:, bass.ds(e, 1), (tile % 2) * KD + tile // 2]).then_inc(hi_done, 1)

            def exponent(e, pair, step, i):
                u = UNITS * pair + 2 * step + i
                act.wait_ge(s_full, PAIRS * UNITS * e + (u + 1))
                if u >= PRING:
                    act.wait_ge(pv_done, PAIRS * STEPS * e + (u // 2 - 1))
                bias = dict(bias=key_bias[:]) if step % NB == NB - 1 else {}
                nc.scalar.activation(p[:, u % PRING, :], bank[:, u % RING, 0:CW], ACT.Exp, scale=HD ** -0.5, **bias)\
                    .then_inc(exp_done, 1)

            def high_max(e, pair, first=False):
                act.wait_ge(turned_max, PAIRS * e + (pair + 1))
                if not first:
                    act.wait_ge(max_loaded, 64 * PAIRS * e + 64 * pair)
                nc.scalar.activation(m_hi[:], bank[0:MAX_TILES, 3, 0:P], ACT.Copy).then_inc(m_hi_done, 1)

            def weighted(e, b):
                act.wait_ge(z_used, 2 * NB * e + max(2 * b, 2))
                nc.scalar.activation(z[b % 2][:], x1[:, b, :], ACT.Identity, scale=scale[:, b:b + 1],
                                     bias=shift[:, b:b + 1]).then_inc(z_full, 1)

            def body(e, before, after):
                high(e, 2)
                high(e, 3)
                for pair in range(PAIRS):
                    for step in range(STEPS):
                        for i in range(2):
                            exponent(e, pair, step, i)
                        if before and pair == 0 and step == 3:
                            act.wait_ge(scaled, e)
                        if before and pair == 0 and step % 2 and 0 <= (step - 3) // 2 < NB:
                            weighted(e - 1, (step - 3) // 2)
                        if step == TURN_STEP + 1 and pair + 1 < PAIRS:
                            high_max(e, pair + 1)
                act.wait_ge(stats_done, 2 * e + 1)
                nc.scalar.activation(std[:], mean_var[:, :, 1], ACT.Sqrt, bias=g.eps[:]).then_inc(std_done, 1)
                if after:
                    high(e + 1, 0)
                    high(e + 1, 1)
                n = 0
                for b0, nb in TG:
                    for k in range(KD):
                        act.wait_ge(x1t_full, 6 * e + (n + 1))
                        act.sem_inc(act_seen, 1)
                        c = 2 * KD + FT + k
                        nc.scalar.activation(x1_t[:, k, b0 * P:(b0 + nb) * P], row[n % 2][:, 0:nb * P], ACT.Identity,
                                             scale=cols[:, bass.ds(e, 1), c], bias=cols[:, bass.ds(e, 1), c + KD])\
                            .then_inc(x1t_done, 1)
                        n += 1
                f = 0
                for b0, nb in HALVES:
                    w = nb * P // 2
                    for n in range(F_UNITS):
                        t, c = n // 2, n % 2
                        act.wait_ge(f1_full, 2 * F_UNITS * e + (f + 1))
                        act.sem_inc(act_seen, 1)
                        nc.scalar.activation(h[:, t, c * w:(c + 1) * w], bank[:, f % RING, 0:w], ACT.Gelu,
                                             bias=cols[:, bass.ds(e, 1), 2 * KD + t]).then_inc(h_done, 1)
                        f += 1
                    for b in range(b0, b0 + nb):
                        act.wait_ge(f2_added, NB * e + (b + 1))
                        nc.scalar.activation(tmp[b % 2][:], tmp[b % 2][:], ACT.Gelu).then_inc(gelu_done, 1)
                if after:
                    high_max(e + 1, 0)
                act.wait_ge(stats_done, 2 * e + 2)
                nc.scalar.activation(std[:], mean_var[:, :, 1], ACT.Sqrt, bias=g.eps[:]).then_inc(std_done, 1)

            act.wait_ge(cols_loaded, 16)
            act.wait_ge(const_made, 4)
            high(0, 0)
            high(0, 1)
            high_max(0, 0, first=True)
            over_experts(act, body)
            act.wait_ge(scaled, experts)
            for b in range(NB):
                weighted(experts - 1, b)

        @block.vector
        def _(dve):
            n, base = [0], [0]

            def link(instruction):
                n[0] += 1
                instruction.then_inc(v_step, 1)
                dve.wait_ge(v_step, base[0] + n[0])

            def low(e, tile):
                hi, lo = ((hi_a, lo_a), (hi_b, lo_b))[tile // 2]
                dve.wait_ge(hi_done, 4 * e + (tile + 1))
                nc.vector.scalar_tensor_tensor(out=lo[:, tile % 2, :].rearrange("p (c n) -> p c n", c=CH),
                                               in0=wide[tile % 2][:, :, 0:CW],
                                               scalar=cols[:, bass.ds(e, 1), (tile % 2) * KD + tile // 2],
                                               in1=hi[:, tile % 2, :].rearrange("p (c n) -> p c n", c=CH),
                                               op0=ALU.add, op1=ALU.subtract).then_inc(lo_done, 1)

            def read_v(e, b):
                if b == 0:
                    dve.wait_ge(front_loaded, 32 * e + 32)
                dve.wait_ge(v_full, NB * e + (b + 1))
                nc.vector.tensor_tensor(v[:, b, :], row[b % 2][:, 0:D], bv[:], ALU.add).then_inc(v_read, 1)

            def row_max(e, pair, m):
                dve.wait_ge(max_full, PAIRS * MAX_CHUNKS * e + (MAX_CHUNKS * pair + m + 1))
                nc.vector.tensor_reduce(chunk_max[:, m // CH, m % CH:m % CH + 1], bank[:, 3 + m % RING, 0:KCH[m % CH][1]],
                                        AX_X, ALU.max, negate=True).then_inc(max_done, 1)

            def join_max(e, pair):
                dve.wait_ge(max_done, PAIRS * MAX_CHUNKS * e + MAX_CHUNKS * (pair + 1))
                nc.vector.tensor_reduce(neg_max[:], chunk_max[:], AX_X, ALU.min).then_inc(joined_max, 1)

            def low_max(e, pair):
                dve.wait_ge(m_hi_done, PAIRS * e + (pair + 1))
                nc.vector.tensor_tensor(m_lo[:], bank[0:MAX_TILES, 3, 0:P], m_hi[:], ALU.subtract).then_inc(m_lo_done, 1)

            def normalise(e, pair, c):
                chunk = CH * pair + c
                out = row[chunk % 2]
                dve.wait_ge(pv_done, PAIRS * STEPS * e + NB * (chunk + 1))
                link(nc.vector.reciprocal(inv_sum[:, chunk % 2, :], out[2 * HD:4 * HD, 0:CW]))
                lane = 2 * HD * (pair % 2)
                nc.vector.tensor_tensor(ctx_t[lane:lane + 2 * HD, pair // 2, c * CW:(c + 1) * CW], out[0:2 * HD, 0:CW],
                                        inv_sum[:, chunk % 2, :], ALU.mult).then_inc(ctx_done, 1)

            def statistics():
                dve.sem_inc(v_seen, 1)
                for b in range(NB - 1):
                    nc.vector.bn_aggr(mean_var[:, b, :], stats[:, b, :]).then_inc(aggr_step, 1)
                nc.vector.bn_aggr(mean_var[:, NB - 1, :], stats[:, NB - 1, :]).then_inc(stats_done, 1)

            def body(e, before, after):
                low(e, 2)
                low(e, 3)
                for pair in range(PAIRS):
                    for step in range(STEPS):
                        chunks = MAX_AT.get(step, []) if pair + 1 < PAIRS else []
                        for m in chunks:
                            row_max(e, pair + 1, m)
                        if step == TURN_STEP and pair + 1 < PAIRS:
                            join_max(e, pair + 1)
                        if step % NB == NB - 1 and step < STEPS - 1:
                            normalise(e, pair, step // NB)
                        if step == TURN_STEP + 1 and pair + 1 < PAIRS:
                            low_max(e, pair + 1)
                    normalise(e, pair, CH - 1)

                for b in range(NB):
                    dve.wait_ge(wo_full, NB * e + (b + 1))
                    if b == 0 and before:
                        dve.wait_ge(z_full, NB * e)
                    nc.vector.tensor_tensor(x1[:, b, :], row[b % 2][:, 0:D], bo, ALU.add).then_inc(wo_read, 1)
                    dve.wait_ge(wo_read, NB * e + (b + 1))
                    link(nc.vector.tensor_tensor(x1[:, b, :], x1[:, b, :], g.xn[:, b, :], ALU.add))
                    link(nc.vector.bn_stats(stats[:, b, :], x1[:, b, :]))
                statistics()
                dve.wait_ge(std_done, 2 * e + 1)
                link(nc.vector.reciprocal(std[:], std[:]))
                for b in range(NB):
                    nc.vector.tensor_scalar(x1[:, b, :], x1[:, b, :], mean_var[:, b, 0:1], std[:, b:b + 1],
                                            ALU.subtract, ALU.mult).then_inc(y_done, 1)
                if after:
                    low(e + 1, 0)
                    low(e + 1, 1)
                    for b in range(NB):
                        read_v(e + 1, b)

                def row_end(b):
                    dve.wait_ge(gelu_done, NB * e + (b + 1))
                    dve.wait_ge(x1_done, NB * e + (b + 1))
                    link(nc.vector.tensor_tensor(x1[:, b, :], tmp[b % 2][:], x1[:, b, :], ALU.add))
                    link(nc.vector.bn_stats(stats[:, b, :], x1[:, b, :]))

                for i, (b0, nb) in enumerate(HALVES):
                    if i == 1 and after:
                        for t in range(F_UNITS):
                            for m in FRONT_F1[t]:
                                row_max(e + 1, 0, m)
                    for b in range(b0, b0 + nb):
                        dve.wait_ge(f2_full, NB * e + (b + 1))
                        nc.vector.tensor_tensor(tmp[b % 2][:], row[b % 2][:, 0:D], bf2, ALU.add).then_inc(f2_added, 1)
                        if after:
                            for m in FRONT_F2[b]:
                                row_max(e + 1, 0, m)
                        row_end(b)
                if after:
                    join_max(e + 1, 0)
                    low_max(e + 1, 0)
                statistics()
                dve.wait_ge(std_done, 2 * e + 2)
                link(nc.vector.reciprocal(std[:], std[:]))
                link(nc.vector.tensor_tensor(scale[:], std[:], weights[:, :, bass.ds(e, 1)].rearrange("p b o -> p (b o)"),
                                             ALU.mult))
                nc.vector.scalar_tensor_tensor(out=shift[:], in0=mean_var[:, :, 0], scalar=-1.0, in1=scale[:],
                                               op0=ALU.mult, op1=ALU.mult).then_inc(scaled, 1)

            def counted_body(e, before, after):
                n[0] = 0
                base[0] = V_LINKS * e
                body(e, before, after)
                assert n[0] == V_LINKS, n[0]

            dve.wait_ge(cols_loaded, 16)
            low(0, 0)
            low(0, 1)
            for b in range(NB):
                read_v(0, b)
            for m in range(MAX_CHUNKS):
                row_max(0, 0, m)
            join_max(0, 0)
            low_max(0, 0)
            over_experts(dve, counted_body)


def transformer_experts(nc, g, a):
    with ExitStack() as ctx:
        s = Pool(nc, ctx, "te")
        experts = a["L2_ffn_Wqkv"].shape[0]
        weights, mask = s.sb("weights", [P, NB, experts]), s.sb("mask", [P, NB, experts])
        stage_route(nc, g, "ter", g.xn_t, a["L2_ffn_expert_queries"], experts, "keys", weights, mask,
                    keys=(a["L2_ffn_gate_Wk"], a["L2_ffn_gate_bk"]))
        stage_spread(nc, g, "tes", weights, experts, a["L2_ffn_be2"], g.x, True)
        stage_transformer_experts(nc, g, a, weights, g.x)



class Global:
    pass


def stage_clear(nc):
    used = sorted(nc.released_uncleared_semaphores)
    block_ctx = ExitStack()
    with block_ctx:
        block = block_ctx.enter_context(nc.Block())

        @block.gpsimd
        def _(pool):
            pool.sem_clear(range(used[0], used[-1] + 1))


def stage_store(nc, g, out):
    with ExitStack() as ctx:
        s = Pool(nc, ctx, "store")
        stored = s.sem("stored")
        block = ctx.enter_context(nc.Block())

        @block.sync
        def _(sync):
            full = N // P
            sync.dma_start(out[0:full * P, :].rearrange("(b p) d -> p b d", p=P), g.x[:, 0:full, :]).then_inc(stored, 16)
            sync.dma_start(out[full * P:N, :], g.x[0:N - full * P, full, :]).then_inc(stored, 16)
            sync.wait_ge(stored, 32)


def program(nc, a, out, start=0, stop=8):
    with ExitStack() as ctx:
        s = Pool(nc, ctx, "g")
        g = Global()
        g.adj_loaded, g.adj_loads = s.sem("adj_loaded"), 0
        g.x = s.sb("x", [P, NB, D])
        g.xn = s.sb("xn", [P, NB, D])
        g.xn_t = s.sb("xn_t", [P, KD, NP])
        g.ident = s.sb("ident", [P, P])
        g.eps = s.sb("eps", [P, 1])
        g.one = s.sb("one", [P, 1])
        g.ramp = s.sb("ramp", [P, NB, 8])
        g.mask_dram = nc.dram_tensor("expert_masks", [8, NT], F32, kind="Internal").ap()
        stage_load(nc, g, a["x"])
        blocks = [lambda: gat_layers(nc, g, a["L0_gnn_W_stack"]),
                  lambda: two_level_experts(nc, g, a),
                  lambda: masked_attention(nc, g, a["L1_gnn_W"], a["L1_gnn_U"], a["adj"]),
                  lambda: shared_and_routed(nc, g, a),
                  lambda: aggregate_only(nc, g, a),
                  lambda: transformer_experts(nc, g, a),
                  lambda: hyperbolic(nc, g, a),
                  lambda: normalised_experts(nc, g, a)]
        for i in range(start, stop):
            stage_clear(nc)
            stage_norm(nc, g, f"ln{i}", g.x, g.xn, g.xn_t)
            if i % 2 == 0:
                with ExitStack() as inner:
                    g.adj_t = Pool(nc, inner, f"g{i}").sb("adj_t", [P, NB, NP], BF16)
                    stage_adjacency(nc, g, f"adj{i}", a["adj_t"])
                    blocks[i]()
            else:
                blocks[i]()
        stage_store(nc, g, out)


def columns(b):
    return np.ascontiguousarray(b.reshape(-1, P).T)


def lay_out(inputs):
    a = {name: np.ascontiguousarray(np.asarray(v)) for name, v in inputs.items()}
    x, adj = a.pop("x"), a.pop("adj")
    a["x"] = np.zeros((NP, D), x.dtype)
    a["x"][:N] = x
    a["adj"] = np.zeros((NP, N), adj.dtype)
    a["adj"][:N] = adj
    a["adj_t"] = np.zeros((NP, NP), adj.dtype)
    a["adj_t"][:N, :N] = adj.T
    a["L0_ffn_b1_0"], a["L0_ffn_b1_1"], a["L3_ffn_b1"] = (columns(a[k]) for k in ("L0_ffn_b1_0", "L0_ffn_b1_1", "L3_ffn_b1"))
    a["L1_ffn_gates"] = np.concatenate([a["L1_ffn_expert_gate_w"], a.pop("L1_ffn_group_gate_w")]).T.copy()
    a["L1_ffn_gate_bias"] = np.concatenate([a.pop("L1_ffn_expert_bias"), a.pop("L1_ffn_group_bias")])
    a["L1_ffn_out_bias"] = np.concatenate([a.pop("L1_ffn_expert_out_bias"), a.pop("L1_ffn_shared_out_b")[None]])
    a["L1_ffn_affine"] = np.concatenate([columns(a.pop("L1_ffn_ln_scale")), columns(a.pop("L1_ffn_ln_bias"))], 1)
    for k in ("L1_ffn_shared_in_w", "L1_ffn_expert_in_w", "L1_ffn_shared_out_w"):
        a[k] = a[k].T.copy()
    a["L1_ffn_expert_out_weight"] = a["L1_ffn_expert_out_weight"].transpose(2, 0, 1).reshape(HID, -1).copy()
    for k in ("L2_ffn_Wqkv", "L2_ffn_Wo", "L2_ffn_W1", "L2_ffn_W2"):
        a[k] = a[k].transpose(0, 2, 1).copy()
    a["L2_ffn_gate_Wk"] = a["L2_ffn_gate_Wk"].T.copy()
    a["L2_ffn_expert_queries"] = a["L2_ffn_expert_queries"].T.copy()
    a["L2_ffn_gate_bk"] = columns(a["L2_ffn_gate_bk"])
    bqkv, g1, be1 = a.pop("L2_ffn_bqkv"), a["L2_ffn_g1"], a.pop("L2_ffn_be1")
    per_feature = np.concatenate([bqkv[:, :2 * D], a.pop("L2_ffn_bf1"), g1, be1], 1)
    a["L2_ffn_cols"] = columns(per_feature).reshape(P, len(g1), -1)
    a["L2_ffn_bv"] = bqkv[:, 2 * D:].copy()
    a["L2_ffn_rows"] = np.stack([a.pop(f"L2_ffn_{k}") for k in ("bo", "bf2", "g2")] + [be1, a.pop("L2_ffn_g1")], 1)
    return a



def kernel(**inputs):
    import concourse.bacc as bacc
    from concourse.bass_utils import run_bass_kernel_spmd

    nc = bacc.Bacc("TRN2", target_bir_lowering=False, num_devices=1)
    arrays, args = {}, {}
    for name, array in lay_out(inputs).items():
        arrays[f"in_{name}"] = array
        args[name] = nc.dram_tensor(f"in_{name}", array.shape, mybir.dt.from_np(array.dtype), kind="ExternalInput").ap()
    out = nc.dram_tensor("out_x", (N, D), F32, kind="ExternalOutput").ap()
    program(nc, args, out)
    result = run_bass_kernel_spmd(nc, [arrays], core_ids=[0])
    return result.results[0]["out_x"]
```

```python
from contextlib import ExitStack

import numpy as np

import concourse.bass as bass
from concourse import mybir

F32 = mybir.dt.float32
F32R = mybir.dt.float32r
BF16 = mybir.dt.bfloat16
ALU = mybir.AluOpType
ACT = mybir.ActivationFunctionType
AX_X = mybir.AxisListType.X

P = 128
N = 1354
D = 256
KD = D // P
NB = -(-N // P)
NP = NB * P
CH = 3
CW = -(-N // CH)
NT = CH * CW
TG = [(0, 4), (4, 4), (8, 3)]
KCH = [(0, 512), (512, 512), (1024, N - 1024)]
BANK = 512
LN_EPS = 1e-5
BIG = 1e30
FF = 1024
FT = FF // P
LOG2_HALF_ULP = 1.1920929e-07


class Pool:

    def __init__(self, nc, ctx, tag):
        self.nc, self.ctx, self.tag = nc, ctx, tag

    def sb(self, name, shape, dt=F32):
        return self.ctx.enter_context(self.nc.sbuf_tensor(f"{self.tag}_{name}", shape, dt))

    def ps(self, name, shape, dt=F32):
        return self.ctx.enter_context(self.nc.psum_tensor(f"{self.tag}_{name}", shape, dt))

    def sem(self, name):
        return self.ctx.enter_context(self.nc.semaphore(f"{self.tag}_{name}"))


def slab(nc, s, name, width):
    at = -(-nc.sbuf_base // 32) * 32
    s.sb(name, [P, width])
    assert nc.sbuf_base == at + 4 * width, (nc.sbuf_base, at, width)
    return at


def whole_and_low(nc, s, name, shape):
    at = slab(nc, s, name, shape[1] * shape[2])
    return [nc.alloc_sbuf_tensor_at(f"{s.tag}_{name}_{kind}", shape, dt, offset=at) for kind, dt in
            (("whole", F32), ("low", F32R))]


def chain(eng, sem, count=0):
    n = [count]

    def link(instruction):
        n[0] += 1
        instruction.then_inc(sem, 1)
        eng.wait_ge(sem, n[0])
    return link


def split_products(nc, out, stationary, moving, first, last):
    for n, (i, j) in enumerate(((0, 0), (1, 0), (0, 1))):
        ins = nc.tensor.matmul(out, stationary[i], moving[j], start=first and n == 0, stop=last and n == 2)
    return ins


def over(col, width):
    return col.unsqueeze(2).to_broadcast([P, NB, width])



def stage_load(nc, g, x):
    with ExitStack() as ctx:
        s = Pool(nc, ctx, "load")
        x_loaded, zeroed, made = s.sem("x_loaded"), s.sem("zeroed"), s.sem("made")
        block = ctx.enter_context(nc.Block())

        @block.sync
        def _(sync):
            sync.dma_start(g.x[:], x.rearrange("(b p) d -> p b d", p=P)).then_inc(x_loaded, 16)
            sync.wait_ge(x_loaded, 16)

        @block.gpsimd
        def _(pool):
            nc.gpsimd.memset(g.ident[:], 0.0).then_inc(zeroed, 1)
            pool.wait_ge(zeroed, 1)
            nc.gpsimd.affine_select(out=g.ident[:], in_=g.ident[:], compare_op=ALU.not_equal, fill=1.0, base=0,
                                    pattern=[[-1, P]], channel_multiplier=1).then_inc(made, 1)
            nc.gpsimd.memset(g.eps[:], LN_EPS).then_inc(made, 1)
            nc.gpsimd.memset(g.one[:], 1.0).then_inc(made, 1)
            for e in range(8):
                nc.gpsimd.memset(g.ramp[:, :, e], float(8 - e)).then_inc(made, 1)
            pool.wait_ge(made, 11)


def load_adjacency(g, pool):
    g.adj_loads += 1
    pool.dma_start(g.adj_t[:], g.adj_t_dram.rearrange("(b p) q -> p b q", p=P)).then_inc(g.adj_loaded, 16)



def stage_norm(nc, g, tag, src, dst, dst_t, gain=None, shift=None, adjacency=False):
    with ExitStack() as ctx:
        s = Pool(nc, ctx, tag)
        stats = s.sb("stats", [P, NB, 6])
        mean_var = s.sb("mean_var", [P, NB, 2])
        std = s.sb("std", [P, NB])
        rstd = s.sb("rstd", [P, NB])
        turned = [s.ps(f"turned{i}", [P, BANK]) for i in range(4)]
        v_step, std_done, normed = s.sem("v_step"), s.sem("std_done"), s.sem("normed")
        turned_full, turned_read = s.sem("turned_full"), s.sem("turned_read")
        normalise = dst is not None
        out = dst if normalise else src
        block = ctx.enter_context(nc.Block())

        if adjacency:
            @block.gpsimd
            def _(pool):
                load_adjacency(g, pool)

        if normalise:
            @block.vector
            def _(dve):
                for b in range(NB):
                    nc.vector.bn_stats(stats[:, b, :], src[:, b, :]).then_inc(v_step, 1)
                dve.wait_ge(v_step, NB)
                for b in range(NB):
                    nc.vector.bn_aggr(mean_var[:, b, :], stats[:, b, :]).then_inc(v_step, 1)
                dve.wait_ge(std_done, 1)
                nc.vector.reciprocal(rstd[:], std[:]).then_inc(v_step, 1)
                dve.wait_ge(v_step, 2 * NB + 1)
                for b in range(NB):
                    nc.vector.tensor_scalar(dst[:, b, :], src[:, b, :], mean_var[:, b, 0:1], rstd[:, b:b + 1],
                                            ALU.subtract, ALU.mult).then_inc(normed, 1)

        @block.tensor
        def _(pe):
            t = 0
            for b0, nb in TG:
                for k in range(KD):
                    if t >= 4:
                        pe.wait_ge(turned_read, t - 3)
                    for b in range(b0, b0 + nb):
                        if normalise:
                            pe.wait_ge(normed, b + 1)
                        last = nc.tensor.transpose(turned[t % 4][:, (b - b0) * P:(b - b0 + 1) * P],
                                                   out[:, b, k * P:(k + 1) * P], g.ident[:])
                    last.then_inc(turned_full, 1)
                    t += 1

        @block.scalar
        def _(act):
            if normalise:
                act.wait_ge(v_step, 2 * NB)
                nc.scalar.activation(std[:], mean_var[:, :, 1], ACT.Sqrt, bias=g.eps[:]).then_inc(std_done, 1)
            t = 0
            for b0, nb in TG:
                for k in range(KD):
                    act.wait_ge(turned_full, t + 1)
                    into = dst_t[:, k, b0 * P:(b0 + nb) * P]
                    if gain is None:
                        nc.scalar.activation(into, turned[t % 4][:, 0:nb * P], ACT.Copy).then_inc(turned_read, 1)
                    else:
                        nc.scalar.activation(into, turned[t % 4][:, 0:nb * P], ACT.Identity, scale=gain[:, k:k + 1],
                                             bias=shift[:, k:k + 1]).then_inc(turned_read, 1)
                    t += 1



def stage_project(nc, g, tag, src_t, w_dram, feature_major, token_major, adjacency=False):
    cols = w_dram.shape[1]
    tiles = [(c0 + j * P, target, j) for c0, target in feature_major for j in range(KD)]
    with ExitStack() as ctx:
        s = Pool(nc, ctx, tag)
        w = s.sb("w", [P, KD, cols])
        wide = [s.ps(f"wide{i}", [P, CH, BANK]) for i in range(2)]
        row = [s.ps(f"row{i}", [P, BANK]) for i in range(2)]
        w_loaded, pads_zero = s.sem("w_loaded"), s.sem("pads_zero")
        wide_full, row_full = s.sem("wide_full"), s.sem("row_full")
        wide_read_act, wide_read_dve = s.sem("wide_read_act"), s.sem("wide_read_dve")
        row_read_act, row_read_dve = s.sem("row_read_act"), s.sem("row_read_dve")
        block = ctx.enter_context(nc.Block())

        @block.sync
        def _(sync):
            sync.dma_start(w[:], w_dram.rearrange("(k p) o -> p k o", p=P)).then_inc(w_loaded, 16)

        @block.gpsimd
        def _(pool):
            if adjacency:
                load_adjacency(g, pool)
            for _, target in feature_major:
                nc.gpsimd.memset(target[:, :, NT:NP], 0.0).then_inc(pads_zero, 1)
            pool.wait_ge(pads_zero, len(feature_major))

        @block.tensor
        def _(pe):
            pe.wait_ge(w_loaded, 16)
            for t, (c0, _, _) in enumerate(tiles):
                if t >= 2:
                    pe.wait_ge([wide_read_act, wide_read_dve][t % 2], t // 2)
                for c in range(CH):
                    for k in range(KD):
                        last = nc.tensor.matmul(wide[t % 2][:, c, 0:CW], w[:, k, c0:c0 + P],
                                                src_t[:, k, c * CW:(c + 1) * CW], start=(k == 0), stop=(k == KD - 1))
                last.then_inc(wide_full, 1)
            if token_major:
                c0 = token_major[0]
                for b in range(NB):
                    if b >= 2:
                        pe.wait_ge([row_read_act, row_read_dve][b % 2], b // 2)
                    for k in range(KD):
                        last = nc.tensor.matmul(row[b % 2][:, 0:D], src_t[:, k, b * P:(b + 1) * P],
                                                w[:, k, c0:c0 + D], start=(k == 0), stop=(k == KD - 1))
                    last.then_inc(row_full, 1)

        def drain(eng, copy, parity, wide_read, row_read):
            for t, (_, target, j) in enumerate(tiles):
                if t % 2 == parity:
                    eng.wait_ge(wide_full, t + 1)
                    copy(target[:, j, 0:NT].rearrange("p (c n) -> p c n", c=CH), wide[t % 2][:, :, 0:CW])\
                        .then_inc(wide_read, 1)
            if token_major:
                for b in range(parity, NB, 2):
                    eng.wait_ge(row_full, b + 1)
                    copy(token_major[1][:, b, :], row[b % 2][:, 0:D]).then_inc(row_read, 1)

        @block.scalar
        def _(act):
            drain(act, lambda o, i: nc.scalar.activation(o, i, ACT.Copy), 0, wide_read_act, row_read_act)

        @block.vector
        def _(dve):
            drain(dve, nc.vector.tensor_copy, 1, wide_read_dve, row_read_dve)



def stage_graph_attention(nc, g, tag, q_t, k_t, v, finish, masked_rows=None):
    with ExitStack() as ctx:
        s = Pool(nc, ctx, tag)
        e = [s.sb(f"e{i}", [P, NP]) for i in range(2)]
        e_t = s.sb("e_t", [P, NB, P])
        e_hi, e_lo = s.sb("e_hi", [P, NB, P], F32R), s.sb("e_lo", [P, NB, P], F32R)
        q_hi, k_hi, v_hi = s.sb("q_hi", [P, KD, NP], F32R), s.sb("k_hi", [P, KD, NP], F32R), s.sb("v_hi", [P, NB, D], F32R)
        every = slice(None)
        pieces = [[tile[every, i, j] for tile in (*two, high)]
                  for two, high, i, j in ((q_t, q_hi, every, slice(0, P)), (k_t, k_hi, 0, every), (k_t, k_hi, 1, every),
                                          (q_t, q_hi, every, slice(P, NP)), (v, v_hi, slice(0, 6), every),
                                          (v, v_hi, slice(6, NB), every))]
        neg_max = s.sb("neg_max", [P, NB])
        row_sum = s.sb("row_sum", [P, NB])
        inv = s.sb("inv", [P, NB])
        scratch = s.sb("scratch", [P, D])
        scores = [s.ps(f"scores{i}", [P, CH * BANK]) for i in range(2)]
        turned = s.ps("turned", [P, BANK])
        out = s.ps("out", [P, BANK])
        scores_full, turned_full, out_full = s.sem("scores_full"), s.sem("turned_full"), s.sem("out_full")
        max_done, exp_done, e_pad = s.sem("max_done"), s.sem("exp_done"), s.sem("e_pad")
        e_t_done, finished, v_step = s.sem("e_t_done"), s.sem("finished"), s.sem("v_step")
        part_hi, part_lo, e_hi_done, e_lo_done = (s.sem(n) for n in ("part_hi", "part_lo", "e_hi_done", "e_lo_done"))
        if masked_rows is not None:
            rows = [s.sb(f"rows{i}", [P, N]) for i in range(2)]
            kept = [s.sb(f"kept{i}", [P, N]) for i in range(2)]
            rows_loaded, bias_done = [s.sem(f"rows_loaded{i}") for i in range(2)], s.sem("bias_done")
            pool_step, self_added = s.sem("pool_step"), s.sem("self_added")
        block = ctx.enter_context(nc.Block())

        if masked_rows is not None:
            @block.sync
            def _(sync):
                for b in range(NB):
                    if b >= 2:
                        sync.wait_ge(max_done, b - 1)
                    sync.dma_start(rows[b % 2][:], masked_rows[b * P:(b + 1) * P, 0:N]).then_inc(rows_loaded[b % 2], 16)

        @block.gpsimd
        def _(pool):
            for i in range(2):
                nc.gpsimd.memset(e[i][:, N:NP], 0.0).then_inc(e_pad, 1)
            if masked_rows is not None:
                pool.wait_ge(g.adj_loaded, 16 * g.adj_loads)
                link = chain(pool, pool_step)
                for b in range(NB):
                    own = g.adj_t[:, b, b * P:(b + 1) * P]
                    nc.gpsimd.tensor_tensor(own, own, g.ident[:], ALU.add).then_inc(self_added, 1)
                for b in range(NB):
                    pool.wait_ge(rows_loaded[b % 2], 16 * (b // 2 + 1))
                    r = rows[b % 2]
                    nc_last = nc.gpsimd.tensor_scalar(r[:], r[:], -1.0, BIG, ALU.add, ALU.mult)
                    link(nc_last)
                    w = min(P, N - b * P)
                    own = r[:, b * P:b * P + w]
                    nc.gpsimd.affine_select(out=own, in_=own, compare_op=ALU.not_equal, fill=0.0, base=0,
                                            pattern=[[-1, w]], channel_multiplier=1).then_inc(bias_done, 1)
                pool.wait_ge(e_t_done, CH * NB)
                for b in range(NB):
                    own = g.adj_t[:, b, b * P:(b + 1) * P]
                    nc.gpsimd.tensor_tensor(own, own, g.ident[:], ALU.subtract).then_inc(self_added, 1)
                pool.wait_ge(self_added, 2 * NB)
            pool.wait_ge(e_pad, 2)

        @block.tensor
        def _(pe):
            def score(b, c):
                c = (c + CH - 1) % CH
                if b < 2 and c == CH - 1:
                    pe.wait_ge(part_lo, 3 + b)
                if c == CH - 1 and b >= 2:
                    pe.wait_ge(max_done if masked_rows is not None else exp_done, b - 1)
                k0, w = KCH[c]
                for k in range(KD):
                    last = split_products(nc, scores[b % 2][:, k0:k0 + w],
                                          [part[:, k, b * P:(b + 1) * P] for part in (q_hi, q_t[1])],
                                          [part[:, k, k0:k0 + w] for part in (k_hi, k_t[1])], k == 0, k == KD - 1)
                if c == CH - 2:
                    last.then_inc(scores_full, 1)

            def turn(b, c):
                if c == 0:
                    pe.wait_ge(exp_done, b + 1)
                    pe.wait_ge(e_pad, 2)
                if b + c:
                    pe.wait_ge(e_t_done, CH * b + c)
                t0, n = TG[c]
                for t in range(t0, t0 + n):
                    last = nc.tensor.transpose(turned[:, (t - t0) * P:(t - t0 + 1) * P],
                                               e[b % 2][:, t * P:(t + 1) * P], g.ident[:])
                last.then_inc(turned_full, 1)

            def mix(b):
                if b:
                    pe.wait_ge(finished, b)
                else:
                    pe.wait_ge(part_lo, len(pieces))
                for c, (t0, n) in enumerate(TG):
                    pe.wait_ge(e_lo_done, CH * b + c + 1)
                    for t in range(t0, t0 + n):
                        last = split_products(nc, out[:, 0:D], (e_hi[:, t, :], e_lo[:, t, :]),
                                              (v_hi[:, t, :], v[1][:, t, :]), t == 0, t == NB - 1)
                last.then_inc(out_full, 1)

            for c in range(CH):
                score(0, c)
            for b in range(NB):
                for c in range(CH):
                    turn(b, c)
                    if b + 1 < NB:
                        score(b + 1, c)
                mix(b)

        @block.scalar
        def _(act):
            for whole, _, high in pieces:
                nc.scalar.activation(high, whole, ACT.Copy).then_inc(part_hi, 1)

            def exp(b):
                act.wait_ge(max_done, b + 1)
                if b >= 2:
                    act.wait_ge(turned_full, CH * (b - 1))
                seen = scores[b % 2][:, 0:N] if masked_rows is None else kept[b % 2][:]
                nc.scalar.activation(e[b % 2][:, 0:N], seen, ACT.Exp, bias=neg_max[:, b:b + 1],
                                     accum_out=row_sum[:, b:b + 1]).then_inc(exp_done, 1)

            exp(0)
            for b in range(NB):
                for c, (t0, n) in enumerate(TG):
                    act.wait_ge(e_t_done, CH * b + c + 1)
                    if b:
                        act.wait_ge(out_full, b)
                    nc.scalar.activation(e_hi[:, t0:t0 + n, :], e_t[:, t0:t0 + n, :], ACT.Copy).then_inc(e_hi_done, 1)
                if b + 1 < NB:
                    exp(b + 1)

        @block.vector
        def _(dve):
            link = chain(dve, v_step)

            def row_max(b):
                dve.wait_ge(scores_full, b + 1)
                if masked_rows is None:
                    nc.vector.tensor_reduce(neg_max[:, b:b + 1], scores[b % 2][:, 0:N], AX_X, ALU.max, negate=True)\
                        .then_inc(max_done, 1)
                    return
                dve.wait_ge(bias_done, b + 1)
                if b >= 2:
                    dve.wait_ge(exp_done, b - 1)
                link(nc.vector.tensor_tensor(kept[b % 2][:], scores[b % 2][:, 0:N], rows[b % 2][:], ALU.add))
                nc.vector.tensor_reduce(neg_max[:, b:b + 1], kept[b % 2][:], AX_X, ALU.max, negate=True)\
                    .then_inc(max_done, 1)

            def low(i):
                whole, rest, high = pieces[i]
                dve.wait_ge(part_hi, i + 1)
                nc.vector.tensor_tensor(rest, whole, high, ALU.subtract).then_inc(part_lo, 1)

            def e_low(b, c):
                t0, n = TG[c]
                dve.wait_ge(e_hi_done, CH * b + c + 1)
                nc.vector.tensor_tensor(e_lo[:, t0:t0 + n, :], e_t[:, t0:t0 + n, :], e_hi[:, t0:t0 + n, :],
                                        ALU.subtract).then_inc(e_lo_done, 1)

            for i in range(4):
                low(i)
            row_max(0)
            for i in range(4, len(pieces)):
                low(i)
            dve.wait_ge(g.adj_loaded, 16 * g.adj_loads)
            if masked_rows is not None:
                dve.wait_ge(self_added, NB)
            for b in range(NB):
                for c, (t0, n) in enumerate(TG):
                    dve.wait_ge(turned_full, CH * b + c + 1)
                    if b:
                        dve.wait_ge(e_lo_done, CH * b - CH + c + 1)
                    nc.vector.tensor_tensor(e_t[:, t0:t0 + n, :],
                                            turned[:, 0:n * P].rearrange("p (t q) -> p t q", q=P),
                                            g.adj_t[:, t0:t0 + n, b * P:(b + 1) * P], ALU.mult).then_inc(e_t_done, 1)
                    if c:
                        e_low(b, c - 1)
                e_low(b, CH - 1)
                if b + 1 < NB:
                    row_max(b + 1)
                link(nc.vector.reciprocal(inv[:, b:b + 1], row_sum[:, b:b + 1]))
                dve.wait_ge(out_full, b + 1)
                finish(link, b, out[:, 0:D], inv[:, b:b + 1], scratch).then_inc(finished, 1)
            dve.wait_ge(finished, NB)


def gat_layers(nc, g, w_stack):
    layers = w_stack.shape[0]
    for layer in range(layers):
        with ExitStack() as ctx:
            s = Pool(nc, ctx, f"gat{layer}")
            wh_t, ws_t = whole_and_low(nc, s, "wh_t", [P, KD, NP]), whole_and_low(nc, s, "ws_t", [P, KD, NP])
            wh = whole_and_low(nc, s, "wh", [P, NB, D])
            stage_project(nc, g, f"gat{layer}p", g.xn_t, w_stack[layer], [(0, wh_t[0]), (D, ws_t[0])], (0, wh[0]),
                          adjacency=layer == 0)
            last_layer = layer == layers - 1

            def finish(link, b, out, inv, scratch):
                link(nc.vector.scalar_tensor_tensor(out=scratch[:], in0=out, scalar=inv, in1=g.xn[:, b, :],
                                                    op0=ALU.mult, op1=ALU.add))
                leaky = nc.vector.scalar_tensor_tensor(out=g.xn[:, b, :], in0=scratch[:], scalar=0.01, in1=scratch[:],
                                                       op0=ALU.mult, op1=ALU.max)
                if not last_layer:
                    return leaky
                link(leaky)
                return nc.vector.tensor_tensor(g.x[:, b, :], g.x[:, b, :], g.xn[:, b, :], ALU.add)

            stage_graph_attention(nc, g, f"gat{layer}a", wh_t, ws_t, wh, finish)
        if not last_layer:
            stage_norm(nc, g, f"gat{layer}t", g.xn, None, g.xn_t)


def masked_attention(nc, g, w, u, adj):
    with ExitStack() as ctx:
        s = Pool(nc, ctx, "nbr")
        h_t, hu_t = whole_and_low(nc, s, "h_t", [P, KD, NP]), whole_and_low(nc, s, "hu_t", [P, KD, NP])
        h = whole_and_low(nc, s, "h", [P, NB, D])
        stage_project(nc, g, "nbrh", g.xn_t, w, [(0, h_t[0])], (0, h[0]), adjacency=True)
        stage_project(nc, g, "nbru", h_t[0], u, [(0, hu_t[0])], None)

        def finish(link, b, out, inv, scratch):
            return nc.vector.scalar_tensor_tensor(out=g.x[:, b, :], in0=out, scalar=inv, in1=g.x[:, b, :],
                                                  op0=ALU.mult, op1=ALU.add)

        stage_graph_attention(nc, g, "nbra", hu_t, h_t, h, finish, masked_rows=adj)



def top_two(link, nc, g, values, mask, work, work2, col, width, below):
    ramp = g.ramp[:, :, 0:width]
    left = values
    for turn in range(2):
        link(nc.vector.tensor_reduce(col, left, AX_X, ALU.max))
        link(nc.vector.tensor_tensor(work, left, over(col, width), ALU.is_equal))
        link(nc.vector.tensor_tensor(work, work, ramp, ALU.mult))
        link(nc.vector.tensor_reduce(col, work, AX_X, ALU.max))
        link(nc.vector.tensor_tensor(work, work, over(col, width), ALU.is_equal))
        if turn == 0:
            link(nc.vector.tensor_copy(mask, work))
            link(nc.vector.tensor_scalar(work2, work, -below, None, ALU.mult))
            link(nc.vector.tensor_tensor(work2, work2, values, ALU.add))
            left = work2
        else:
            link(nc.vector.tensor_tensor(mask, mask, work, ALU.add))


def softmax_to(link, nc, dve, values, probs, col, width, exp_asked, exp_done, n):
    link(nc.vector.tensor_reduce(col, values, AX_X, ALU.max))
    nc.vector.tensor_tensor(probs, values, over(col, width), ALU.subtract).then_inc(exp_asked, 1)
    dve.wait_ge(exp_done, n)


def divide_by_sum(link, nc, values, col, width, eps=None):
    link(nc.vector.tensor_reduce(col, values, AX_X, ALU.add))
    if eps is not None:
        link(nc.vector.tensor_scalar(col, col, eps, None, ALU.add))
    link(nc.vector.reciprocal(col, col))
    link(nc.vector.tensor_tensor(values, values, over(col, width), ALU.mult))


def stage_route(nc, g, tag, src_t, gate, width, rule, weights, mask, bias=None, keys=None):
    with ExitStack() as ctx:
        s = Pool(nc, ctx, tag)
        w = s.sb("w", [P, KD, width])
        logits = s.sb("logits", [P, NB, width])
        work = [s.sb(f"work{i}", [P, NB, 8]) for i in range(4)]
        cols = [s.sb(f"col{i}", [P, NB]) for i in range(3)]
        ps = s.ps("ps", [P, NB, width])
        w_loaded, full, v_step = s.sem("w_loaded"), s.sem("full"), s.sem("v_step")
        exp_asked, exp_done = s.sem("exp_asked"), s.sem("exp_done")
        if bias is not None:
            bias_all = s.sb("bias_all", [P, width])
        if keys is not None:
            wk = s.sb("wk", [P, KD, D])
            bk = s.sb("bk", [P, KD])
            keys_t = s.sb("keys_t", [P, KD, NP])
            wide = [s.ps(f"wide{i}", [P, CH, BANK]) for i in range(2)]
            keys_full, keys_done, pads = s.sem("keys_full"), s.sem("keys_done"), s.sem("pads")
        weights_view = weights[:] if rule != "grouped" else work[3][:, :, 0:4]
        loads = 1 + (bias is not None) + 2 * (keys is not None)
        block = ctx.enter_context(nc.Block())

        @block.sync
        def _(sync):
            sync.dma_start(w[:], gate.rearrange("(k p) e -> p k e", p=P)).then_inc(w_loaded, 16)
            if bias is not None:
                sync.dma_start(bias_all[:], bias.partition_broadcast(P)).then_inc(w_loaded, 16)
            if keys is not None:
                sync.dma_start(wk[:], keys[0].rearrange("(k p) o -> p k o", p=P)).then_inc(w_loaded, 16)
                sync.dma_start(bk[:], keys[1]).then_inc(w_loaded, 16)

        if keys is not None:
            @block.gpsimd
            def _(pool):
                nc.gpsimd.memset(keys_t[:, :, NT:NP], 0.0).then_inc(pads, 1)

        @block.tensor
        def _(pe):
            pe.wait_ge(w_loaded, 16 * loads)
            seen = src_t
            if keys is not None:
                for j in range(KD):
                    for c in range(CH):
                        for k in range(KD):
                            last = nc.tensor.matmul(wide[j][:, c, 0:CW], wk[:, k, j * P:(j + 1) * P],
                                                    src_t[:, k, c * CW:(c + 1) * CW], start=(k == 0), stop=(k == KD - 1))
                    last.then_inc(keys_full, 1)
                pe.wait_ge(keys_done, KD)
                pe.wait_ge(pads, 1)
                seen = keys_t
            for b in range(NB):
                for k in range(KD):
                    last = nc.tensor.matmul(ps[:, b, :], seen[:, k, b * P:(b + 1) * P], w[:, k, :],
                                            start=(k == 0), stop=(k == KD - 1))
            last.then_inc(full, 1)

        @block.scalar
        def _(act):
            if keys is not None:
                act.wait_ge(w_loaded, 16 * loads)
                for j in range(KD):
                    act.wait_ge(keys_full, j + 1)
                    nc.scalar.activation(keys_t[:, j, 0:NT].rearrange("p (c n) -> p c n", c=CH), wide[j][:, :, 0:CW],
                                         ACT.Identity, bias=bk[:, j:j + 1]).then_inc(keys_done, 1)
            act.wait_ge(exp_asked, 1)
            nc.scalar.activation(weights_view, weights_view, ACT.Exp).then_inc(exp_done, 1)

        @block.vector
        def _(dve):
            link = chain(dve, v_step)
            dve.wait_ge(full, 1)
            c0, c1, c2 = (c[:] for c in cols)
            if rule == "grouped":
                dve.wait_ge(w_loaded, 16 * loads)
                link(nc.vector.tensor_tensor(logits[:], ps[:], bias_all[:].unsqueeze(1).to_broadcast([P, NB, width]),
                                             ALU.add))
                first, second = c1, c2
                link(nc.vector.tensor_tensor(first, logits[:, :, 8], logits[:, :, 9], ALU.is_ge))
                link(nc.vector.tensor_scalar(second, first, -1.0, 1.0, ALU.mult, ALU.add))
                chosen, other, exps = work[0][:, :, 0:4], work[1][:, :, 0:4], work[3][:, :, 0:4]
                link(nc.vector.tensor_tensor(chosen, logits[:, :, 0:4], over(first, 4), ALU.mult))
                link(nc.vector.tensor_tensor(other, logits[:, :, 4:8], over(second, 4), ALU.mult))
                link(nc.vector.tensor_tensor(chosen, chosen, other, ALU.add))
                softmax_to(link, nc, dve, chosen, exps, c0, 4, exp_asked, exp_done, 1)
                divide_by_sum(link, nc, exps, c0, 4)
                picked = work[2][:, :, 4:8]
                top_two(link, nc, g, exps, picked, work[0][:, :, 0:4], work[1][:, :, 0:4], c0, 4, 2.0)
                link(nc.vector.tensor_tensor(exps, exps, picked, ALU.mult))
                divide_by_sum(link, nc, exps, c0, 4, 1e-8)
                for i, group in enumerate((first, second)):
                    link(nc.vector.tensor_tensor(weights[:, :, 4 * i:4 * i + 4], exps, over(group, 4), ALU.mult))
                    link(nc.vector.tensor_tensor(mask[:, :, 4 * i:4 * i + 4], picked, over(group, 4), ALU.mult))
                return
            scale = D ** -0.5 if rule == "keys" else 1.0
            link(nc.vector.tensor_scalar(logits[:], ps[:], scale, None, ALU.mult))
            a, b2 = work[0][:, :, 0:width], work[1][:, :, 0:width]
            softmax_to(link, nc, dve, logits[:], weights[:], c0, width, exp_asked, exp_done, 1)
            if rule == "logits":
                top_two(link, nc, g, logits[:], mask[:], a, b2, c0, width, BIG)
                link(nc.vector.tensor_tensor(weights[:], weights[:], mask[:], ALU.mult))
                divide_by_sum(link, nc, weights[:], c0, width)
                return
            divide_by_sum(link, nc, weights[:], c0, width)
            top_two(link, nc, g, weights[:], mask[:], a, b2, c0, width, 2.0)
            if rule == "keys":
                link(nc.vector.tensor_tensor(weights[:], weights[:], mask[:], ALU.mult))
                divide_by_sum(link, nc, weights[:], c0, width, 1e-9)


def stage_spread(nc, g, tag, coefficients, width, table_dram, acc, add, mask=None, mask_dram=None):
    with ExitStack() as ctx:
        s = Pool(nc, ctx, tag)
        table = s.sb("table", [width, D])
        turned_sb = s.sb("turned_sb", [width, NP])
        mask_sb = s.sb("mask_sb", [width, NP])
        turned = s.ps("turned", [width, CH, BANK])
        mask_ps = s.ps("mask_ps", [width, CH, BANK])
        row = [s.ps(f"row{i}", [P, BANK]) for i in range(2)]
        loaded, turned_full, turned_read = s.sem("loaded"), s.sem("turned_full"), s.sem("turned_read")
        row_full, row_read, stored = s.sem("row_full"), s.sem("row_read"), s.sem("stored")
        block = ctx.enter_context(nc.Block())

        @block.sync
        def _(sync):
            sync.dma_start(table[:], table_dram).then_inc(loaded, 16)
            if mask is not None:
                sync.wait_ge(turned_read, 2 * CH)
                sync.dma_start(mask_dram[0:width, :], mask_sb[:, 0:NT]).then_inc(stored, 16)
                sync.wait_ge(stored, 16)

        @block.tensor
        def _(pe):
            for src, into in ((coefficients, turned), (mask, mask_ps)):
                if src is None:
                    continue
                for c, (b0, n) in enumerate(TG):
                    for b in range(b0, b0 + n):
                        last = nc.tensor.transpose(into[:, c, (b - b0) * P:(b - b0 + 1) * P], src[:, b, :], g.ident[:])
                    last.then_inc(turned_full, 1)
            pe.wait_ge(turned_read, CH)
            pe.wait_ge(loaded, 16)
            for b in range(NB):
                if b >= 2:
                    pe.wait_ge(row_read, b - 1)
                nc.tensor.matmul(row[b % 2][:, 0:D], turned_sb[:, b * P:(b + 1) * P], table[:], start=True, stop=True)\
                    .then_inc(row_full, 1)

        @block.scalar
        def _(act):
            n_read = 0
            for src, into, sb in ((coefficients, turned, turned_sb), (mask, mask_ps, mask_sb)):
                if src is None:
                    continue
                for c, (b0, n) in enumerate(TG):
                    n_read += 1
                    act.wait_ge(turned_full, n_read)
                    nc.scalar.activation(sb[:, b0 * P:(b0 + n) * P], into[:, c, 0:n * P], ACT.Copy).then_inc(turned_read, 1)

        @block.vector
        def _(dve):
            for b in range(NB):
                dve.wait_ge(row_full, b + 1)
                if add:
                    nc.vector.tensor_tensor(acc[:, b, :], row[b % 2][:, 0:D], acc[:, b, :], ALU.add).then_inc(row_read, 1)
                else:
                    nc.vector.tensor_copy(acc[:, b, :], row[b % 2][:, 0:D]).then_inc(row_read, 1)



def stage_normalised_experts(nc, g, tag, src_t, w1_dram, b1_dram, w2_dram, b2_dram, gamma_dram, weights, acc):
    experts, _, hidden = w1_dram.shape
    ht = hidden // P
    links = NB + NB + 3
    with ExitStack() as ctx:
        s = Pool(nc, ctx, tag)
        w1, w2 = s.sb("w1", [P, KD, hidden]), s.sb("w2", [P, ht, D])
        b1 = s.sb("b1", [P, experts * ht])
        h = s.sb("h", [P, ht, NP])
        b2, gamma = s.sb("b2", [P, experts, D]), s.sb("gamma", [P, experts, D])
        y = s.sb("y", [P, NB, D])
        z = s.sb("z", [P, NB, D])
        stats, mean_var = s.sb("stats", [P, NB, 6]), s.sb("mean_var", [P, NB, 2])
        std, scale, shift = s.sb("std", [P, NB]), s.sb("scale", [P, NB]), s.sb("shift", [P, NB])
        wide = [s.ps(f"wide{i}", [P, CH, BANK]) for i in range(2)]
        row = [s.ps(f"row{i}", [P, BANK]) for i in range(2)]
        w1_loaded, w2_loaded, b1_loaded, b2_loaded, gamma_loaded = (
            s.sem(n) for n in ("w1_loaded", "w2_loaded", "b1_loaded", "b2_loaded", "gamma_loaded"))
        wide_full, row_full = s.sem("wide_full"), s.sem("row_full")
        wide_read, std_done, z_full, act_seen = (
            s.sem(n) for n in ("wide_read", "std_done", "z_full", "act_seen"))
        row_read, tiles_seen, stats_done, scaled, v_step = (
            s.sem(n) for n in ("row_read", "tiles_seen", "stats_done", "scaled", "v_step"))
        h_pad, z_used, pool_seen = s.sem("h_pad"), s.sem("z_used"), s.sem("pool_seen")
        w1_v = w1_dram.rearrange("e (k p) o -> e p k o", p=P)
        w2_v = w2_dram.rearrange("e (f p) o -> e p f o", p=P)
        block = ctx.enter_context(nc.Block())

        @block.sync
        def _(sync):
            sync.dma_start(w1[:], w1_v[0]).then_inc(w1_loaded, 16)
            sync.dma_start(b1[:], b1_dram).then_inc(b1_loaded, 16)
            sync.dma_start(w2[:], w2_v[0]).then_inc(w2_loaded, 16)
            sync.dma_start(b2[:], b2_dram.partition_broadcast(P)).then_inc(b2_loaded, 16)
            sync.dma_start(gamma[:], gamma_dram.partition_broadcast(P)).then_inc(gamma_loaded, 16)
            with sync.Fori(1, experts) as e:
                sync.wait_ge(wide_full, ht * e)
                sync.dma_start(w1[:], w1_v[e]).then_inc(w1_loaded, 16)
                sync.wait_ge(row_full, NB * e)
                sync.dma_start(w2[:], w2_v[e]).then_inc(w2_loaded, 16)

        @block.gpsimd
        def _(pool):
            nc.gpsimd.memset(h[:, :, NT:NP], 0.0).then_inc(h_pad, 1)
            pool.sem_inc(z_used, 2 * NB)
            pool.wait_ge(gamma_loaded, 16)
            with pool.Fori(0, experts) as e:
                for b in range(NB):
                    z_b = z[:, b, :]
                    pool.wait_ge(z_full, NB * e + (b + 1))
                    pool.sem_inc(pool_seen, 1)
                    nc.gpsimd.tensor_tensor(z_b, z_b, gamma[:, bass.ds(e, 1), :].rearrange("p o d -> p (o d)"), ALU.mult).then_inc(z_used, 1)
                    pool.wait_ge(z_used, 2 * NB * e + (2 * NB + 2 * b + 1))
                    nc.gpsimd.tensor_tensor(acc[:, b, :], acc[:, b, :], z_b, ALU.add).then_inc(z_used, 1)
                    pool.wait_ge(z_used, 2 * NB * e + (2 * NB + 2 * b + 2))

        @block.tensor
        def _(pe):
            pe.wait_ge(h_pad, 1)
            with pe.Fori(0, experts) as e:
                pe.wait_ge(w1_loaded, 16 * e + 16)
                for f in range(ht):
                    pe.wait_ge(wide_read, ht * e + (f + 1))
                    for c in range(CH):
                        for k in range(KD):
                            last = nc.tensor.matmul(wide[f % 2][:, c, 0:CW], w1[:, k, f * P:(f + 1) * P],
                                                    src_t[:, k, c * CW:(c + 1) * CW], start=(k == 0), stop=(k == KD - 1))
                    last.then_inc(wide_full, 1)
                pe.wait_ge(wide_read, ht * e + (ht + 2))
                pe.wait_ge(w2_loaded, 16 * e + 16)
                for b in range(NB):
                    pe.wait_ge(row_read, NB * e + max(b + 1, 2))
                    for f in range(ht):
                        last = nc.tensor.matmul(row[b % 2][:, 0:D], h[:, f, b * P:(b + 1) * P], w2[:, f, :],
                                                start=(f == 0), stop=(f == ht - 1))
                    last.then_inc(row_full, 1)

        @block.scalar
        def _(act):
            def normalise(e):
                act.wait_ge(scaled, e + 1)
                for b in range(NB):
                    act.wait_ge(z_used, 2 * NB * e + (2 * b + 2))
                    nc.scalar.activation(z[:, b, :], y[:, b, :], ACT.Identity, scale=scale[:, b:b + 1],
                                         bias=shift[:, b:b + 1]).then_inc(z_full, 1)

            def body(e, before):
                for f in range(ht):
                    act.wait_ge(wide_full, ht * e + (f + 1))
                    act.sem_inc(act_seen, 1)
                    nc.scalar.activation(h[:, f, 0:NT].rearrange("p (c n) -> p c n", c=CH), wide[f % 2][:, :, 0:CW],
                                         ACT.Relu, bias=b1[:, bass.ds(e * ht + f, 1)]).then_inc(wide_read, 1)
                if before:
                    normalise(e - 1)
                act.wait_ge(stats_done, e + 1)
                nc.scalar.activation(std[:], mean_var[:, :, 1], ACT.Sqrt, bias=g.eps[:]).then_inc(std_done, 1)

            act.sem_inc(wide_read, 2)
            act.wait_ge(b1_loaded, 16)
            body(0, False)
            with act.Fori(1, experts) as e:
                body(e, True)
            normalise(experts - 1)

        @block.vector
        def _(dve):
            def body(e, before):
                for b in range(NB):
                    dve.wait_ge(row_full, NB * e + (b + 1))
                    if before:
                        dve.wait_ge(z_full, NB * e + (b + 1 - NB))
                    nc.vector.tensor_tensor(y[:, b, :], row[b % 2][:, 0:D],
                                            b2[:, e, :] if isinstance(e, int) else
                                            b2[:, bass.ds(e, 1), :].rearrange("p o d -> p (o d)"), ALU.add).then_inc(row_read, 1)
                    dve.wait_ge(row_read, NB * e + (b + 3))
                    nc.vector.bn_stats(stats[:, b, :], y[:, b, :]).then_inc(v_step, 1)
                dve.wait_ge(v_step, links * e + NB)
                dve.sem_inc(tiles_seen, 1)
                for b in range(NB):
                    nc.vector.bn_aggr(mean_var[:, b, :], stats[:, b, :]).then_inc(v_step, 1)
                dve.wait_ge(v_step, links * e + 2 * NB)
                dve.sem_inc(stats_done, 1)
                dve.wait_ge(std_done, e + 1)
                nc.vector.reciprocal(std[:], std[:]).then_inc(v_step, 1)
                dve.wait_ge(v_step, links * e + (2 * NB + 1))
                nc.vector.tensor_tensor(scale[:], std[:], weights[:, :, bass.ds(e, 1)].rearrange("p b o -> p (b o)"),
                                        ALU.mult).then_inc(v_step, 1)
                dve.wait_ge(v_step, links * e + (2 * NB + 2))
                nc.vector.scalar_tensor_tensor(out=shift[:], in0=mean_var[:, :, 0], scalar=-1.0, in1=scale[:],
                                               op0=ALU.mult, op1=ALU.mult).then_inc(v_step, 1)
                dve.wait_ge(v_step, links * e + (2 * NB + 3))
                dve.sem_inc(scaled, 1)

            dve.sem_inc(row_read, 2)
            dve.wait_ge(b2_loaded, 16)
            body(0, False)
            with dve.Fori(1, experts) as e:
                body(e, True)


HALVES = [(0, 6), (6, 5)]
SPLIT_RING = 4
PLAIN_RING = 4


def stage_masked_experts(nc, g, tag, src_t, w1_dram, b1_dram, w2_dram, weights, acc, mask_dram):
    experts, _, hidden = w1_dram.shape
    ht = hidden // P
    units = 2 * ht
    pieces = [(kind, k) for kind in ("w1", "x") for k in range(KD)]
    half_rows = HALVES[0][1] * P
    with ExitStack() as ctx:
        s = Pool(nc, ctx, tag)
        w1, w2 = s.sb("w1", [P, KD, hidden]), s.sb("w2", [P, ht, D])
        w1_parts = [s.sb(f"w1_{n}", [P, KD, hidden], F32R) for n in ("hi", "lo")]
        w2_parts = [s.sb(f"w2_{n}", [P, ht, D], F32R) for n in ("hi", "lo")]
        b1 = s.sb("b1", [P, experts * ht])
        mask = s.sb("mask", [P, NT])
        xm = s.sb("xm", [P, KD, NP])
        x_parts = [s.sb(f"x_{n}", [P, KD, NP], F32R) for n in ("hi", "lo")]
        plain = s.sb("plain", [P, PLAIN_RING, half_rows // 2])
        h_parts = [s.sb(f"h_{n}", [P, ht, half_rows], F32R) for n in ("hi", "lo")]
        wide = s.ps("wide", [P, SPLIT_RING, BANK])
        row = [s.ps(f"row{i}", [P, BANK]) for i in range(2)]
        w1_loaded, w2_loaded, b1_loaded, mask_loaded = (
            s.sem(n) for n in ("w1_loaded", "w2_loaded", "b1_loaded", "mask_loaded"))
        masked, wide_full, row_full = s.sem("masked"), s.sem("wide_full"), s.sem("row_full")
        plain_done, front_hi, w2_hi, act_seen = (
            s.sem(n) for n in ("plain_done", "front_hi", "w2_hi", "act_seen"))
        h_hi, h_lo, front_lo, w2_lo, row_read = (
            s.sem(n) for n in ("h_hi", "h_lo", "front_lo", "w2_lo", "row_read"))
        w1_v = w1_dram.rearrange("e (k p) o -> e p k o", p=P)
        w2_v = w2_dram.rearrange("e (f p) o -> e p f o", p=P)
        front = {"w1": (w1, w1_parts), "x": (xm, x_parts)}

        def over_experts(eng, body):
            with eng.Fori(0, experts - 1) as e:
                body(e, True)
            body(experts - 1, False)

        block = ctx.enter_context(nc.Block())

        @block.sync
        def _(sync):
            sync.dma_start(mask[:], mask_dram[0].partition_broadcast(P)).then_inc(mask_loaded, 16)
            sync.dma_start(w1[:], w1_v[0]).then_inc(w1_loaded, 16)
            sync.dma_start(b1[:], b1_dram).then_inc(b1_loaded, 16)
            sync.dma_start(w2[:], w2_v[0]).then_inc(w2_loaded, 16)
            with sync.Fori(1, experts) as e:
                sync.wait_ge(masked, KD * e + 1)
                sync.dma_start(mask[:], mask_dram[e].partition_broadcast(P)).then_inc(mask_loaded, 16)
                sync.wait_ge(front_lo, 4 * e)
                sync.dma_start(w1[:], w1_v[e]).then_inc(w1_loaded, 16)
                sync.wait_ge(w2_lo, 2 * e)
                sync.dma_start(w2[:], w2_v[e]).then_inc(w2_loaded, 16)

        @block.gpsimd
        def _(pool):
            def apply_mask():
                for k in range(KD):
                    nc.gpsimd.tensor_tensor(xm[:, k, 0:NT], src_t[:, k, 0:NT], mask[:], ALU.mult).then_inc(masked, 1)

            nc.gpsimd.memset(xm[:, :, NT:NP], 0.0).then_inc(masked, 1)
            pool.wait_ge(mask_loaded, 16)
            apply_mask()
            with pool.Fori(1, experts) as e:
                pool.wait_ge(mask_loaded, 16 * e + 16)
                pool.wait_ge(front_lo, 4 * e)
                apply_mask()

        @block.tensor
        def _(pe):
            def body(e, after):
                pe.wait_ge(front_lo, 4 * e + 4)
                f = 0
                for i, (b0, nb) in enumerate(HALVES):
                    w = nb * P // 2
                    for n in range(units):
                        t, c0 = n // 2, b0 * P + (n % 2) * w
                        pe.wait_ge(plain_done, 2 * units * e + (f + 1))
                        for k in range(KD):
                            last = split_products(nc, wide[:, f % SPLIT_RING, 0:w],
                                                  [part[:, k, t * P:(t + 1) * P] for part in w1_parts],
                                                  [part[:, k, c0:c0 + w] for part in x_parts], k == 0, k == KD - 1)
                        last.then_inc(wide_full, 1)
                        f += 1
                    if i == 0:
                        pe.wait_ge(w2_lo, 2 * e + 2)
                    pe.wait_ge(h_lo, 2 * units * e + f)
                    for b in range(b0, b0 + nb):
                        pe.wait_ge(row_read, NB * e + max(b + 1, 2))
                        for t in range(ht):
                            last = split_products(nc, row[b % 2][:, 0:D],
                                                  [part[:, t, (b - b0) * P:(b - b0 + 1) * P] for part in h_parts],
                                                  [part[:, t, :] for part in w2_parts], t == 0, t == ht - 1)
                        last.then_inc(row_full, 1)

            over_experts(pe, body)

        @block.scalar
        def _(act):
            def front_high(e):
                act.wait_ge(w1_loaded, 16 * e + 16)
                for kind, k in pieces:
                    if kind == "x" and k == 0:
                        act.wait_ge(masked, KD * e + (KD + 1))
                    whole, parts = front[kind]
                    nc.scalar.activation(parts[0][:, k, :], whole[:, k, :], ACT.Copy).then_inc(front_hi, 1)

            def w2_high(e):
                act.wait_ge(w2_loaded, 16 * e + 16)
                for i in range(2):
                    part = slice(i * ht // 2, (i + 1) * ht // 2)
                    nc.scalar.activation(w2_parts[0][:, part, :], w2[:, part, :], ACT.Copy).then_inc(w2_hi, 1)

            def body(e, after):
                f = 0
                for b0, nb in HALVES:
                    w = nb * P // 2
                    for n in range(units):
                        act.wait_ge(wide_full, 2 * units * e + (f + 1))
                        if f >= PLAIN_RING:
                            act.wait_ge(h_lo, 2 * units * e + (f + 1 - PLAIN_RING))
                        act.sem_inc(act_seen, 1)
                        nc.scalar.activation(plain[:, f % PLAIN_RING, 0:w], wide[:, f % SPLIT_RING, 0:w], ACT.Relu,
                                             bias=b1[:, bass.ds(e * ht + n // 2, 1)]).then_inc(plain_done, 1)
                        f += 1
                if after:
                    front_high(e + 1)
                    act.wait_ge(row_full, NB * e + NB)
                    w2_high(e + 1)

            act.sem_inc(plain_done, SPLIT_RING)
            act.wait_ge(b1_loaded, 16)
            front_high(0)
            w2_high(0)
            over_experts(act, body)

        @block.vector
        def _(dve):
            def front_low(e, piece):
                kind, k = pieces[piece]
                whole, parts = front[kind]
                dve.wait_ge(front_hi, 4 * e + (piece + 1))
                nc.vector.tensor_tensor(parts[1][:, k, :], whole[:, k, :], parts[0][:, k, :], ALU.subtract)\
                    .then_inc(front_lo, 1)

            def w2_low(e):
                for i in range(2):
                    part = slice(i * ht // 2, (i + 1) * ht // 2)
                    dve.wait_ge(w2_hi, 2 * e + (i + 1))
                    nc.vector.tensor_tensor(w2_parts[1][:, part, :], w2[:, part, :], w2_parts[0][:, part, :],
                                            ALU.subtract).then_inc(w2_lo, 1)

            def body(e, after):
                f = 0
                for i, (b0, nb) in enumerate(HALVES):
                    w = nb * P // 2
                    part = lambda j, n: h_parts[j][:, n // 2, (n % 2) * w:(n % 2) * w + w]

                    def low(f, n):
                        dve.wait_ge(h_hi, 2 * units * e + (f + 1))
                        nc.vector.tensor_tensor(part(1, n), plain[:, f % PLAIN_RING, 0:w], part(0, n), ALU.subtract)\
                            .then_inc(h_lo, 1)

                    for n in range(units):
                        dve.wait_ge(plain_done, 2 * units * e + (f + 1 + SPLIT_RING))
                        if n == 0:
                            dve.wait_ge(row_full, NB * e + b0) if i else dve.wait_ge(row_read, NB * e + 2)
                        nc.vector.tensor_copy(part(0, n), plain[:, f % PLAIN_RING, 0:w]).then_inc(h_hi, 1)
                        if n >= 1:
                            low(f - 1, n - 1)
                        f += 1
                    low(f - 1, units - 1)
                    for b in range(b0, b0 + nb):
                        dve.wait_ge(row_full, NB * e + (b + 1))
                        dve.wait_ge(row_read, NB * e + (b + 1))
                        nc.vector.scalar_tensor_tensor(out=acc[:, b, :], in0=row[b % 2][:, 0:D],
                                                       scalar=weights[:, b, bass.ds(e, 1)], in1=acc[:, b, :],
                                                       op0=ALU.mult, op1=ALU.add).then_inc(row_read, 1)
                        if i == 1 and after and b < NB - 1:
                            front_low(e + 1, b - b0)
                if after:
                    w2_low(e + 1)

            dve.sem_inc(row_read, 2)
            for piece in range(len(pieces)):
                front_low(0, piece)
            w2_low(0)
            over_experts(dve, body)


def two_level_experts(nc, g, a):
    with ExitStack() as ctx:
        s = Pool(nc, ctx, "lv")
        h0 = s.sb("h0", [P, NB, D])
        for level, experts in enumerate((a["L0_ffn_Wr0"].shape[1], a["L0_ffn_Wr1"].shape[1])):
            with ExitStack() as inner:
                t = Pool(nc, inner, f"lv{level}")
                probs, mask = t.sb("probs", [P, NB, experts]), t.sb("mask", [P, NB, experts])
                acc = (h0, g.x)[level]
                stage_route(nc, g, f"lv{level}r", g.xn_t, a[f"L0_ffn_Wr{level}"], experts, "probs", probs, mask)
                stage_spread(nc, g, f"lv{level}s", probs, experts, a[f"L0_ffn_b2_{level}"], acc, level == 1,
                             mask, g.mask_dram)
                stage_masked_experts(nc, g, f"lv{level}e", g.xn_t, a[f"L0_ffn_W1_{level}"], a[f"L0_ffn_b1_{level}"],
                              a[f"L0_ffn_W2_{level}"], probs, acc, g.mask_dram)
            if level == 0:
                stage_norm(nc, g, "lvt", h0, None, g.xn_t)


def normalised_experts(nc, g, a):
    with ExitStack() as ctx:
        s = Pool(nc, ctx, "ne")
        experts = a["L3_ffn_Wg"].shape[1]
        weights, mask = s.sb("weights", [P, NB, experts]), s.sb("mask", [P, NB, experts])
        stage_route(nc, g, "ner", g.xn_t, a["L3_ffn_Wg"], experts, "logits", weights, mask)
        stage_spread(nc, g, "nes", weights, experts, a["L3_ffn_beta"], g.x, True)
        stage_normalised_experts(nc, g, "nee", g.xn_t, a["L3_ffn_W1"], a["L3_ffn_b1"], a["L3_ffn_W2"],
                                 a["L3_ffn_b2"], a["L3_ffn_gamma"], weights, g.x)



def stage_aggregate(nc, g, tag, values, width, finish):
    with ExitStack() as ctx:
        s = Pool(nc, ctx, tag)
        part = [s.sb(f"part{i}", [P, NB, width], BF16) for i in range(3)]
        rest = s.sb("rest", [P, NB, width])
        out = [s.ps(f"out{i}", [P, BANK]) for i in range(4)]
        split, v_step, out_full, out_read = s.sem("split"), s.sem("v_step"), s.sem("out_full"), s.sem("out_read")
        block = ctx.enter_context(nc.Block())

        @block.vector
        def _(dve):
            link = chain(dve, v_step)
            for b0, n in TG:
                v, r = values[:, b0:b0 + n, :], rest[:, b0:b0 + n, :]
                hi, mid, lo = (p[:, b0:b0 + n, :] for p in part)
                link(nc.vector.tensor_copy(hi, v))
                link(nc.vector.tensor_tensor(r, v, hi, ALU.subtract))
                link(nc.vector.tensor_copy(mid, r))
                nc.vector.tensor_tensor(lo, r, mid, ALU.subtract).then_inc(split, 1)
            for b in range(NB):
                dve.wait_ge(out_full, b + 1)
                finish(b, out[b % 4][:, 0:width]).then_inc(out_read, 1)

        @block.tensor
        def _(pe):
            pe.wait_ge(g.adj_loaded, 16 * g.adj_loads)
            for b in range(NB):
                if b >= 4:
                    pe.wait_ge(out_read, b - 3)
                for t in range(NB):
                    if b == 0:
                        pe.wait_ge(split, t // 4 + 1)
                        pe.wait_ge(v_step, 3 * (t // 4 + 1))
                    for i in range(3):
                        last = nc.tensor.matmul(out[b % 4][:, 0:width], g.adj_t[:, t, b * P:(b + 1) * P],
                                                part[i][:, t, :], start=(t == 0 and i == 0),
                                                stop=(t == NB - 1 and i == 2))
                last.then_inc(out_full, 1)


def aggregate_only(nc, g, a):
    with ExitStack() as ctx:
        s = Pool(nc, ctx, "agg")
        w, hidden = s.sb("w", [P, D]), s.sb("hidden", [P, NB, D])
        with ExitStack() as inner:
            t = Pool(nc, inner, "aggw")
            w_loaded, scaled = t.sem("w_loaded"), t.sem("scaled")
            block = inner.enter_context(nc.Block())

            @block.sync
            def _(sync):
                sync.dma_start(w[:], a["L2_gnn_W"].partition_broadcast(P)).then_inc(w_loaded, 16)

            @block.vector
            def _(dve):
                dve.wait_ge(w_loaded, 16)
                nc.vector.tensor_tensor(hidden[:], g.xn[:], w[:].unsqueeze(1).to_broadcast([P, NB, D]), ALU.mult)\
                    .then_inc(scaled, 1)
                dve.wait_ge(scaled, 1)

        def finish(b, out):
            return nc.vector.tensor_tensor(g.x[:, b, :], out, g.x[:, b, :], ALU.add)

        stage_aggregate(nc, g, "agga", hidden, D, finish)



TINY = 1e-10
ARTANH_TOP = 1.0 - 1e-7
SERIES_BELOW = 0.25


def hyperbolic(nc, g, a):
    with ExitStack() as ctx:
        s = Pool(nc, ctx, "hyp")
        mx = s.sb("mx", [P, NB, D + 2])
        gathered = s.sb("gathered", [P, NB, D + 2])
        prod = s.sb("prod", [P, NB, D])
        stage_project(nc, g, "hypw", g.xn_t, a["L3_gnn_W"], [], (0, prod), adjacency=True)
        stage_hyperbolic_values(nc, g, prod, mx)

        def finish(b, out):
            return nc.vector.tensor_copy(gathered[:, b, :], out)

        stage_aggregate(nc, g, "hypa", mx, D + 2, finish)
        stage_hyperbolic_end(nc, g, gathered)


def artanh(link, nc, x, log_plus, log_minus, series, square, out):
    link(nc.vector.tensor_tensor(out, log_plus, log_minus, ALU.subtract))
    link(nc.vector.tensor_scalar(out, out, 0.5, None, ALU.mult))
    link(nc.vector.tensor_tensor(square, x, x, ALU.mult))
    link(nc.vector.tensor_scalar(series, square, 1 / 11, 1 / 9, ALU.mult, ALU.add))
    for c in (1 / 7, 1 / 5, 1 / 3, 1.0):
        link(nc.vector.tensor_tensor(series, series, square, ALU.mult))
        link(nc.vector.tensor_scalar(series, series, c, None, ALU.add))
    link(nc.vector.tensor_tensor(series, series, x, ALU.mult))
    link(nc.vector.tensor_tensor(series, series, out, ALU.subtract))
    link(nc.vector.tensor_scalar(square, x, SERIES_BELOW, None, ALU.is_lt))
    link(nc.vector.tensor_tensor(series, series, square, ALU.mult))
    link(nc.vector.tensor_tensor(out, out, series, ALU.add))


def turns(eng, own, other):
    n = [0, 0]

    def hand(instruction):
        n[0] += 1
        instruction.then_inc(own, 1)

    def take():
        n[1] += 1
        eng.wait_ge(other, n[1])
    return hand, take


def stage_hyperbolic_values(nc, g, prod, values):
    with ExitStack() as ctx:
        s = Pool(nc, ctx, "hypv")
        x_norm, m_norm, clipped, log_plus, log_minus, series, square, at, factor, gamma = (
            s.sb(n, [P, NB]) for n in ("x_norm", "m_norm", "clipped", "log_plus", "log_minus", "series", "square",
                                       "at", "factor", "gamma"))
        squares = s.sb("squares", [P, 3 * NB, D], BF16)
        v_step, v_turn, a_turn, a_step = s.sem("v_step"), s.sem("v_turn"), s.sem("a_turn"), s.sem("a_step")
        block = ctx.enter_context(nc.Block())

        @block.scalar
        def _(act):
            hand, take = turns(act, a_turn, v_turn)
            for b in range(NB):
                nc.scalar.activation(squares[:, b, :], g.xn[:, b, :], ACT.Square, accum_out=x_norm[:, b:b + 1])\
                    .then_inc(a_step, 1)
                nc.scalar.activation(squares[:, NB + b, :], prod[:, b, :], ACT.Square, accum_out=m_norm[:, b:b + 1])\
                    .then_inc(a_step, 1)
            take()
            nc.scalar.activation(m_norm[:], m_norm[:], ACT.Sqrt).then_inc(a_step, 1)
            act.wait_ge(a_step, 2 * NB + 1)
            hand(nc.scalar.activation(x_norm[:], x_norm[:], ACT.Sqrt))
            take()
            nc.scalar.activation(log_plus[:], clipped[:], ACT.Ln, bias=g.one[:]).then_inc(a_step, 1)
            act.wait_ge(a_step, 2 * NB + 2)
            hand(nc.scalar.activation(log_minus[:], clipped[:], ACT.Ln, bias=g.one[:], scale=-1.0))
            take()
            hand(nc.scalar.activation(at[:], at[:], ACT.Tanh))
            take()
            for b in range(NB):
                nc.scalar.activation(squares[:, 2 * NB + b, :], prod[:, b, :], ACT.Square,
                                     accum_out=square[:, b:b + 1]).then_inc(a_step, 1)

        @block.vector
        def _(dve):
            link = chain(dve, v_step)
            hand, take = turns(dve, v_turn, a_turn)
            dve.wait_ge(a_step, 2 * NB)
            link(nc.vector.tensor_scalar(x_norm[:], x_norm[:], TINY * TINY, None, ALU.max))
            hand(nc.vector.tensor_scalar(m_norm[:], m_norm[:], TINY * TINY, None, ALU.max))
            take()
            link(nc.vector.reciprocal(factor[:], x_norm[:]))
            link(nc.vector.tensor_tensor(factor[:], factor[:], m_norm[:], ALU.mult))
            hand(nc.vector.tensor_scalar(clipped[:], x_norm[:], ARTANH_TOP, None, ALU.min))
            take()
            artanh(link, nc, clipped[:], log_plus[:], log_minus[:], series[:], square[:], at[:])
            hand(nc.vector.tensor_tensor(at[:], at[:], factor[:], ALU.mult))
            take()
            link(nc.vector.reciprocal(factor[:], m_norm[:]))
            link(nc.vector.tensor_tensor(factor[:], factor[:], at[:], ALU.mult))
            link(nc.vector.tensor_scalar(series[:], m_norm[:], TINY, None, ALU.is_gt))
            link(nc.vector.tensor_tensor(factor[:], factor[:], series[:], ALU.mult))
            for b in range(NB - 1):
                link(nc.vector.tensor_scalar(prod[:, b, :], prod[:, b, :], factor[:, b:b + 1], None, ALU.mult))
            hand(nc.vector.tensor_scalar(prod[:, NB - 1, :], prod[:, NB - 1, :], factor[:, NB - 1:NB], None, ALU.mult))
            dve.wait_ge(a_step, 3 * NB + 2)
            link(nc.vector.tensor_scalar(gamma[:], square[:], -1.0, 1.0, ALU.mult, ALU.add))
            link(nc.vector.reciprocal(gamma[:], gamma[:]))
            link(nc.vector.tensor_scalar(gamma[:], gamma[:], 2.0, 1e-15, ALU.mult, ALU.max))
            for b in range(NB):
                link(nc.vector.tensor_scalar(values[:, b, 0:D], prod[:, b, :], gamma[:, b:b + 1], None, ALU.mult))
            link(nc.vector.tensor_scalar(values[:, :, D], gamma[:], -1.0, None, ALU.add))
            link(nc.vector.memset(values[:, :, D + 1], 1.0))


def stage_hyperbolic_end(nc, g, gathered):
    with ExitStack() as ctx:
        s = Pool(nc, ctx, "hype")
        inv, sq, root, n, clipped, log_plus, log_minus, series, square, at, factor, scale = (
            s.sb(nm, [P, NB]) for nm in ("inv", "sq", "root", "n", "clipped", "log_plus", "log_minus", "series",
                                         "square", "at", "factor", "scale"))
        squares = s.sb("squares", [P, 2 * NB, D], BF16)
        r = s.sb("r", [P, NB, D])
        v_step, v_turn, a_turn, a_step = s.sem("v_step"), s.sem("v_turn"), s.sem("a_turn"), s.sem("a_step")
        denom, alpha = gathered[:, :, D], gathered[:, :, D + 1]
        block = ctx.enter_context(nc.Block())

        @block.scalar
        def _(act):
            hand, take = turns(act, a_turn, v_turn)
            take()
            for b in range(NB):
                last = nc.scalar.activation(squares[:, b, :], gathered[:, b, 0:D], ACT.Square, scale=inv[:, b:b + 1],
                                            accum_out=sq[:, b:b + 1])
                if b < NB - 1:
                    last.then_inc(a_step, 1)
            hand(last)
            for col in (root, n):
                take()
                hand(nc.scalar.activation(col[:], col[:], ACT.Sqrt))

            def logs():
                take()
                nc.scalar.activation(log_plus[:], clipped[:], ACT.Ln, bias=g.one[:]).then_inc(a_step, 1)
                hand(nc.scalar.activation(log_minus[:], clipped[:], ACT.Ln, bias=g.one[:], scale=-1.0))

            logs()
            take()
            hand(nc.scalar.activation(at[:], at[:], ACT.Tanh))
            take()
            hand(nc.scalar.activation(root[:], root[:], ACT.Sqrt))
            logs()
            take()
            for b in range(NB):
                nc.scalar.activation(r[:, b, :], gathered[:, b, 0:D], ACT.Relu, scale=scale[:, b:b + 1])\
                    .then_inc(a_step, 1)
            act.wait_ge(a_step, NB - 1 + 2 + NB)
            for b in range(NB):
                last = nc.scalar.activation(squares[:, NB + b, :], r[:, b, :], ACT.Square, accum_out=sq[:, b:b + 1])
                if b < NB - 1:
                    last.then_inc(a_step, 1)
            hand(last)
            take()
            nc.scalar.activation(root[:], sq[:], ACT.Sqrt).then_inc(a_step, 1)
            act.wait_ge(a_step, 3 * NB + 1)
            hand(nc.scalar.activation(at[:], root[:], ACT.Tanh))

        @block.vector
        def _(dve):
            link = chain(dve, v_step)
            hand, take = turns(dve, v_turn, a_turn)
            link(nc.vector.tensor_scalar(sq[:], denom, 0.0, None, ALU.is_ge))
            link(nc.vector.tensor_scalar(sq[:], sq[:], 2.0, -1.0, ALU.mult, ALU.add))
            link(nc.vector.tensor_tensor(inv[:], denom, sq[:], ALU.mult))
            link(nc.vector.tensor_scalar(inv[:], inv[:], TINY, None, ALU.max))
            link(nc.vector.tensor_tensor(inv[:], inv[:], sq[:], ALU.mult))
            hand(nc.vector.reciprocal(inv[:], inv[:]))
            take()
            dve.wait_ge(a_step, NB - 1)
            link(nc.vector.tensor_scalar(root[:], sq[:], -1.0, 1.0, ALU.mult, ALU.add))
            hand(nc.vector.tensor_scalar(root[:], root[:], TINY, None, ALU.max))
            take()
            link(nc.vector.tensor_scalar(root[:], root[:], 1.0, None, ALU.add))
            link(nc.vector.reciprocal(factor[:], root[:]))
            link(nc.vector.tensor_tensor(sq[:], sq[:], factor[:], ALU.mult))
            link(nc.vector.tensor_tensor(sq[:], sq[:], factor[:], ALU.mult))
            hand(nc.vector.tensor_scalar(n[:], sq[:], TINY * TINY, None, ALU.max))
            take()
            hand(nc.vector.tensor_scalar(clipped[:], n[:], ARTANH_TOP, None, ALU.min))
            take()
            artanh(link, nc, clipped[:], log_plus[:], log_minus[:], series[:], square[:], at[:])
            hand(nc.vector.tensor_tensor(at[:], at[:], alpha, ALU.mult))
            take()
            link(nc.vector.reciprocal(n[:], n[:]))
            link(nc.vector.tensor_tensor(at[:], at[:], n[:], ALU.mult))
            link(nc.vector.tensor_tensor(factor[:], factor[:], at[:], ALU.mult))
            link(nc.vector.tensor_tensor(root[:], sq[:], at[:], ALU.mult))
            link(nc.vector.tensor_tensor(root[:], root[:], at[:], ALU.mult))
            hand(nc.vector.tensor_scalar(root[:], root[:], TINY * TINY, None, ALU.max))
            take()
            hand(nc.vector.tensor_scalar(clipped[:], root[:], ARTANH_TOP, None, ALU.min))
            take()
            artanh(link, nc, clipped[:], log_plus[:], log_minus[:], series[:], square[:], at[:])
            link(nc.vector.reciprocal(root[:], root[:]))
            link(nc.vector.tensor_tensor(at[:], at[:], root[:], ALU.mult))
            link(nc.vector.tensor_tensor(scale[:], factor[:], at[:], ALU.mult))
            hand(nc.vector.tensor_tensor(scale[:], scale[:], inv[:], ALU.mult))
            take()
            dve.wait_ge(a_step, 3 * NB)
            hand(nc.vector.tensor_scalar(sq[:], sq[:], TINY * TINY, None, ALU.max))
            take()
            link(nc.vector.reciprocal(root[:], root[:]))
            link(nc.vector.tensor_tensor(at[:], at[:], root[:], ALU.mult))
            for b in range(NB):
                link(nc.vector.scalar_tensor_tensor(out=g.x[:, b, :], in0=r[:, b, :], scalar=at[:, b:b + 1],
                                                    in1=g.x[:, b, :], op0=ALU.mult, op1=ALU.add))



HID = 512
HT = HID // P


def stage_gated_hidden(nc, g, tag, src_t, w_drams, h):
    pairs = [(i, j) for i in range(len(w_drams)) for j in range(HT)]
    with ExitStack() as ctx:
        s = Pool(nc, ctx, tag)
        w = [s.sb(f"w{i}", [P, KD, 2 * HID]) for i in range(len(w_drams))]
        gate = [s.sb(f"gate{i}", [P, NT]) for i in range(2)]
        wide = [s.ps(f"wide{i}", [P, CH, BANK]) for i in range(2)]
        w_loaded = [s.sem(f"w_loaded{i}") for i in range(len(w_drams))]
        pad, a_full, b_full, gate_done, h_done = (s.sem("pad"), s.sem("a_full"), s.sem("b_full"), s.sem("gate_done"),
                                                  s.sem("h_done"))
        block = ctx.enter_context(nc.Block())

        @block.sync
        def _(sync):
            for i, dram in enumerate(w_drams):
                sync.dma_start(w[i][:], dram.rearrange("(k p) o -> p k o", p=P)).then_inc(w_loaded[i], 16)

        @block.gpsimd
        def _(pool):
            nc.gpsimd.memset(h[:, :, NT:NP], 0.0).then_inc(pad, 1)
            pool.wait_ge(pad, 1)

        @block.tensor
        def _(pe):
            for t, (i, j) in enumerate(pairs):
                if j == 0:
                    pe.wait_ge(w_loaded[i], 16)
                for half, (full, read) in enumerate(((a_full, gate_done), (b_full, h_done))):
                    if t:
                        pe.wait_ge(read, t)
                    for c in range(CH):
                        for k in range(KD):
                            last = nc.tensor.matmul(wide[half][:, c, 0:CW],
                                                    w[i][:, k, half * HID + j * P:half * HID + (j + 1) * P],
                                                    src_t[:, k, c * CW:(c + 1) * CW], start=(k == 0), stop=(k == KD - 1))
                    last.then_inc(full, 1)

        @block.scalar
        def _(act):
            for t in range(len(pairs)):
                act.wait_ge(a_full, t + 1)
                if t >= 2:
                    act.wait_ge(h_done, t - 1)
                nc.scalar.activation(gate[t % 2][:].rearrange("p (c n) -> p c n", c=CH), wide[0][:, :, 0:CW], ACT.Silu)\
                    .then_inc(gate_done, 1)

        @block.vector
        def _(dve):
            for t in range(len(pairs)):
                dve.wait_ge(b_full, t + 1)
                dve.wait_ge(gate_done, t + 1)
                nc.vector.tensor_tensor(h[:, t, 0:NT].rearrange("p (c n) -> p c n", c=CH), wide[1][:, :, 0:CW],
                                        gate[t % 2][:].rearrange("p (c n) -> p c n", c=CH), ALU.mult).then_inc(h_done, 1)


def stage_routed_out(nc, g, tag, h, shared_dram, expert_dram, weights, experts):
    pairs = experts // 2
    with ExitStack() as ctx:
        s = Pool(nc, ctx, tag)
        ws = s.sb("ws", [P, HT, D])
        we = s.sb("we", [P, HT, experts * D])
        ring = [s.ps(f"ring{i}", [P, BANK]) for i in range(8)]
        ws_loaded, we_loaded, full, read = s.sem("ws_loaded"), s.sem("we_loaded"), s.sem("full"), s.sem("read")
        v_step = s.sem("v_step")
        block = ctx.enter_context(nc.Block())

        @block.sync
        def _(sync):
            sync.dma_start(ws[:], shared_dram.rearrange("(k p) o -> p k o", p=P)).then_inc(ws_loaded, 16)
            sync.dma_start(we[:], expert_dram.rearrange("(k p) o -> p k o", p=P)).then_inc(we_loaded, 16)

        @block.tensor
        def _(pe):
            pe.wait_ge(ws_loaded, 16)
            n = 0
            for b in range(NB):
                for j in range(1 + pairs):
                    if n >= 8:
                        pe.wait_ge(read, n - 7)
                    if n == 1:
                        pe.wait_ge(we_loaded, 16)
                    width = D if j == 0 else 2 * D
                    for f in range(HT):
                        lhs = h[:, f + (HT if j else 0), b * P:(b + 1) * P]
                        rhs = ws[:, f, :] if j == 0 else we[:, f, (j - 1) * 2 * D:j * 2 * D]
                        last = nc.tensor.matmul(ring[n % 8][:, 0:width], lhs, rhs, start=(f == 0), stop=(f == HT - 1))
                    last.then_inc(full, 1)
                    n += 1

        @block.vector
        def _(dve):
            link = chain(dve, v_step)
            n = 0
            for b in range(NB):
                for j in range(1 + pairs):
                    dve.wait_ge(full, n + 1)
                    if j == 0:
                        last = nc.vector.tensor_tensor(g.x[:, b, :], ring[n % 8][:, 0:D], g.x[:, b, :], ALU.add)
                    else:
                        e = 2 * (j - 1)
                        link(nc.vector.scalar_tensor_tensor(out=g.x[:, b, :], in0=ring[n % 8][:, 0:D],
                                                            scalar=weights[:, b, e:e + 1], in1=g.x[:, b, :],
                                                            op0=ALU.mult, op1=ALU.add))
                        last = nc.vector.scalar_tensor_tensor(out=g.x[:, b, :], in0=ring[n % 8][:, D:2 * D],
                                                              scalar=weights[:, b, e + 1:e + 2], in1=g.x[:, b, :],
                                                              op0=ALU.mult, op1=ALU.add)
                    last.then_inc(read, 1)
                    n += 1
                    dve.wait_ge(read, n)


def shared_and_routed(nc, g, a):
    experts = a["L1_ffn_expert_gate_w"].shape[0]
    with ExitStack() as ctx:
        s = Pool(nc, ctx, "sr")
        weights = s.sb("weights", [P, NB, experts])
        counts = s.sb("counts", [P, NB, experts + 1])
        affine = s.sb("affine", [P, 2 * KD])
        with ExitStack() as inner:
            t = Pool(nc, inner, "srl")
            loaded, ones = t.sem("loaded"), t.sem("ones")
            block = inner.enter_context(nc.Block())

            @block.sync
            def _(sync):
                sync.dma_start(affine[:], a["L1_ffn_affine"]).then_inc(loaded, 16)
                sync.wait_ge(loaded, 16)

            @block.gpsimd
            def _(pool):
                nc.gpsimd.memset(counts[:, :, experts], 1.0).then_inc(ones, 1)
                pool.wait_ge(ones, 1)

        stage_norm(nc, g, "srn", g.xn, g.xn, g.xn_t, affine[:, 0:KD], affine[:, KD:2 * KD])
        stage_route(nc, g, "srr", g.xn_t, a["L1_ffn_gates"], experts + 2, "grouped", weights, counts,
                    bias=a["L1_ffn_gate_bias"])
        stage_spread(nc, g, "srs", counts, experts + 1, a["L1_ffn_out_bias"], g.x, True)
        h = s.sb("h", [P, 2 * HT, NP])
        stage_gated_hidden(nc, g, "srh", g.xn_t, [a["L1_ffn_shared_in_w"], a["L1_ffn_expert_in_w"]], h)
        stage_routed_out(nc, g, "sro", h, a["L1_ffn_shared_out_w"], a["L1_ffn_expert_out_weight"], weights, experts)



HEADS = 8
HD = D // HEADS
PAIRS = HEADS // 2
QR = 3 * HD
STEPS = CH * NB
UNITS = 2 * STEPS
RING = 3
PRING = 4
MAX_TILES = 2 * NB
MAX_CHUNKS = MAX_TILES * CH
TURN_STEP = STEPS - 5
MAX_STEPS = [s for s in range(4, TURN_STEP + 1) if s % NB > 1]
MAX_AT = {s: [m for m in range(MAX_CHUNKS) if m * len(MAX_STEPS) // MAX_CHUNKS == i] for i, s in enumerate(MAX_STEPS)}
F_UNITS = 2 * FT
V_LINKS = CH * PAIRS + NB + 1 + 2 * NB + 2


def shares(items, slots):
    items = list(items)
    return [[m for n, m in enumerate(items) if n * slots // len(items) == i] for i in range(slots)]


FRONT_F2 = shares(range(0, 24), 6) + shares(range(46, MAX_CHUNKS), 5)
FRONT_F1 = shares(range(24, 46), F_UNITS)


def stage_transformer_experts(nc, g, a, weights, acc):
    experts = a["L2_ffn_Wqkv"].shape[0]
    with ExitStack() as ctx:
        s = Pool(nc, ctx, "tx")
        wqkv, wo = s.sb("wqkv", [P, KD, 3 * D]), s.sb("wo", [P, KD, D])
        w1, w2 = s.sb("w1", [P, KD, FF]), s.sb("w2", [P, FT, D])
        bv = s.sb("bv", [P, D])
        rows = s.sb("rows", [P, 5, D])
        bo, bf2, g2, be1_row, g1_row = (rows[:, i, :] for i in range(5))
        cols = s.sb("cols", [P, experts, 2 * KD + FT + 2 * KD])
        parts_a = s.sb("parts_a", [P, 4, NT], F32R)
        half = HALVES[0][1] * P
        at = slab(nc, s, "slab", FT * half)
        parts_b = nc.alloc_sbuf_tensor_at("tx_parts_b", [P, 4, NT], F32R, offset=at)
        h = nc.alloc_sbuf_tensor_at("tx_h", [P, FT, half], F32, offset=at)
        ops = s.sb("ops", [P, 2, 4, NP], F32R)
        v = s.sb("v", [P, NB, D])
        at2 = slab(nc, s, "slab2", KD * NP)
        ctx_t = nc.alloc_sbuf_tensor_at("tx_ctx", [P, KD, NP], F32, offset=at2)
        x1_t = nc.alloc_sbuf_tensor_at("tx_x1t", [P, KD, NP], F32, offset=at2)
        p = s.sb("p", [P, PRING, CW])
        x1 = s.sb("x1", [P, NB, D])
        inv_sum = s.sb("inv_sum", [2 * HD, 2, CW])
        chunk_max = s.sb("chunk_max", [P, MAX_TILES, CH])
        neg_max = s.sb("neg_max", [P, MAX_TILES])
        m_hi, m_lo = s.sb("m_hi", [MAX_TILES, P], F32R), s.sb("m_lo", [MAX_TILES, P], F32R)
        ones = s.sb("ones", [P, HD])
        key_bias = s.sb("key_bias", [P, 1])
        tmp = [s.sb(f"tmp{i}", [P, D]) for i in range(2)]
        z = [s.sb(f"z{i}", [P, D]) for i in range(2)]
        stats, mean_var = s.sb("stats", [P, NB, 6]), s.sb("mean_var", [P, NB, 2])
        std, scale, shift = s.sb("std", [P, NB]), s.sb("scale", [P, NB]), s.sb("shift", [P, NB])

        bank = s.ps("bank", [P, 8, BANK])
        wide = [bank[:, 0:3, :], bank[:, 3:6, :]]
        row = [bank[:, 6, :], bank[:, 7, :]]
        turned = [bank[0:MAX_TILES, 7, 0:P], bank[0:MAX_TILES, 3, 0:P]]

        front_loaded, w_loaded, cols_loaded = s.sem("front_loaded"), s.sem("w_loaded"), s.sem("cols_loaded")
        ops_loaded = [s.sem("ops_loaded_even"), s.sem("ops_loaded_odd")]
        max_loaded, const_made = s.sem("max_loaded"), s.sem("const_made")
        qk_full, v_full, max_full, turned_max, s_full, pv_done = (
            s.sem(n) for n in ("qk_full", "v_full", "max_full", "turned_max", "s_full", "pv_done"))
        wo_full, x1t_full, f1_full, f2_full = (s.sem(n) for n in ("wo_full", "x1t_full", "f1_full", "f2_full"))
        hi_done, m_hi_done, exp_done, std_done, x1t_done, h_done, gelu_done, z_full, act_seen = (
            s.sem(n) for n in ("hi_done", "m_hi_done", "exp_done", "std_done", "x1t_done", "h_done", "gelu_done",
                               "z_full", "act_seen"))
        lo_done, v_read, max_done, m_lo_done, ctx_done, wo_read, y_done, stats_done, scaled, v_step, v_seen, f2_added = (
            s.sem(n) for n in ("lo_done", "v_read", "max_done", "m_lo_done", "ctx_done", "wo_read", "y_done",
                               "stats_done", "scaled", "v_step", "v_seen", "f2_added"))
        aggr_step, joined_max = s.sem("aggr_step"), s.sem("joined_max")
        x1_done, z_used, rows_used, pool_step, key_zero, pads_zero, pool_seen, residual = (
            s.sem(n) for n in ("x1_done", "z_used", "rows_used", "pool_step", "key_zero", "pads_zero", "pool_seen",
                               "residual"))

        def over_experts(eng, body):
            body(0, False, True)
            with eng.Fori(1, experts - 1) as e:
                body(e, True, True)
            body(experts - 1, True, False)

        block = ctx.enter_context(nc.Block())
        nc.disable_value_cache = True

        @block.sync
        def _(sync):
            def load_front(e):
                sync.dma_start(wqkv[:], a["L2_ffn_Wqkv"][e].rearrange("(k p) o -> p k o", p=P)).then_inc(front_loaded, 16)
                sync.dma_start(bv[:], a["L2_ffn_bv"][e].partition_broadcast(P)).then_inc(front_loaded, 16)

            def load_pair(pair):
                parts = parts_a if pair < 2 else parts_b
                for head in (2 * pair, 2 * pair + 1):
                    lanes = slice(HD * (head % 4), HD * (head % 4) + HD)
                    for i, two in enumerate((slice(1, 3), slice(0, 3, 2), slice(1, 4, 2))):
                        sync.dma_start(ops[HD * i:HD * (i + 1), :, head % 4, 0:NT].bitcast(F32),
                                       parts[lanes, two, :].bitcast(F32)).then_inc(ops_loaded[pair % 2], 16)

            def load_first_pairs(e):
                sync.wait_ge(lo_done, 4 * e + 2)
                load_pair(0)
                load_pair(1)

            def load_max(e, pair):
                sync.wait_ge(m_hi_done, PAIRS * e + (pair + 1))
                sync.wait_ge(m_lo_done, PAIRS * e + (pair + 1))
                slot = 2 * pair % 4
                for r, part in enumerate((m_hi, m_lo)):
                    sync.dma_start(ops[QR + r:QR + r + 1, 0, slot:slot + 2, :].bitcast(F32),
                                   part[:].bitcast(F32)).then_inc(max_loaded, 16)

            def body(e, before, after):
                load_max(e, 0)
                if after:
                    sync.wait_ge(qk_full, 4 * e + 4)
                    load_front(e + 1)
                if before:
                    sync.wait_ge(f2_full, NB * e)
                sync.dma_start(wo[:], a["L2_ffn_Wo"][e].rearrange("(k p) o -> p k o", p=P)).then_inc(w_loaded, 16)
                sync.dma_start(w1[:], a["L2_ffn_W1"][e].rearrange("(k p) o -> p k o", p=P)).then_inc(w_loaded, 16)
                sync.dma_start(w2[:], a["L2_ffn_W2"][e].rearrange("(f p) o -> p f o", p=P)).then_inc(w_loaded, 16)
                if before:
                    sync.wait_ge(rows_used, e)
                sync.dma_start(rows[:], a["L2_ffn_rows"][e].partition_broadcast(P)).then_inc(w_loaded, 16)
                load_max(e, 1)
                sync.wait_ge(lo_done, 4 * e + 4)
                for pair in (2, 3):
                    sync.wait_ge(pv_done, PAIRS * STEPS * e + (pair - 1) * STEPS)
                    load_pair(pair)
                    load_max(e, pair)
                if after:
                    load_first_pairs(e + 1)

            load_front(0)
            sync.dma_start(cols[:], a["L2_ffn_cols"]).then_inc(cols_loaded, 16)
            sync.wait_ge(const_made, 4)
            load_first_pairs(0)
            over_experts(sync, body)

        @block.gpsimd
        def _(pool):
            nc.gpsimd.memset(ones[:], 1.0).then_inc(const_made, 1)
            pool.wait_ge(const_made, 1)
            nc.gpsimd.memset(ops[QR:QR + 2, 1, :, :].bitcast(F32), 1.0).then_inc(const_made, 1)
            pool.wait_ge(const_made, 2)
            nc.gpsimd.memset(ops[0:QR, :, :, NT:NP].bitcast(F32), 0.0).then_inc(const_made, 1)
            pool.wait_ge(const_made, 3)
            nc.gpsimd.memset(key_bias[:], 0.0).then_inc(key_zero, 1)
            pool.wait_ge(key_zero, 1)
            nc.gpsimd.affine_select(out=key_bias[:], in_=key_bias[:], compare_op=ALU.is_gt, fill=-BIG,
                                    base=N - (NB - 1) * P, pattern=[[0, 1]], channel_multiplier=-1)\
                .then_inc(const_made, 1)
            pool.sem_inc(z_used, 2)

            def add_result(e):
                for b in range(NB):
                    z_b = z[b % 2]
                    pool.wait_ge(z_full, NB * e + (b + 1))
                    nc.gpsimd.tensor_tensor(z_b[:], z_b[:], g2, ALU.mult).then_inc(z_used, 1)
                    pool.wait_ge(z_used, 2 * NB * e + (2 * b + 3))
                    nc.gpsimd.tensor_tensor(acc[:, b, :], acc[:, b, :], z_b[:], ALU.add).then_inc(z_used, 1)
                    pool.wait_ge(z_used, 2 * NB * e + (2 * b + 4))
                pool.sem_inc(rows_used, 1)

            def body(e, before, after):
                pool.wait_ge(qk_full, 4 * e + 3)
                pool.sem_inc(pool_seen, 1)
                nc.gpsimd.memset(ctx_t[:, :, NT:NP], 0.0).then_inc(pads_zero, 1)
                if before:
                    add_result(e - 1)
                pool.wait_ge(w_loaded, 64 * e + 64)
                for b in range(NB):
                    nc.gpsimd.tensor_tensor(x1[:, b, :], g.xn[:, b, :], bo, ALU.add).then_inc(residual, 1)
                for b in range(NB):
                    pool.wait_ge(x1t_full, 6 * e + KD * (b // 4 + 1))
                    nc.gpsimd.tensor_tensor(x1[:, b, :], x1[:, b, :], g1_row, ALU.mult).then_inc(pool_step, 1)
                    pool.wait_ge(pool_step, NB * e + (b + 1))
                    nc.gpsimd.tensor_tensor(x1[:, b, :], x1[:, b, :], be1_row, ALU.add).then_inc(x1_done, 1)

            over_experts(pool, body)
            add_result(experts - 1)

        @block.tensor
        def _(pe):
            def project(e, tile, between=None):
                c0 = (tile % 2) * D + (tile // 2) * P
                for c in range(CH):
                    if between is not None and c == CH - 1:
                        between()
                    for k in range(KD):
                        last = nc.tensor.matmul(wide[tile % 2][:, c, 0:CW], wqkv[:, k, c0:c0 + P],
                                                g.xn_t[:, k, c * CW:(c + 1) * CW], start=(k == 0), stop=(k == KD - 1))
                last.then_inc(qk_full, 1)

            def project_v(e, b):
                if b >= 2:
                    pe.wait_ge(v_read, NB * e + (b - 1))
                for k in range(KD):
                    last = nc.tensor.matmul(row[b % 2][:, 0:D], g.xn_t[:, k, b * P:(b + 1) * P],
                                            wqkv[:, k, 2 * D:3 * D], start=(k == 0), stop=(k == KD - 1))
                last.then_inc(v_full, 1)

            def max_scores(e, pair, m):
                tile, c = m // CH, m % CH
                head, b = 2 * pair + tile // NB, tile % NB
                if m == 0:
                    pe.wait_ge(ops_loaded[pair % 2], 192 * e + 96 * (pair // 2 + 1))
                    if pair == 0:
                        pe.wait_ge(lo_done, 4 * e + 2)
                    elif pair == 1:
                        pe.wait_ge(lo_done, 4 * e + 4)
                    else:
                        pe.wait_ge(m_lo_done, PAIRS * e + pair)
                if m >= RING:
                    pe.wait_ge(max_done, PAIRS * MAX_CHUNKS * e + (MAX_CHUNKS * pair + m - RING + 1))
                k0, w = KCH[c]
                nc.tensor.matmul(bank[:, 3 + m % RING, 0:w], ops[0:QR, 0, head % 4, b * P:(b + 1) * P],
                                 ops[0:QR, 1, head % 4, k0:k0 + w], start=True, stop=True).then_inc(max_full, 1)

            def turn_max(e, pair):
                pe.wait_ge(joined_max, PAIRS * e + (pair + 1))
                nc.tensor.transpose(turned[min(pair, 1)], neg_max[:], g.ident[:]).then_inc(turned_max, 1)

            def scores(e, pair, step):
                c, t = step // NB, step % NB
                if step == 0:
                    pe.wait_ge(max_loaded, 32 * PAIRS * e + 32 * (pair + 1))
                    if pair == 0:
                        pe.wait_ge(lo_done, 4 * e + 3)
                for i in range(2):
                    u = UNITS * pair + 2 * step + i
                    if u >= RING:
                        pe.wait_ge(exp_done, PAIRS * UNITS * e + (u - RING + 1))
                    slot = (2 * pair + i) % 4
                    nc.tensor.matmul(bank[:, u % RING, 0:CW], ops[0:QR + 2, 1, slot, t * P:(t + 1) * P],
                                     ops[0:QR + 2, 0, slot, c * CW:(c + 1) * CW], start=True, stop=True)\
                        .then_inc(s_full, 1)

            def mix(e, pair, step, before):
                c, t = step // NB, step % NB
                chunk = CH * pair + c
                u = UNITS * pair + 2 * step
                if t == 0 and chunk >= 2:
                    pe.wait_ge(ctx_done, CH * PAIRS * e + (chunk - 1))
                if t == 0 and chunk == 0:
                    pe.wait_ge(v_read, NB * e + NB)
                    if before:
                        pe.wait_ge(f2_added, NB * e)
                pe.wait_ge(exp_done, PAIRS * UNITS * e + (u + 2))
                for i in range(2):
                    head = 2 * pair + i
                    for j, lhs in enumerate((v[:, t, head * HD:(head + 1) * HD], ones[:])):
                        lane = HD * (i + 2 * j)
                        last = nc.tensor.matmul(row[chunk % 2][lane:lane + HD, 0:CW], lhs, p[:, (u + i) % PRING, :],
                                                start=(t == 0), stop=(t == NB - 1), tile_position=(0, lane))
                last.then_inc(pv_done, 1)

            def body(e, before, after):
                pe.wait_ge(f2_added, NB * e) if before else pe.wait_ge(v_read, NB)
                turn_max(e, 0)
                project(e, 2)
                project(e, 3, between=lambda: scores(e, 0, 0))
                for pair in range(PAIRS):
                    for step in range(STEPS):
                        if step + 1 < STEPS:
                            scores(e, pair, step + 1)
                        elif pair + 1 < PAIRS:
                            scores(e, pair + 1, 0)
                        chunks = MAX_AT.get(step, []) if pair + 1 < PAIRS else []
                        for m in chunks[:1]:
                            max_scores(e, pair + 1, m)
                        mix(e, pair, step, before)
                        for m in chunks[1:]:
                            max_scores(e, pair + 1, m)
                        if step == TURN_STEP + 1 and pair + 1 < PAIRS:
                            turn_max(e, pair + 1)

                if after:
                    pe.wait_ge(front_loaded, 32 * e + 64)
                    project(e + 1, 0)
                pe.wait_ge(w_loaded, 64 * e + 64)
                pe.wait_ge(ctx_done, CH * PAIRS * e + CH * PAIRS)
                pe.wait_ge(pads_zero, e + 1)
                for b in range(NB):
                    if b >= 2:
                        pe.wait_ge(wo_read, NB * e + (b - 1))
                    for k in range(KD):
                        last = nc.tensor.matmul(row[b % 2][:, 0:D], ctx_t[:, k, b * P:(b + 1) * P], wo[:, k, :],
                                                start=(k == 0), stop=(k == KD - 1))
                    last.then_inc(wo_full, 1)
                if after:
                    project(e + 1, 1)
                pe.wait_ge(wo_read, NB * e + NB)
                n = 0
                for b0, nb in TG:
                    for k in range(KD):
                        if n >= 2:
                            pe.wait_ge(x1t_done, 6 * e + (n - 1))
                        for b in range(b0, b0 + nb):
                            if k == 0:
                                pe.wait_ge(y_done, NB * e + (b + 1))
                            last = nc.tensor.transpose(row[n % 2][:, (b - b0) * P:(b - b0 + 1) * P],
                                                       x1[:, b, k * P:(k + 1) * P], g.ident[:])
                        last.then_inc(x1t_full, 1)
                        n += 1
                pe.wait_ge(x1t_done, 6 * e + 6)
                if after:
                    pe.wait_ge(lo_done, 4 * (e + 1) + 1)
                f = 0
                done = 0
                for i, (b0, nb) in enumerate(HALVES):
                    w = nb * P // 2
                    for n in range(F_UNITS):
                        t, c = n // 2, n % 2
                        if f >= RING:
                            pe.wait_ge(h_done, 2 * F_UNITS * e + (f - RING + 1))
                        for k in range(KD):
                            c0 = b0 * P + c * w
                            last = nc.tensor.matmul(bank[:, f % RING, 0:w], w1[:, k, t * P:(t + 1) * P],
                                                    x1_t[:, k, c0:c0 + w], start=(k == 0), stop=(k == KD - 1))
                        last.then_inc(f1_full, 1)
                        f += 1
                        if after and i == 0 and 3 <= n < 3 + NB:
                            project_v(e + 1, n - 3)
                        if after and i == 1:
                            for m in FRONT_F1[n]:
                                max_scores(e + 1, 0, m)
                    pe.wait_ge(h_done, 2 * F_UNITS * e + f)
                    for b in range(b0, b0 + nb):
                        if b == 0 and after:
                            pe.wait_ge(v_read, NB * (e + 1) + NB)
                        if b >= 2:
                            pe.wait_ge(f2_added, NB * e + (b - 1))
                        for t in range(FT):
                            if after and t % 2:
                                for m in FRONT_F2[b][t // 2:t // 2 + 1]:
                                    max_scores(e + 1, 0, m)
                            last = nc.tensor.matmul(row[b % 2][:, 0:D], h[:, t, (b - b0) * P:(b - b0 + 1) * P],
                                                    w2[:, t, :], start=(t == 0), stop=(t == FT - 1))
                        last.then_inc(f2_full, 1)
                        if after:
                            for m in FRONT_F2[b][FT // 2:]:
                                max_scores(e + 1, 0, m)

            pe.wait_ge(const_made, 4)
            pe.wait_ge(front_loaded, 32)
            project(0, 0)
            project(0, 1)
            for b in range(NB):
                project_v(0, b)
            for m in range(MAX_CHUNKS):
                max_scores(0, 0, m)
            over_experts(pe, body)

        @block.scalar
        def _(act):
            def high(e, tile):
                into = (parts_a, parts_b)[tile // 2]
                act.wait_ge(qk_full, 4 * e + (tile + 1))
                act.sem_inc(act_seen, 1)
                nc.scalar.activation(into[:, 1 + tile % 2, :].rearrange("p (c n) -> p c n", c=CH),
                                     wide[tile % 2][:, :, 0:CW], ACT.Identity,
                                     bias=cols[:, bass.ds(e, 1), (tile % 2) * KD + tile // 2]).then_inc(hi_done, 1)

            def exponent(e, pair, step, i):
                u = UNITS * pair + 2 * step + i
                act.wait_ge(s_full, PAIRS * UNITS * e + (u + 1))
                if u >= PRING:
                    act.wait_ge(pv_done, PAIRS * STEPS * e + (u // 2 - 1))
                bias = dict(bias=key_bias[:]) if step % NB == NB - 1 else {}
                nc.scalar.activation(p[:, u % PRING, :], bank[:, u % RING, 0:CW], ACT.Exp, scale=HD ** -0.5, **bias)\
                    .then_inc(exp_done, 1)

            def high_max(e, pair, first=False):
                act.wait_ge(turned_max, PAIRS * e + (pair + 1))
                if not first:
                    act.wait_ge(max_loaded, 32 * PAIRS * e + 32 * pair)
                nc.scalar.activation(m_hi[:], turned[min(pair, 1)], ACT.Copy).then_inc(m_hi_done, 1)

            def weighted(e, b):
                act.wait_ge(z_used, 2 * NB * e + max(2 * b, 2))
                nc.scalar.activation(z[b % 2][:], x1[:, b, :], ACT.Identity, scale=scale[:, b:b + 1],
                                     bias=shift[:, b:b + 1]).then_inc(z_full, 1)

            def body(e, before, after):
                high(e, 2)
                for pair in range(PAIRS):
                    for step in range(STEPS):
                        for i in range(2):
                            exponent(e, pair, step, i)
                        if pair == 0 and step == 0:
                            high(e, 3)
                        if before and pair == 0 and step == 3:
                            act.wait_ge(scaled, e)
                        if before and pair == 0 and step % 2 and 0 <= (step - 3) // 2 < NB:
                            weighted(e - 1, (step - 3) // 2)
                        if step == TURN_STEP + 1 and pair + 1 < PAIRS:
                            high_max(e, pair + 1)
                act.wait_ge(stats_done, 2 * e + 1)
                nc.scalar.activation(std[:], mean_var[:, :, 1], ACT.Sqrt, bias=g.eps[:]).then_inc(std_done, 1)
                if after:
                    high(e + 1, 0)
                    high(e + 1, 1)
                n = 0
                for b0, nb in TG:
                    for k in range(KD):
                        act.wait_ge(x1t_full, 6 * e + (n + 1))
                        act.sem_inc(act_seen, 1)
                        c = 2 * KD + FT + k
                        nc.scalar.activation(x1_t[:, k, b0 * P:(b0 + nb) * P], row[n % 2][:, 0:nb * P], ACT.Identity,
                                             scale=cols[:, bass.ds(e, 1), c], bias=cols[:, bass.ds(e, 1), c + KD])\
                            .then_inc(x1t_done, 1)
                        n += 1
                f = 0
                for b0, nb in HALVES:
                    w = nb * P // 2
                    for n in range(F_UNITS):
                        t, c = n // 2, n % 2
                        act.wait_ge(f1_full, 2 * F_UNITS * e + (f + 1))
                        act.sem_inc(act_seen, 1)
                        nc.scalar.activation(h[:, t, c * w:(c + 1) * w], bank[:, f % RING, 0:w], ACT.Gelu,
                                             bias=cols[:, bass.ds(e, 1), 2 * KD + t]).then_inc(h_done, 1)
                        f += 1
                    for b in range(b0, b0 + nb):
                        act.wait_ge(f2_added, NB * e + (b + 1))
                        nc.scalar.activation(tmp[b % 2][:], tmp[b % 2][:], ACT.Gelu).then_inc(gelu_done, 1)
                if after:
                    high_max(e + 1, 0)
                act.wait_ge(stats_done, 2 * e + 2)
                nc.scalar.activation(std[:], mean_var[:, :, 1], ACT.Sqrt, bias=g.eps[:]).then_inc(std_done, 1)

            act.wait_ge(cols_loaded, 16)
            act.wait_ge(const_made, 4)
            high(0, 0)
            high(0, 1)
            high_max(0, 0, first=True)
            over_experts(act, body)
            act.wait_ge(scaled, experts)
            for b in range(NB):
                weighted(experts - 1, b)

        @block.vector
        def _(dve):
            n, base = [0], [0]

            def link(instruction):
                n[0] += 1
                instruction.then_inc(v_step, 1)
                dve.wait_ge(v_step, base[0] + n[0])

            def low(e, tile):
                parts = (parts_a, parts_b)[tile // 2]
                dve.wait_ge(hi_done, 4 * e + (tile + 1))
                nc.vector.scalar_tensor_tensor(out=parts[:, 3 * (tile % 2), :].rearrange("p (c n) -> p c n", c=CH),
                                               in0=wide[tile % 2][:, :, 0:CW],
                                               scalar=cols[:, bass.ds(e, 1), (tile % 2) * KD + tile // 2],
                                               in1=parts[:, 1 + tile % 2, :].rearrange("p (c n) -> p c n", c=CH),
                                               op0=ALU.add, op1=ALU.subtract).then_inc(lo_done, 1)

            def read_v(e, b):
                if b == 0:
                    dve.wait_ge(front_loaded, 32 * e + 32)
                dve.wait_ge(v_full, NB * e + (b + 1))
                nc.vector.tensor_tensor(v[:, b, :], row[b % 2][:, 0:D], bv[:], ALU.add).then_inc(v_read, 1)

            def row_max(e, pair, m):
                dve.wait_ge(max_full, PAIRS * MAX_CHUNKS * e + (MAX_CHUNKS * pair + m + 1))
                nc.vector.tensor_reduce(chunk_max[:, m // CH, m % CH:m % CH + 1], bank[:, 3 + m % RING, 0:KCH[m % CH][1]],
                                        AX_X, ALU.max, negate=True).then_inc(max_done, 1)

            def join_max(e, pair):
                dve.wait_ge(max_done, PAIRS * MAX_CHUNKS * e + MAX_CHUNKS * (pair + 1))
                nc.vector.tensor_reduce(neg_max[:], chunk_max[:], AX_X, ALU.min).then_inc(joined_max, 1)

            def low_max(e, pair):
                dve.wait_ge(m_hi_done, PAIRS * e + (pair + 1))
                nc.vector.tensor_tensor(m_lo[:], turned[min(pair, 1)], m_hi[:], ALU.subtract).then_inc(m_lo_done, 1)

            def normalise(e, pair, c):
                chunk = CH * pair + c
                out = row[chunk % 2]
                dve.wait_ge(pv_done, PAIRS * STEPS * e + NB * (chunk + 1))
                link(nc.vector.reciprocal(inv_sum[:, chunk % 2, :], out[2 * HD:4 * HD, 0:CW]))
                lane = 2 * HD * (pair % 2)
                nc.vector.tensor_tensor(ctx_t[lane:lane + 2 * HD, pair // 2, c * CW:(c + 1) * CW], out[0:2 * HD, 0:CW],
                                        inv_sum[:, chunk % 2, :], ALU.mult).then_inc(ctx_done, 1)

            def statistics():
                dve.sem_inc(v_seen, 1)
                for b in range(NB - 1):
                    nc.vector.bn_aggr(mean_var[:, b, :], stats[:, b, :]).then_inc(aggr_step, 1)
                nc.vector.bn_aggr(mean_var[:, NB - 1, :], stats[:, NB - 1, :]).then_inc(stats_done, 1)

            def body(e, before, after):
                low(e, 2)
                low(e, 3)
                for pair in range(PAIRS):
                    for step in range(STEPS):
                        chunks = MAX_AT.get(step, []) if pair + 1 < PAIRS else []
                        for m in chunks:
                            row_max(e, pair + 1, m)
                        if step == TURN_STEP and pair + 1 < PAIRS:
                            join_max(e, pair + 1)
                        if step % NB == NB - 1 and step < STEPS - 1:
                            normalise(e, pair, step // NB)
                        if step == TURN_STEP + 1 and pair + 1 < PAIRS:
                            low_max(e, pair + 1)
                    normalise(e, pair, CH - 1)

                for b in range(NB):
                    dve.wait_ge(wo_full, NB * e + (b + 1))
                    dve.wait_ge(residual, NB * e + (b + 1))
                    nc.vector.tensor_tensor(x1[:, b, :], row[b % 2][:, 0:D], x1[:, b, :], ALU.add).then_inc(wo_read, 1)
                    dve.wait_ge(wo_read, NB * e + (b + 1))
                    link(nc.vector.bn_stats(stats[:, b, :], x1[:, b, :]))
                statistics()
                dve.wait_ge(std_done, 2 * e + 1)
                link(nc.vector.reciprocal(std[:], std[:]))
                for b in range(NB):
                    nc.vector.tensor_scalar(x1[:, b, :], x1[:, b, :], mean_var[:, b, 0:1], std[:, b:b + 1],
                                            ALU.subtract, ALU.mult).then_inc(y_done, 1)
                if after:
                    low(e + 1, 0)
                    low(e + 1, 1)
                    for b in range(NB):
                        read_v(e + 1, b)

                def row_end(b):
                    dve.wait_ge(gelu_done, NB * e + (b + 1))
                    dve.wait_ge(x1_done, NB * e + (b + 1))
                    link(nc.vector.tensor_tensor(x1[:, b, :], tmp[b % 2][:], x1[:, b, :], ALU.add))
                    link(nc.vector.bn_stats(stats[:, b, :], x1[:, b, :]))

                for i, (b0, nb) in enumerate(HALVES):
                    if i == 1 and after:
                        for t in range(F_UNITS):
                            for m in FRONT_F1[t]:
                                row_max(e + 1, 0, m)
                    for b in range(b0, b0 + nb):
                        if after:
                            for m in FRONT_F2[b][:FT // 2]:
                                row_max(e + 1, 0, m)
                        dve.wait_ge(f2_full, NB * e + (b + 1))
                        nc.vector.tensor_tensor(tmp[b % 2][:], row[b % 2][:, 0:D], bf2, ALU.add).then_inc(f2_added, 1)
                        if after:
                            for m in FRONT_F2[b][FT // 2:]:
                                row_max(e + 1, 0, m)
                        if after and b == NB - 1:
                            join_max(e + 1, 0)
                        row_end(b)
                if after:
                    low_max(e + 1, 0)
                statistics()
                dve.wait_ge(std_done, 2 * e + 2)
                link(nc.vector.reciprocal(std[:], std[:]))
                link(nc.vector.tensor_tensor(scale[:], std[:], weights[:, :, bass.ds(e, 1)].rearrange("p b o -> p (b o)"),
                                             ALU.mult))
                nc.vector.scalar_tensor_tensor(out=shift[:], in0=mean_var[:, :, 0], scalar=-1.0, in1=scale[:],
                                               op0=ALU.mult, op1=ALU.mult).then_inc(scaled, 1)

            def counted_body(e, before, after):
                n[0] = 0
                base[0] = V_LINKS * e
                body(e, before, after)
                assert n[0] == V_LINKS, n[0]

            dve.wait_ge(cols_loaded, 16)
            low(0, 0)
            low(0, 1)
            for b in range(NB):
                read_v(0, b)
            for m in range(MAX_CHUNKS):
                row_max(0, 0, m)
            join_max(0, 0)
            low_max(0, 0)
            over_experts(dve, counted_body)


def transformer_experts(nc, g, a):
    with ExitStack() as ctx:
        s = Pool(nc, ctx, "te")
        experts = a["L2_ffn_Wqkv"].shape[0]
        weights, mask = s.sb("weights", [P, NB, experts]), s.sb("mask", [P, NB, experts])
        stage_route(nc, g, "ter", g.xn_t, a["L2_ffn_expert_queries"], experts, "keys", weights, mask,
                    keys=(a["L2_ffn_gate_Wk"], a["L2_ffn_gate_bk"]))
        stage_spread(nc, g, "tes", weights, experts, a["L2_ffn_be2"], g.x, True)
        stage_transformer_experts(nc, g, a, weights, g.x)



class Global:
    pass


def stage_clear(nc):
    used = sorted(nc.released_uncleared_semaphores)
    block_ctx = ExitStack()
    with block_ctx:
        block = block_ctx.enter_context(nc.Block())

        @block.gpsimd
        def _(pool):
            pool.sem_clear(range(used[0], used[-1] + 1))


def stage_store(nc, g, out):
    with ExitStack() as ctx:
        s = Pool(nc, ctx, "store")
        stored = s.sem("stored")
        block = ctx.enter_context(nc.Block())

        @block.sync
        def _(sync):
            full = N // P
            sync.dma_start(out[0:full * P, :].rearrange("(b p) d -> p b d", p=P), g.x[:, 0:full, :]).then_inc(stored, 16)
            sync.dma_start(out[full * P:N, :], g.x[0:N - full * P, full, :]).then_inc(stored, 16)
            sync.wait_ge(stored, 32)


def program(nc, a, out, start=0, stop=8):
    with ExitStack() as ctx:
        s = Pool(nc, ctx, "g")
        g = Global()
        g.adj_loaded, g.adj_loads = s.sem("adj_loaded"), 0
        g.x = s.sb("x", [P, NB, D])
        g.xn = s.sb("xn", [P, NB, D])
        g.xn_t = s.sb("xn_t", [P, KD, NP])
        g.ident = s.sb("ident", [P, P])
        g.eps = s.sb("eps", [P, 1])
        g.one = s.sb("one", [P, 1])
        g.ramp = s.sb("ramp", [P, NB, 8])
        g.mask_dram = nc.dram_tensor("expert_masks", [8, NT], F32, kind="Internal").ap()
        g.adj_t_dram = a["adj_t"]
        stage_load(nc, g, a["x"])
        blocks = [lambda: gat_layers(nc, g, a["L0_gnn_W_stack"]),
                  lambda: two_level_experts(nc, g, a),
                  lambda: masked_attention(nc, g, a["L1_gnn_W"], a["L1_gnn_U"], a["adj"]),
                  lambda: shared_and_routed(nc, g, a),
                  lambda: aggregate_only(nc, g, a),
                  lambda: transformer_experts(nc, g, a),
                  lambda: hyperbolic(nc, g, a),
                  lambda: normalised_experts(nc, g, a)]
        for i in range(start, stop):
            stage_clear(nc)
            with ExitStack() as inner:
                if i % 2 == 0:
                    g.adj_t = Pool(nc, inner, f"g{i}").sb("adj_t", [P, NB, NP], BF16)
                stage_norm(nc, g, f"ln{i}", g.x, g.xn, g.xn_t, adjacency=(i == 4))
                blocks[i]()
        stage_store(nc, g, out)


def columns(b):
    return np.ascontiguousarray(b.reshape(-1, P).T)


def lay_out(inputs):
    a = {name: np.ascontiguousarray(np.asarray(v)) for name, v in inputs.items()}
    x, adj = a.pop("x"), a.pop("adj")
    a["x"] = np.zeros((NP, D), x.dtype)
    a["x"][:N] = x
    a["adj"] = np.zeros((NP, N), adj.dtype)
    a["adj"][:N] = adj
    a["adj_t"] = np.zeros((NP, NP), adj.dtype)
    a["adj_t"][:N, :N] = adj.T
    a["L0_ffn_b1_0"], a["L0_ffn_b1_1"], a["L3_ffn_b1"] = (columns(a[k]) for k in ("L0_ffn_b1_0", "L0_ffn_b1_1", "L3_ffn_b1"))
    a["L1_ffn_gates"] = np.concatenate([a["L1_ffn_expert_gate_w"], a.pop("L1_ffn_group_gate_w")]).T.copy()
    a["L1_ffn_gate_bias"] = np.concatenate([a.pop("L1_ffn_expert_bias"), a.pop("L1_ffn_group_bias")])
    a["L1_ffn_out_bias"] = np.concatenate([a.pop("L1_ffn_expert_out_bias"), a.pop("L1_ffn_shared_out_b")[None]])
    a["L1_ffn_affine"] = np.concatenate([columns(a.pop("L1_ffn_ln_scale")), columns(a.pop("L1_ffn_ln_bias"))], 1)
    for k in ("L1_ffn_shared_in_w", "L1_ffn_expert_in_w", "L1_ffn_shared_out_w"):
        a[k] = a[k].T.copy()
    a["L1_ffn_expert_out_weight"] = a["L1_ffn_expert_out_weight"].transpose(2, 0, 1).reshape(HID, -1).copy()
    for k in ("L2_ffn_Wqkv", "L2_ffn_Wo", "L2_ffn_W1", "L2_ffn_W2"):
        a[k] = a[k].transpose(0, 2, 1).copy()
    a["L2_ffn_gate_Wk"] = a["L2_ffn_gate_Wk"].T.copy()
    a["L2_ffn_expert_queries"] = a["L2_ffn_expert_queries"].T.copy()
    a["L2_ffn_gate_bk"] = columns(a["L2_ffn_gate_bk"])
    bqkv, g1, be1 = a.pop("L2_ffn_bqkv"), a["L2_ffn_g1"], a.pop("L2_ffn_be1")
    per_feature = np.concatenate([bqkv[:, :2 * D], a.pop("L2_ffn_bf1"), g1, be1], 1)
    a["L2_ffn_cols"] = columns(per_feature).reshape(P, len(g1), -1)
    a["L2_ffn_bv"] = bqkv[:, 2 * D:].copy()
    a["L2_ffn_rows"] = np.stack([a.pop(f"L2_ffn_{k}") for k in ("bo", "bf2", "g2")] + [be1, a.pop("L2_ffn_g1")], 1)
    return a



def kernel(**inputs):
    import concourse.bacc as bacc
    from concourse.bass_utils import run_bass_kernel_spmd

    nc = bacc.Bacc("TRN2", target_bir_lowering=False, num_devices=1)
    arrays, args = {}, {}
    for name, array in lay_out(inputs).items():
        arrays[f"in_{name}"] = array
        args[name] = nc.dram_tensor(f"in_{name}", array.shape, mybir.dt.from_np(array.dtype), kind="ExternalInput").ap()
    out = nc.dram_tensor("out_x", (N, D), F32, kind="ExternalOutput").ap()
    program(nc, args, out)
    result = run_bass_kernel_spmd(nc, [arrays], core_ids=[0])
    return result.results[0]["out_x"]
```
